# Optimizing a Trainium2 kernel written in Bass

```python
import numpy as np
import jax
import jax.numpy as jnp

def _softmax(x, axis=-1):
    return jax.nn.softmax(x, axis=axis)

def _gelu(x):
    return jax.nn.gelu(x, approximate=True)

def _silu(x):
    return jax.nn.silu(x)

def _sigmoid(x):
    return jax.nn.sigmoid(x)

def _layernorm(x, axis=-1, eps=1e-05):
    m = jnp.mean(x, axis=axis, keepdims=True)
    v = jnp.var(x, axis=axis, keepdims=True)
    return (x - m) / jnp.sqrt(v + eps)

def _scatter_add(tgt, idx, src, axis=0):
    return tgt.at[idx].add(src)

def _segment_sum(src, seg, n):
    return jax.ops.segment_sum(src, seg, n)
kernel_name = 'mk_vit_tower_cls_d1_tok_img1024_r4_9b51c9'

def setup_inputs(seed: int=0):
    np.random.seed(seed)
    _w = jnp.asarray

    def _rec_inputs():
        import jax
        import jax.numpy as jnp
        _rk = jax.random.key(seed)
        x = 7.22013e-05 + 1.00017 * jax.random.normal(jax.random.fold_in(_rk, 1), (16, 64, 256, 4), jnp.float32)
        cls_tok = 0.02 * jax.random.normal(jax.random.fold_in(_rk, 5), (1, 1, 256), jnp.float32)
        return (x, cls_tok)
    x, cls_tok = _rec_inputs()

    def _L0_tok_setup():
        import jax, jax.numpy as jnp
        import numpy as np
        B, F, L, H, D = (8, 64, 256, 4, 64)
        MODEL = H * F
        WIN = 128

        def _local_mask():
            m = np.ones((L, L), dtype=bool)
            m = np.tril(m, WIN - 1)
            m = np.triu(m, -(WIN - 1))
            return jnp.asarray(m)

        def _flatten(y):
            n = y.shape[0]
            return y.transpose(0, 2, 3, 1).reshape(n, L, -1)
        key = jax.random.key(seed)
        ks = jax.random.split(key, 12)
        s = lambda n: 1.0 / np.sqrt(n)
        xav = np.sqrt(6.0 / (L + L))
        return {'x': jax.random.normal(ks[0], (B, F, L, H), jnp.float32), 'Wq_w': jax.random.normal(ks[1], (D, F), jnp.float32) * s(F), 'Wq_b': jnp.zeros((D,), jnp.float32), 'Wk_w': jax.random.normal(ks[2], (D, F), jnp.float32) * s(F), 'Wk_b': jnp.zeros((D,), jnp.float32), 'Wv_w': jax.random.normal(ks[3], (D, F), jnp.float32) * s(F), 'Wv_b': jnp.zeros((D,), jnp.float32), 'w_bias': jax.random.uniform(ks[4], (L, L), jnp.float32, -xav, xav), 'out_w': jax.random.normal(ks[5], (H * D, MODEL), jnp.float32) * s(H * D), 'out_b': jnp.zeros((MODEL,), jnp.float32), 'ln_g': jnp.ones((MODEL,), jnp.float32), 'ln_b': jnp.zeros((MODEL,), jnp.float32), 'local_mask': _local_mask()}
    _L0_tok_all = _L0_tok_setup()
    _L0_tok_in = {k: v for k, v in _L0_tok_all.items() if k in ('Wq_w', 'Wq_b', 'Wk_w', 'Wk_b', 'Wv_w', 'Wv_b', 'w_bias', 'out_w', 'out_b', 'ln_g', 'ln_b', 'local_mask')}
    del _L0_tok_all

    def _L0_attn_setup():
        import jax, jax.numpy as jnp
        import numpy as np
        D_MODEL = 256
        D_STATE = 256
        BATCH = 4
        SEQ = 1024

        def _linear_init(key, fan_in, fan_out):
            k1, k2 = jax.random.split(key)
            bound = 1.0 / np.sqrt(fan_in)
            W = jax.random.uniform(k1, (fan_in, fan_out), minval=-bound, maxval=bound, dtype=jnp.float32)
            b = jax.random.uniform(k2, (fan_out,), minval=-bound, maxval=bound, dtype=jnp.float32)
            return (W, b)
        key = jax.random.key(seed)
        ks = jax.random.split(key, 6)
        x = jax.random.normal(ks[0], (BATCH, SEQ, D_MODEL), dtype=jnp.float32)
        W_in, b_in = _linear_init(ks[1], D_MODEL, D_STATE)
        W_r, b_r = _linear_init(ks[2], D_MODEL, D_STATE)
        W_i, b_i = _linear_init(ks[3], D_MODEL, D_STATE)
        W_out, b_out = _linear_init(ks[4], D_STATE, D_MODEL)
        log_a = jax.random.uniform(ks[5], (D_STATE,), minval=-4.0, maxval=-1.0, dtype=jnp.float32)
        return {'x': x, 'W_in': W_in, 'b_in': b_in, 'W_r': W_r, 'b_r': b_r, 'W_i': W_i, 'b_i': b_i, 'W_out': W_out, 'b_out': b_out, 'log_a': log_a}
    _L0_attn_all = _L0_attn_setup()
    _L0_attn_in = {k: v for k, v in _L0_attn_all.items() if k in ('W_in', 'b_in', 'W_r', 'b_r', 'W_i', 'b_i', 'W_out', 'b_out', 'log_a')}
    del _L0_attn_all

    def _L0_ffn_setup():
        import jax, jax.numpy as jnp
        import numpy as np
        import math
        N_EMBD = 256
        HIDDEN = 4 * N_EMBD
        N_EXPERTS = 8
        TOP_K = 2
        B, T = (4, 512)

        def new_gelu(x):
            c = math.sqrt(2.0 / math.pi)
            return 0.5 * x * (1.0 + jnp.tanh(c * (x + 0.044715 * x * x * x)))

        def _moe_forward(x, Wfc_s, bfc_s, Wproj_s, bproj_s, Wr, Wfc, bfc, Wproj, bproj):
            Bb, Tt, C = x.shape
            xf = x.reshape(Bb * Tt, C)
            N = Bb * Tt
            shared = new_gelu(xf @ Wfc_s + bfc_s) @ Wproj_s + bproj_s
            logits = xf @ Wr
            probs = jax.nn.softmax(logits, axis=-1)
            topk_p, topk_i = jax.lax.top_k(probs, TOP_K)
            topk_p = topk_p / jnp.sum(topk_p, axis=-1, keepdims=True)
            gate = jnp.zeros((N, N_EXPERTS), dtype=xf.dtype)
            gate = gate.at[jnp.arange(N)[:, None], topk_i].add(topk_p)
            routed = jnp.zeros_like(xf)
            for e in range(N_EXPERTS):
                h = new_gelu(xf @ Wfc[e] + bfc[e]) @ Wproj[e] + bproj[e]
                routed = routed + h * gate[:, e:e + 1]
            return (shared + routed).reshape(Bb, Tt, C)
        key = jax.random.key(seed)
        ks = jax.random.split(key, 10)
        s = 0.02
        return {'x': jax.random.normal(ks[0], (B, T, N_EMBD), dtype=jnp.float32), 'Wfc_s': jax.random.normal(ks[1], (N_EMBD, HIDDEN), dtype=jnp.float32) * s, 'bfc_s': jnp.zeros((HIDDEN,), dtype=jnp.float32), 'Wproj_s': jax.random.normal(ks[2], (HIDDEN, N_EMBD), dtype=jnp.float32) * s, 'bproj_s': jnp.zeros((N_EMBD,), dtype=jnp.float32), 'Wr': jax.random.normal(ks[3], (N_EMBD, N_EXPERTS), dtype=jnp.float32) * s, 'Wfc': jax.random.normal(ks[4], (N_EXPERTS, N_EMBD, HIDDEN), dtype=jnp.float32) * s, 'bfc': jnp.zeros((N_EXPERTS, HIDDEN), dtype=jnp.float32), 'Wproj': jax.random.normal(ks[5], (N_EXPERTS, HIDDEN, N_EMBD), dtype=jnp.float32) * s, 'bproj': jnp.zeros((N_EXPERTS, N_EMBD), dtype=jnp.float32)}
    _L0_ffn_all = _L0_ffn_setup()
    _L0_ffn_in = {k: v for k, v in _L0_ffn_all.items() if k in ('Wfc_s', 'bfc_s', 'Wproj_s', 'bproj_s', 'Wr', 'Wfc', 'bfc', 'Wproj', 'bproj')}
    del _L0_ffn_all
    return {'x': x, 'cls_tok': cls_tok, 'L0_tok_Wq_w': _L0_tok_in['Wq_w'], 'L0_tok_Wq_b': _L0_tok_in['Wq_b'], 'L0_tok_Wk_w': _L0_tok_in['Wk_w'], 'L0_tok_Wk_b': _L0_tok_in['Wk_b'], 'L0_tok_Wv_w': _L0_tok_in['Wv_w'], 'L0_tok_Wv_b': _L0_tok_in['Wv_b'], 'L0_tok_w_bias': _L0_tok_in['w_bias'], 'L0_tok_out_w': _L0_tok_in['out_w'], 'L0_tok_out_b': _L0_tok_in['out_b'], 'L0_tok_ln_g': _L0_tok_in['ln_g'], 'L0_tok_ln_b': _L0_tok_in['ln_b'], 'L0_tok_local_mask': _L0_tok_in['local_mask'], 'L0_attn_W_in': _L0_attn_in['W_in'], 'L0_attn_b_in': _L0_attn_in['b_in'], 'L0_attn_W_r': _L0_attn_in['W_r'], 'L0_attn_b_r': _L0_attn_in['b_r'], 'L0_attn_W_i': _L0_attn_in['W_i'], 'L0_attn_b_i': _L0_attn_in['b_i'], 'L0_attn_W_out': _L0_attn_in['W_out'], 'L0_attn_b_out': _L0_attn_in['b_out'], 'L0_attn_log_a': _L0_attn_in['log_a'], 'L0_ffn_Wfc_s': _L0_ffn_in['Wfc_s'], 'L0_ffn_bfc_s': _L0_ffn_in['bfc_s'], 'L0_ffn_Wproj_s': _L0_ffn_in['Wproj_s'], 'L0_ffn_bproj_s': _L0_ffn_in['bproj_s'], 'L0_ffn_Wr': _L0_ffn_in['Wr'], 'L0_ffn_Wfc': _L0_ffn_in['Wfc'], 'L0_ffn_bfc': _L0_ffn_in['bfc'], 'L0_ffn_Wproj': _L0_ffn_in['Wproj'], 'L0_ffn_bproj': _L0_ffn_in['bproj']}

def reference(x, cls_tok, L0_tok_Wq_w, L0_tok_Wq_b, L0_tok_Wk_w, L0_tok_Wk_b, L0_tok_Wv_w, L0_tok_Wv_b, L0_tok_w_bias, L0_tok_out_w, L0_tok_out_b, L0_tok_ln_g, L0_tok_ln_b, L0_tok_local_mask, L0_attn_W_in, L0_attn_b_in, L0_attn_W_r, L0_attn_b_r, L0_attn_W_i, L0_attn_b_i, L0_attn_W_out, L0_attn_b_out, L0_attn_log_a, L0_ffn_Wfc_s, L0_ffn_bfc_s, L0_ffn_Wproj_s, L0_ffn_bproj_s, L0_ffn_Wr, L0_ffn_Wfc, L0_ffn_bfc, L0_ffn_Wproj, L0_ffn_bproj):
    import jax
    import jax.numpy as jnp

    def _L0_tok_ref(x, Wq_w, Wq_b, Wk_w, Wk_b, Wv_w, Wv_b, w_bias, out_w, out_b, ln_g, ln_b, local_mask):
        import jax, jax.numpy as jnp
        import numpy as np
        B, F, L, H, D = (8, 64, 256, 4, 64)
        MODEL = H * F
        WIN = 128

        def _local_mask():
            m = np.ones((L, L), dtype=bool)
            m = np.tril(m, WIN - 1)
            m = np.triu(m, -(WIN - 1))
            return jnp.asarray(m)

        def _flatten(y):
            n = y.shape[0]
            return y.transpose(0, 2, 3, 1).reshape(n, L, -1)

        def proj(w, b):
            y = jnp.einsum('nclh,dc->ndlh', x, w) + b[None, :, None, None]
            return _flatten(y)
        q = proj(Wq_w, Wq_b)
        k = proj(Wk_w, Wk_b)
        v = proj(Wv_w, Wv_b)
        wb = w_bias * local_mask.astype(w_bias.dtype)
        ew = jnp.exp(wb)
        ek = jnp.exp(k)
        num = jnp.einsum('ts,nsd->ntd', ew, ek * v)
        den = jnp.einsum('ts,nsd->ntd', ew, ek)
        y = jax.nn.sigmoid(q) * num / den
        h = y @ out_w + out_b + _flatten(x)
        mu = jnp.mean(h, axis=-1, keepdims=True)
        var = jnp.mean(jnp.square(h - mu), axis=-1, keepdims=True)
        return (h - mu) * jax.lax.rsqrt(var + 1e-05) * ln_g + ln_b

    def _L0_attn_ref(x, W_in, b_in, W_r, b_r, W_i, b_i, W_out, b_out, log_a):
        import jax, jax.numpy as jnp
        import numpy as np
        D_MODEL = 256
        D_STATE = 256
        BATCH = 4
        SEQ = 1024

        def _linear_init(key, fan_in, fan_out):
            k1, k2 = jax.random.split(key)
            bound = 1.0 / np.sqrt(fan_in)
            W = jax.random.uniform(k1, (fan_in, fan_out), minval=-bound, maxval=bound, dtype=jnp.float32)
            b = jax.random.uniform(k2, (fan_out,), minval=-bound, maxval=bound, dtype=jnp.float32)
            return (W, b)
        input_projected = jnp.einsum('bsd,de->bse', x, W_in) + b_in
        r_gate = jax.nn.sigmoid(jnp.einsum('bsd,de->bse', x, W_r) + b_r)
        i_gate = jax.nn.sigmoid(jnp.einsum('bsd,de->bse', x, W_i) + b_i)
        a = jax.nn.sigmoid(log_a)
        a_t = a * r_gate
        gated_input = i_gate * input_projected
        b_t = (1.0 - a_t) * gated_input

        def step(h, ab):
            a_s, b_s = ab
            h = a_s * h + b_s
            return (h, h)
        h0 = jnp.zeros((x.shape[0], a_t.shape[-1]), dtype=x.dtype)
        _, hs = jax.lax.scan(step, h0, (jnp.swapaxes(a_t, 0, 1), jnp.swapaxes(b_t, 0, 1)))
        output = jnp.swapaxes(hs, 0, 1)
        return jnp.einsum('bsn,nd->bsd', output, W_out) + b_out

    def _L0_ffn_ref(x, Wfc_s, bfc_s, Wproj_s, bproj_s, Wr, Wfc, bfc, Wproj, bproj):
        import jax, jax.numpy as jnp
        import numpy as np
        import math
        N_EMBD = 256
        HIDDEN = 4 * N_EMBD
        N_EXPERTS = 8
        TOP_K = 2
        B, T = (4, 512)

        def new_gelu(x):
            c = math.sqrt(2.0 / math.pi)
            return 0.5 * x * (1.0 + jnp.tanh(c * (x + 0.044715 * x * x * x)))

        def _moe_forward(x, Wfc_s, bfc_s, Wproj_s, bproj_s, Wr, Wfc, bfc, Wproj, bproj):
            Bb, Tt, C = x.shape
            xf = x.reshape(Bb * Tt, C)
            N = Bb * Tt
            shared = new_gelu(xf @ Wfc_s + bfc_s) @ Wproj_s + bproj_s
            logits = xf @ Wr
            probs = jax.nn.softmax(logits, axis=-1)
            topk_p, topk_i = jax.lax.top_k(probs, TOP_K)
            topk_p = topk_p / jnp.sum(topk_p, axis=-1, keepdims=True)
            gate = jnp.zeros((N, N_EXPERTS), dtype=xf.dtype)
            gate = gate.at[jnp.arange(N)[:, None], topk_i].add(topk_p)
            routed = jnp.zeros_like(xf)
            for e in range(N_EXPERTS):
                h = new_gelu(xf @ Wfc[e] + bfc[e]) @ Wproj[e] + bproj[e]
                routed = routed + h * gate[:, e:e + 1]
            return (shared + routed).reshape(Bb, Tt, C)
        return _moe_forward(x, Wfc_s, bfc_s, Wproj_s, bproj_s, Wr, Wfc, bfc, Wproj, bproj)
    h = _L0_tok_ref(x, L0_tok_Wq_w, L0_tok_Wq_b, L0_tok_Wk_w, L0_tok_Wk_b, L0_tok_Wv_w, L0_tok_Wv_b, L0_tok_w_bias, L0_tok_out_w, L0_tok_out_b, L0_tok_ln_g, L0_tok_ln_b, L0_tok_local_mask)
    h = jnp.concatenate([jnp.broadcast_to(cls_tok, (h.shape[0], 1, h.shape[2])), h], axis=1)
    h = h + _L0_attn_ref(_layernorm(h, axis=-1), L0_attn_W_in, L0_attn_b_in, L0_attn_W_r, L0_attn_b_r, L0_attn_W_i, L0_attn_b_i, L0_attn_W_out, L0_attn_b_out, L0_attn_log_a)
    h = h + _L0_ffn_ref(_layernorm(h, axis=-1), L0_ffn_Wfc_s, L0_ffn_bfc_s, L0_ffn_Wproj_s, L0_ffn_bproj_s, L0_ffn_Wr, L0_ffn_Wfc, L0_ffn_bfc, L0_ffn_Wproj, L0_ffn_bproj)
    return h

_drawn_inputs = setup_inputs


def setup_inputs(seed=0):
    import zlib

    import numpy as np

    out = dict(_drawn_inputs(seed))
    spreads = {'L0_tok_Wq_b': (0.0, 0.8),
     'L0_tok_Wk_b': (0.0, 2.0),
     'L0_tok_Wv_b': (0.0, 0.1),
     'L0_tok_out_b': (0.0, 0.1),
     'L0_tok_ln_g': (1.0, 0.2),
     'L0_tok_ln_b': (0.0, 0.1),
     'L0_ffn_bfc_s': (0.0, 0.1),
     'L0_ffn_bproj_s': (0.0, 0.1),
     'L0_ffn_bfc': (0.0, 0.338),
     'L0_ffn_bproj': (0.0, 0.1)}
    factors = {'cls_tok': 17.888,
     'L0_tok_w_bias': 8.0,
     'L0_attn_b_in': 4.507,
     'L0_attn_W_r': 64.0,
     'L0_attn_b_r': 64.0,
     'L0_attn_b_i': 8.0,
     'L0_attn_log_a': 39.216}
    for name, (base, spread) in spreads.items():
        noise = np.random.default_rng([zlib.crc32(name.encode()), seed]).standard_normal(out[name].shape)
        drawn = base * np.exp(spread * noise) if base else spread * noise
        out[name] = jnp.asarray(drawn.astype(out[name].dtype))
    for name, factor in factors.items():
        out[name] = (out[name] * factor).astype(out[name].dtype)
    return out
```

```python
import concourse.bass as bass
from concourse import mybir
from contextlib import ExitStack


def vit_tower(nc, x, cls_tok, w_proj, w_resid, bias_t, mask_t, out_w, ln_g, ln_b, w_in, w_r, w_i,
              w_out, b_in, b_r, b_i, b_out, log_a, w_route, fc_w, fc_b, pj_w, pj_b, out):
    F32, F32R, I32, U32, U8 = (mybir.dt.float32, mybir.dt.float32r, mybir.dt.int32,
                               mybir.dt.uint32, mybir.dt.uint8)
    ALU, ACT, AX = mybir.AluOpType, mybir.ActivationFunctionType, mybir.AxisListType
    P = 128
    NIMG, C, LH = x.shape
    H = w_resid.shape[1]
    L = LH // H
    D = C
    M = H * D
    LT, FT = L // P, M // P
    KA = C + 1
    NT = NIMG * LT
    TILES = NT + 1
    NE = w_route.shape[1]
    HID = fc_w.shape[2]
    HT = HID // P
    BLK = 2 * P
    TOK = NT * P + 1
    SBLK = (TOK + BLK - 1) // BLK
    MAX_BLK = SBLK + (2 * TOK + NE * BLK) // BLK
    MIN_BLK = SBLK + 2 * TOK // BLK
    DUMP = (MAX_BLK + 1) * BLK
    ROWS = DUMP + 2 * P
    EPS = 1e-5

    v_rows = nc.dram_tensor("v_rows", (ROWS, M), F32, kind="Internal").ap()
    y_rows = nc.dram_tensor("y_rows", (ROWS, M), F32, kind="Internal").ap()

    ctx = ExitStack()
    with ctx:
        memory = ctx

        def sb(name, shape, dt=F32):
            return memory.enter_context(nc.sbuf_tensor(name, shape, dt))

        def sem(name):
            return ctx.enter_context(nc.semaphore(name))

        def ps(name, shape):
            return ctx.enter_context(nc.psum_tensor(name, shape, F32))
        ident = sb("ident", [P, P])
        ones_pp = sb("ones_pp", [P, P])
        before = sb("before", [P, P])
        minus_half = sb("minus_half", [P, 2])
        wait_carrier = sb("wait_carrier", [1, 1])
        wait_carrier_d = sb("wait_carrier_d", [1, 1])
        wait_carrier_p = sb("wait_carrier_p", [1, 1])
        h_all = sb("h_all", [P, TILES, M])
        v_all = sb("v_all", [P, TILES, M])
        logits = sb("logits", [P, TILES, NE])
        stage1 = sb("stage1", [P, FT, HID])
        stage2 = sb("stage2", [P, HT, M])
        W1H, W1L, W2H, W2L = [], [], [], []

        def weight_set(i):
            W1H.append(sb(f"w1h{i}", [P, FT, HID], F32R))
            W1L.append(sb(f"w1l{i}", [P, FT, HID], F32R))
            W2H.append(sb(f"w2h{i}", [P, HT, M], F32R))
            W2L.append(sb(f"w2l{i}", [P, HT, M], F32R))

        weight_set(0)
        fcb = [sb(f"fcb{i}", [P, HT]) for i in range(2)]
        pjb = [sb(f"pjb{i}", [P, M]) for i in range(2)]
        zero_rows = sb("zero_rows", [P, 2, M])
        bounds = sb("bounds", [P, NE + 2], I32)
        gates = sb("gates", [P, TILES, 2])
        slots = sb("slots", [P, TILES, 2], U32)

        staged, w_split = sem("staged"), sem("w_split")
        biases_loaded = [sem(f"biases_loaded{i}") for i in range(2)]
        hi_split = sem("hi_split")
        expert_done = sem("expert_done")
        route_dve, route_act, route_pe, route_pool = (sem("route_dve"), sem("route_act"),
                                                      sem("route_pe"), sem("route_pool"))
        bounds_ready, slots_ready, tails_zeroed, scattered = (sem("bounds_ready"), sem("slots_ready"),
                                                              sem("tails_zeroed"), sem("scattered"))
        rest_stored = sem("rest_stored")
        rows_loaded, pt_ready, xh_ready, xl_ready = (sem("rows_loaded"), sem("pt_ready"),
                                                     sem("xh_ready"), sem("xl_ready"))
        fc_ready, gelu_done, gh_done, gl_done = (sem("fc_ready"), sem("gelu_done"), sem("gh_done"),
                                                 sem("gl_done"))
        y_ps, y_done, y_stored = sem("y_ps"), sem("y_done"), sem("y_stored")
        y_zeroed = sem("y_zeroed")
        gathered = [[sem(f"gathered{k}{i}") for i in range(4)] for k in range(2)]
        sum_done, zeroed = sem("sum_done"), sem("zeroed")
        ysh_loaded = [sem(f"ysh_loaded{i}") for i in range(4)]
        out_stored = [sem(f"out_stored{i}") for i in range(4)]
        first_added, combined_both = sem("first_added"), sem("combined_both")

        mixer_memory = ExitStack()
        memory = mixer_memory

        eps = sb("eps", [P, 2])
        wproj = sb("wproj", [KA, 3 * D])
        wresid = sb("wresid", [KA, H, D])
        ewT = sb("ewT", [P, LT, L])
        mask_f = sb("mask_f", [P, LT, L])
        mask_sb = sb("mask_sb", [P, LT, L // 4], I32)
        outw_sb = sb("outw_sb", [P, FT, M])
        win_sb = sb("win_sb", [P, FT, M])
        wr_sb = sb("wr_sb", [P, FT, M])
        wi_sb = sb("wi_sb", [P, FT, M])
        wout_sb = sb("wout_sb", [P, FT, M])
        route_sb = sb("route_sb", [P, FT, NE])
        lng_bc = sb("lng_bc", [P, M])
        lnb_bc = sb("lnb_bc", [P, M])
        bout_bc = sb("bout_bc", [P, M])
        col_raw = sb("col_raw", [P, 4, FT])
        bhalf = sb("bhalf", [P, 2, FT])
        a_clip = sb("a_clip", [P, 2, FT])
        a_exp = sb("a_exp", [P, 2, FT])
        a_rec = sb("a_rec", [P, FT])
        a_den = sb("a_den", [P, FT])
        a_half = sb("a_half", [P, FT])
        X = [sb(f"x{i}", [KA, LH]) for i in range(2)]
        E = sb("E", [P, LT, 2 * M])
        tanh_q = sb("tanh_q", [P, LT, M])
        t1 = sb("t1", [P, LT, M])
        rden = sb("rden", [P, LT, M])
        Y = sb("Y", [P, LT, M])
        YT = sb("YT", [P, FT, L])
        hn = sb("hn", [P, LT, M])
        hg = sb("hg", [P, LT, M])
        U = sb("U", [P, LT, M])
        V = sb("V", [P, LT, M])
        UT = sb("UT", [P, FT, L])
        VT = sb("VT", [P, FT, L])
        TR = sb("TR", [P, FT, L])
        TI = sb("TI", [P, FT, L])
        A = sb("A", [P, FT, L])
        OM = sb("OM", [P, FT, L])
        S = sb("S", [P, FT, L])
        B = sb("B", [P, FT, L])
        HS = sb("HS", [P, FT, L])
        st = [sb(f"st{i}", [P, LT, 6]) for i in range(3)]
        mv = [sb(f"mv{i}", [P, LT, 2]) for i in range(3)]
        ve = [sb(f"ve{i}", [P, LT]) for i in range(3)]
        rstd = [sb(f"rstd{i}", [P, LT]) for i in range(3)]
        c_u = sb("c_u", [1, M])
        c_st = [sb(f"c_st{i}", [1, 6]) for i in range(2)]
        c_mv = [sb(f"c_mv{i}", [1, 2]) for i in range(2)]
        c_ve = [sb(f"c_ve{i}", [1, 2]) for i in range(2)]
        c_rs = [sb(f"c_rs{i}", [1, 2]) for i in range(2)]
        c_ut = sb("c_ut", [P, FT])
        c_vt = sb("c_vt", [P, FT])
        c_g = sb("c_g", [P, 2, FT])
        c_a = sb("c_a", [P, FT])
        c_om = sb("c_om", [P, FT])
        c_s = sb("c_s", [P, FT])
        c_h = sb("c_h", [P, FT])
        ps_proj = ps("ps_proj", [P, H, 256])
        ps_nd = ps("ps_nd", [P, 2, 2 * M])
        ps_t = ps("ps_t", [P, FT, L])
        ps_h = ps("ps_h", [P, LT, M])
        ps_ri = ps("ps_ri", [P, 2, L])
        ps_ip = ps("ps_ip", [P, FT, L])
        ps_lg = ps_proj[:, 0:LT, 3 * D:3 * D + NE]

        w_loaded, x_loaded, v_stored = sem("w_loaded"), sem("x_loaded"), sem("v_stored")
        cls_loaded, cls_row1 = sem("cls_loaded"), sem("cls_row1")
        consts, prep, prep_act = sem("consts"), sem("prep"), sem("prep_act")
        ones_in_x = sem("ones_in_x")
        proj_ready, exp_done, tq_done = sem("proj_ready"), sem("exp_done"), sem("tq_done")
        ekv_done, nd_ready, t1_done = sem("ekv_done"), sem("nd_ready"), sem("t1_done")
        recip_done, y_ready = sem("recip_done"), sem("y_ready")
        yT_ps, yT_sb, h_ready = sem("yT_ps"), sem("yT_sb"), sem("h_ready")
        raw = [sem(f"stats{i}") for i in range(3)]
        mv_done = [sem(f"mv_done{i}") for i in range(3)]
        ve_done = [sem(f"ve_done{i}") for i in range(3)]
        rstd_done = [sem(f"rstd_done{i}") for i in range(3)]
        hn_done, hg_done, h0_done, h0b_done = (sem("hn_done"), sem("hg_done"), sem("h0_done"),
                                               sem("h0b_done"))
        u_ready, uT_ps, uT_sb = sem("u_ready"), sem("uT_ps"), sem("uT_sb")
        ri_ready, ip_ready, tanh_done = sem("ri_ready"), sem("ip_ready"), sem("tanh_done")
        a_done, om_done, s_done = sem("a_done"), sem("om_done"), sem("s_done")
        b_done, scan_done, attn_ready = sem("b_done"), sem("scan_done"), sem("attn_ready")
        h1_done, v_ready, vT_ps, vT_sb = sem("h1_done"), sem("v_ready"), sem("vT_ps"), sem("vT_sb")
        lg_ready, lg_done = sem("lg_ready"), sem("lg_done")
        cls_pe, cls_act, cls_dve, cls_pool = (sem("cls_pe"), sem("cls_act"), sem("cls_dve"),
                                              sem("cls_pool"))

        DEPTH = 4

        def steps(eng, step):
            for t in range(DEPTH):
                step(t, t % 2)
            with eng.Fori(DEPTH // 2, NIMG // 2) as pair:
                step(pair * 2, 0)
                step(pair * 2 + 1, 1)
            for t in range(NIMG, NIMG + DEPTH - 1):
                step(t, t % 2)

        def live(n):
            return not isinstance(n, int) or 0 <= n < NIMG

        def after(eng, semaphore, value):
            if not isinstance(value, int) or value > 0:
                eng.wait_ge(semaphore, value)

        def lone_wait(dve, semaphore, value):
            dve.wait_ge(semaphore, value)
            if not isinstance(value, int):
                dve.memset(wait_carrier[:], 0.0)

        def pool_wait(pool, semaphore, value):
            pool.wait_ge(semaphore, value)
            if not isinstance(value, int):
                pool.tensor_tensor(wait_carrier_p[:], minus_half[0:1, 0:1], minus_half[0:1, 0:1],
                                   ALU.add)

        def wait_apart(eng, semaphore, value):
            if not isinstance(value, int):
                value = eng.snap(value)
                eng.wait_ge(consts, 8)
            eng.wait_ge(semaphore, value)

        def at_most(value, limit):
            return min(value, limit) if isinstance(value, int) else value

        def tiles_of(buf, n):
            return buf[:, bass.ds(n * LT, LT), :]

        W_LOADS = 17

        def mixer_sync(sp):
            def load_x(n, par):
                after(sp, h_ready, LT * (n - 1))
                sp.dma_start(X[par][0:C, :], x[n]).then_inc(x_loaded, 16)

            sp.dma_start(h_all[0:1, NT, :], cls_tok).then_inc(cls_loaded, 16)
            sp.dma_start(wproj[:], w_proj).then_inc(w_loaded, 16)
            load_x(0, 0)
            load_x(1, 1)
            cols = "(t p) -> p t"
            for dst, src in ((col_raw[:, 0], b_r), (col_raw[:, 1], b_i), (col_raw[:, 2], log_a),
                             (col_raw[:, 3], b_in)):
                with nc.allow_non_contiguous_dma(reason="256 values as columns"):
                    sp.dma_start(dst, src.rearrange(cols, p=P)).then_inc(w_loaded, 16)
            rows = "(t p) m -> p t m"
            for dst, src in ((ewT, bias_t), (mask_sb, mask_t), (wr_sb, w_r), (wi_sb, w_i),
                             (win_sb, w_in), (wout_sb, w_out), (outw_sb, out_w)):
                sp.dma_start(dst[:], src.rearrange(rows, p=P)).then_inc(w_loaded, 16)
            sp.dma_start(route_sb[:], w_route.rearrange(rows, p=P)).then_inc(w_loaded, 16)
            sp.dma_start(wresid[:], w_resid).then_inc(w_loaded, 16)
            for dst, src in ((lng_bc, ln_g), (lnb_bc, ln_b), (bout_bc, b_out)):
                sp.dma_start(dst[:], src.rearrange("(a m) -> a m", a=1).to_broadcast([P, M])
                             ).then_inc(w_loaded, 16)

            sp.wait_ge(zeroed, 1)
            for r in range(MIN_BLK * BLK, ROWS, BLK):
                sp.dma_start(y_rows[r:r + BLK, :].rearrange("(p a) m -> p a m", a=2), zero_rows[:]
                             ).then_inc(y_zeroed, 16)

            def step(t, par):
                if live(t) and not (isinstance(t, int) and t < 2):
                    load_x(t, par)
                if live(t - 3):
                    n = t - 3
                    sp.wait_ge(v_ready, LT * (n + 1))
                    dst = v_rows[bass.ds(n * L, L), :].rearrange("(a p) m -> p a m", p=P)
                    sp.dma_start(dst, V[:]).then_inc(v_stored, 16)
                    sp.dma_start(tiles_of(v_all, n), V[:]).then_inc(v_stored, 16)

            return step

        def mixer_pool(pool):
            load_stage(pool, 0)
            load_biases(pool, 0, 0)
            load_biases(pool, 1, 1)
            pool.memset(ones_pp[:], 1.0).then_inc(consts, 1)
            pool.memset(ident[:], 0.0).then_inc(consts, 1)
            pool.memset(minus_half[:], -0.5).then_inc(consts, 1)
            pool.memset(eps[:], EPS).then_inc(consts, 1)
            pool.wait_ge(consts, 4)
            pool.affine_select(out=ident[:], in_=ident[:], compare_op=ALU.not_equal, fill=1.0,
                               base=0, pattern=[[-1, P]], channel_multiplier=1).then_inc(consts, 1)
            pool.affine_select(out=before[:], in_=ones_pp[:], compare_op=ALU.is_gt, fill=0.0,
                               base=0, pattern=[[1, P]], channel_multiplier=-1).then_inc(consts, 1)
            pool.memset(v_all[:, NT, :], 0.0).then_inc(consts, 1)
            pool.memset(logits[:, NT, :], 0.0).then_inc(consts, 1)
            for i in range(2):
                pool.wait_ge(cls_dve, 2 if i == 0 else 10)
                pool.tensor_scalar(c_ve[i][:, 0:1], c_mv[i][:, 1:2], EPS, None, ALU.add
                                   ).then_inc(cls_pool, 1)
                pool.wait_ge(cls_pool, 2 * i + 1)
                pool.tensor_tensor(c_rs[i][:, 0:1], c_ve[i][:, 0:1], minus_half[0:1, 0:1], ALU.pow
                                   ).then_inc(cls_pool, 1)

            def inv_std(i, n):
                pool.wait_ge(mv_done[i], LT * (n + 1))
                pool.tensor_tensor(ve[i][:], mv[i][:, :, 1], eps[:], ALU.add).then_inc(ve_done[i], 1)
                pool.wait_ge(ve_done[i], n + 1)
                after(pool, [hn_done, u_ready, v_ready][i], LT * n)
                pool.tensor_tensor(rstd[i][:], ve[i][:], minus_half[:], ALU.pow
                                   ).then_inc(rstd_done[i], 1)

            def step(t, par):
                if live(t - 3):
                    inv_std(2, t - 3)
                if live(t - 1):
                    n = t - 1
                    inv_std(0, n)
                    inv_std(1, n)
                    pool.wait_ge(u_ready, LT * (n + 1))
                    pool.tensor_tensor(tiles_of(h_all, n), tiles_of(h_all, n),
                                       bout_bc[:].unsqueeze(1).to_broadcast([P, LT, M]), ALU.add
                                       ).then_inc(h0b_done, 1)
                if isinstance(t, int) and t < DEPTH:
                    part = CHUNKS // DEPTH
                    split_weights(pool, 0, 0, range(part * t, part * (t + 1)))
                    if t == DEPTH - 1:
                        load_stage(pool, 1)

            return step

        def mixer_tensor(pe):
            pe.wait_ge(consts, 8)
            pe.wait_ge(cls_dve, 3)
            for k in range(FT):
                last = pe.matmul(ps_ip[:, 0, k:k + 1], c_u[0:1, k * P:(k + 1) * P],
                                 ones_pp[0:1, 0:1], start=True, stop=True)
            last.then_inc(cls_pe, 1)
            pe.wait_ge(w_loaded, 16 * W_LOADS)
            pe.wait_ge(cls_act, 1)
            for i, w in enumerate((wr_sb, wi_sb, win_sb)):
                for e in range(FT):
                    for k in range(FT):
                        last = pe.matmul(ps_ri[:, i // 2, (i % 2) * FT + e:(i % 2) * FT + e + 1],
                                         w[:, k, e * P:(e + 1) * P], c_ut[:, k:k + 1],
                                         start=(k == 0), stop=(k == FT - 1))
            last.then_inc(cls_pe, 1)
            pe.wait_ge(cls_dve, 7)
            for k in range(FT):
                last = pe.matmul(ps_h[0:1, 0, :], c_h[:, k:k + 1], wout_sb[:, k, :],
                                 start=(k == 0), stop=(k == FT - 1))
            last.then_inc(cls_pe, 1)
            pe.wait_ge(cls_dve, 11)
            for k in range(FT):
                last = pe.matmul(ps_ip[:, 0, k:k + 1], v_all[0:1, NT, k * P:(k + 1) * P],
                                 ones_pp[0:1, 0:1], start=True, stop=True)
            last.then_inc(cls_pe, 1)
            pe.wait_ge(cls_act, 4)
            for k in range(FT):
                last = pe.matmul(ps_h[0:1, 1, 0:NE], c_vt[:, k:k + 1], route_sb[:, k, :],
                                 start=(k == 0), stop=(k == FT - 1))
            last.then_inc(cls_pe, 1)
            pe.wait_ge(cls_dve, 12)
            pe.wait_ge(prep_act, 1)
            pe.wait_ge(ones_in_x, 2)

            def head_view(par, lt, h):
                return X[par].rearrange("c (l h) -> c l h", h=H)[:, lt * P:(lt + 1) * P, h]

            def project(n, par, lt):
                pe.wait_ge(x_loaded, 16 * (n + 1))
                after(pe, ekv_done, LT * n + lt)
                if lt == 0:
                    after(pe, lg_done, n - 3)
                for h in range(H):
                    last = pe.matmul(ps_proj[:, h, 0:3 * D], head_view(par, lt, h), wproj[:],
                                     start=True, stop=True)
                last.then_inc(proj_ready, 1)

            def transposes(src):
                for lt in range(LT):
                    for f in range(FT):
                        last = pe.transpose(ps_t[:, f, lt * P:(lt + 1) * P],
                                            src[:, lt, f * P:(f + 1) * P], ident[:])
                return last

            def step(t, par):
                if live(t - 3):
                    n = t - 3
                    pe.wait_ge(scan_done, FT * (n + 1))
                    pe.wait_ge(hn_done, at_most(LT * (n + 2), LT * NIMG))
                    for lt in range(LT):
                        for k in range(FT):
                            last = pe.matmul(ps_h[:, lt, :], HS[:, k, lt * P:(lt + 1) * P],
                                             wout_sb[:, k, :], start=(k == 0), stop=(k == FT - 1))
                    last.then_inc(attn_ready, 1)
                if live(t):
                    project(t, par, 0)
                if live(t - 1):
                    n = t - 1
                    pe.wait_ge(y_ready, n + 1)
                    after(pe, uT_sb, n)
                    transposes(Y).then_inc(yT_ps, 1)
                if live(t):
                    project(t, par, 1)
                if live(t - 1):
                    n = t - 1
                    pe.wait_ge(yT_sb, n + 1)
                    after(pe, h1_done, n - 1)
                    for lt in range(LT):
                        for f in range(FT):
                            pe.matmul(ps_h[:, lt, :], YT[:, f, lt * P:(lt + 1) * P],
                                      outw_sb[:, f, :], start=(f == 0), stop=False)
                        for h in range(H):
                            last = pe.matmul(ps_h[:, lt, h * D:(h + 1) * D],
                                             head_view(1 - par, lt, h), wresid[:, h, :],
                                             start=False, stop=(h == H - 1))
                        last.then_inc(h_ready, 1)
                if live(t - 2):
                    n = t - 2
                    pe.wait_ge(uT_sb, n + 1)
                    after(pe, b_done, FT * n)
                    for e in range(FT):
                        after(pe, tanh_done, FT * n + e)
                        for i, w in enumerate((wr_sb, wi_sb)):
                            for k in range(FT):
                                last = pe.matmul(ps_ri[:, i, :], w[:, k, e * P:(e + 1) * P],
                                                 UT[:, k, :], start=(k == 0), stop=(k == FT - 1))
                        last.then_inc(ri_ready, 1)
                        for k in range(FT):
                            last = pe.matmul(ps_ip[:, e, :], win_sb[:, k, e * P:(e + 1) * P],
                                             UT[:, k, :], start=(k == 0), stop=(k == FT - 1))
                        last.then_inc(ip_ready, 1)
                if live(t - 3):
                    n = t - 3
                    pe.wait_ge(v_ready, LT * (n + 1))
                    pe.wait_ge(yT_sb, at_most(n + 3, NIMG))
                    transposes(V).then_inc(vT_ps, 1)
                if live(t):
                    n = t
                    pe.wait_ge(ekv_done, LT * (n + 1))
                    after(pe, t1_done, LT * n)
                    after(pe, recip_done, LT * n)
                    for tt in range(LT):
                        for s in range(LT):
                            last = pe.matmul(ps_nd[:, tt, :], ewT[:, s, tt * P:(tt + 1) * P],
                                             E[:, s, :], start=(s == 0), stop=(s == LT - 1))
                        last.then_inc(nd_ready, 1)
                if live(t - 1):
                    n = t - 1
                    pe.wait_ge(u_ready, LT * (n + 1))
                    after(pe, vT_sb, n - 1)
                    transposes(U).then_inc(uT_ps, 1)
                if live(t - 3):
                    n = t - 3
                    pe.wait_ge(vT_sb, n + 1)
                    pe.wait_ge(ekv_done, at_most(LT * (n + 4), LT * NIMG))
                    after(pe, lg_done, n)
                    for lt in range(LT):
                        for k in range(FT):
                            last = pe.matmul(ps_lg[:, lt, :], VT[:, k, lt * P:(lt + 1) * P],
                                             route_sb[:, k, :], start=(k == 0), stop=(k == FT - 1))
                    last.then_inc(lg_ready, 1)

            return step

        def mixer_scalar(act):
            act.wait_ge(cls_pe, 1)
            act.copy(c_ut[:], ps_ip[:, 0, 0:FT]).then_inc(cls_act, 1)
            act.wait_ge(prep, 3)
            act.activation(ewT[:], ewT[:], ACT.Exp).then_inc(prep_act, 1)
            act.wait_ge(prep, 4)
            act.activation(a_exp[:, 0], a_clip[:, 0], ACT.Exp)
            act.activation(a_exp[:, 1], a_clip[:, 1], ACT.Exp, scale=-1.0).then_inc(prep_act, 1)
            act.wait_ge(cls_pe, 2)
            for i in range(2):
                for e in range(FT):
                    last = act.activation(c_g[:, i, e:e + 1], ps_ri[:, 0, i * FT + e:i * FT + e + 1],
                                          ACT.Tanh, bias=bhalf[:, i, e:e + 1], scale=0.5)
                last.then_inc(cls_act, 1)
            act.wait_ge(cls_pe, 4)
            act.copy(c_vt[:], ps_ip[:, 0, 0:FT]).then_inc(cls_act, 1)

            def exp_and_tanh(n, lt):
                act.wait_ge(proj_ready, LT * n + lt + 1)
                after(act, nd_ready, LT * n)
                act.activation(E[:, lt, M:2 * M].rearrange("p (h d) -> p h d", h=H),
                               ps_proj[:, :, D:2 * D], ACT.Exp).then_inc(exp_done, 1)
                after(act, t1_done, LT * n)
                act.activation(tanh_q[:, lt, :].rearrange("p (h d) -> p h d", h=H),
                               ps_proj[:, :, 0:D], ACT.Tanh, scale=0.5).then_inc(tq_done, 1)

            def step(t, par):
                if live(t):
                    exp_and_tanh(t, 0)
                if live(t - 1):
                    act.wait_ge(yT_ps, t)
                    act.copy(YT[:], ps_t[:]).then_inc(yT_sb, 1)
                if live(t):
                    exp_and_tanh(t, 1)
                if live(t - 2):
                    n = t - 2
                    for e in range(FT):
                        act.wait_ge(ri_ready, FT * n + e + 1)
                        after(act, s_done, n)
                        act.activation(TR[:, e, :], ps_ri[:, 0, :], ACT.Tanh,
                                       bias=bhalf[:, 0, e:e + 1], scale=0.5)
                        act.activation(TI[:, e, :], ps_ri[:, 1, :], ACT.Tanh,
                                       bias=bhalf[:, 1, e:e + 1], scale=0.5).then_inc(tanh_done, 1)
                if live(t - 3):
                    act.wait_ge(vT_ps, t - 2)
                    act.copy(VT[:], ps_t[:]).then_inc(vT_sb, 1)
                if live(t - 1):
                    act.wait_ge(uT_ps, t)
                    act.copy(UT[:], ps_t[:]).then_inc(uT_sb, 1)

            return step

        def mixer_vector(dve):
            def stats(i, srcs, counter, base):
                for lt, src in enumerate(srcs):
                    dve.bn_stats(st[i][:, lt, :], src).then_inc(raw[i], 1)
                lone_wait(dve, raw[i], base + LT)
                for lt in range(LT):
                    dve.bn_aggr(mv[i][:, lt, :], st[i][:, lt, :]).then_inc(mv_done[i], 1)

            cls_row = h_all[0:1, NT, :]
            dve.memset(zero_rows[:], 0.0).then_inc(zeroed, 1)
            for i in range(2):
                dve.memset(X[i][C:KA, :], 1.0).then_inc(ones_in_x, 1)
            dve.wait_ge(cls_loaded, 16)
            dve.bn_stats(c_st[0][:], cls_row).then_inc(cls_dve, 1)
            dve.wait_ge(cls_dve, 1)
            dve.bn_aggr(c_mv[0][:], c_st[0][:]).then_inc(cls_dve, 1)
            dve.wait_ge(cls_pool, 2)
            dve.tensor_scalar(c_u[:], cls_row, c_mv[0][:, 0:1], c_rs[0][:, 0:1],
                              ALU.subtract, ALU.mult).then_inc(cls_dve, 1)
            dve.wait_ge(w_loaded, 16 * W_LOADS)
            dve.tensor_scalar(bhalf[:], col_raw[:, 0:2], 0.5, None, ALU.mult).then_inc(prep, 1)
            dve.tensor_copy(mask_f[:], mask_sb[:].bitcast(U8)).then_inc(prep, 1)
            dve.wait_ge(prep, 2)
            dve.tensor_tensor(ewT[:], ewT[:], mask_f[:], ALU.mult).then_inc(prep, 1)
            for i, op in enumerate((ALU.min, ALU.max)):
                last = dve.tensor_scalar(a_clip[:, i], col_raw[:, 2], 0.0, None, op)
            last.then_inc(prep, 1)
            dve.wait_ge(prep_act, 2)
            dve.tensor_tensor(a_den[:], a_exp[:, 0], a_exp[:, 1], ALU.add).then_inc(prep, 1)
            dve.wait_ge(prep, 5)
            dve.reciprocal(a_rec[:], a_den[:]).then_inc(prep, 1)
            dve.wait_ge(prep, 6)
            dve.scalar_tensor_tensor(a_half[:], a_exp[:, 0], 0.5, a_rec[:], ALU.mult, ALU.mult
                                     ).then_inc(prep, 1)
            dve.wait_ge(prep, 7)
            dve.wait_ge(cls_act, 3)
            dve.scalar_tensor_tensor(c_a[:], c_g[:, 0], 1.0, a_half[:], ALU.add, ALU.mult
                                     ).then_inc(cls_dve, 1)
            dve.wait_ge(cls_dve, 4)
            dve.tensor_scalar(c_om[:], c_a[:], -0.5, 0.5, ALU.mult, ALU.add).then_inc(cls_dve, 1)
            dve.wait_ge(cls_dve, 5)
            dve.scalar_tensor_tensor(c_s[:], c_g[:, 1], 1.0, c_om[:], ALU.add, ALU.mult
                                     ).then_inc(cls_dve, 1)
            dve.wait_ge(cls_dve, 6)
            for e in range(FT):
                last = dve.scalar_tensor_tensor(c_h[:, e:e + 1], ps_ri[:, 1, e:e + 1],
                                                col_raw[:, 3, e:e + 1], c_s[:, e:e + 1],
                                                ALU.add, ALU.mult)
            last.then_inc(cls_dve, 1)
            dve.wait_ge(cls_pe, 3)
            dve.tensor_tensor(cls_row, cls_row, ps_h[0:1, 0, :], ALU.add).then_inc(cls_row1, 1)
            dve.wait_ge(cls_row1, 1)
            dve.tensor_tensor(cls_row, cls_row, bout_bc[0:1, :], ALU.add).then_inc(cls_dve, 1)
            dve.wait_ge(cls_dve, 8)
            dve.bn_stats(c_st[1][:], cls_row).then_inc(cls_dve, 1)
            dve.wait_ge(cls_dve, 9)
            dve.bn_aggr(c_mv[1][:], c_st[1][:]).then_inc(cls_dve, 1)
            dve.wait_ge(cls_pool, 4)
            dve.wait_ge(consts, 8)
            dve.tensor_scalar(v_all[0:1, NT, :], cls_row, c_mv[1][:, 0:1], c_rs[1][:, 0:1],
                              ALU.subtract, ALU.mult).then_inc(cls_dve, 1)
            dve.wait_ge(cls_pe, 5)
            dve.tensor_copy(logits[0:1, NT, :], ps_h[0:1, 1, 0:NE]).then_inc(cls_dve, 1)

            def ekv(n, lt):
                dve.wait_ge(tq_done, LT * n + lt + 1)
                dve.tensor_tensor(E[:, lt, 0:M].rearrange("p (h d) -> p h d", h=H),
                                  ps_proj[:, :, 2 * D:3 * D],
                                  E[:, lt, M:2 * M].rearrange("p (h d) -> p h d", h=H), ALU.mult
                                  ).then_inc(ekv_done, 1)

            def step(t, par):
                if live(t - 3):
                    n = t - 3
                    dve.wait_ge(attn_ready, n + 1)
                    dve.wait_ge(h0b_done, n + 1)
                    dve.tensor_tensor(tiles_of(h_all, n), tiles_of(h_all, n), ps_h[:], ALU.add
                                      ).then_inc(h1_done, 1)
                    lone_wait(dve, h1_done, n + 1)
                    stats(2, [h_all[:, bass.ds(LT * n + lt, 1), :] for lt in range(LT)], None,
                          LT * n)
                if live(t):
                    ekv(t, 0)
                if live(t - 3):
                    n = t - 3
                    dve.wait_ge(rstd_done[2], n + 1)
                    after(dve, vT_ps, n)
                    after(dve, v_stored, 32 * n)
                    for lt in range(LT):
                        dve.tensor_scalar(V[:, lt:lt + 1, :], h_all[:, bass.ds(LT * n + lt, 1), :],
                                          mv[2][:, lt, 0:1], rstd[2][:, lt:lt + 1],
                                          ALU.subtract, ALU.mult).then_inc(v_ready, 1)
                if live(t):
                    ekv(t, 1)
                if live(t - 1):
                    n = t - 1
                    dve.wait_ge(h_ready, LT * (n + 1))
                    stats(0, [ps_h[:, lt, :] for lt in range(LT)], None, LT * n)
                if live(t - 2):
                    n = t - 2
                    dve.wait_ge(tanh_done, FT * (n + 1))
                    for e in range(FT):
                        dve.tensor_scalar(A[:, e, :], TR[:, e, :], 1.0, a_half[:, e:e + 1],
                                          ALU.add, ALU.mult).then_inc(a_done, 1)
                    dve.wait_ge(a_done, FT * (n + 1))
                    dve.tensor_scalar(OM[:], A[:], -0.5, 0.5, ALU.mult, ALU.add
                                      ).then_inc(om_done, 1)
                if live(t - 1):
                    n = t - 1
                    dve.wait_ge(rstd_done[0], n + 1)
                    for lt in range(LT):
                        dve.tensor_scalar(hn[:, lt, :], ps_h[:, lt, :], mv[0][:, lt, 0:1],
                                          rstd[0][:, lt:lt + 1], ALU.subtract, ALU.mult
                                          ).then_inc(hn_done, 1)
                if live(t - 2):
                    n = t - 2
                    dve.wait_ge(om_done, n + 1)
                    dve.scalar_tensor_tensor(S[:], TI[:], 1.0, OM[:], ALU.add, ALU.mult
                                             ).then_inc(s_done, 1)
                if live(t - 1):
                    n = t - 1
                    dve.wait_ge(hn_done, LT * (n + 1))
                    dve.tensor_tensor(hg[:], hn[:], lng_bc[:].unsqueeze(1).to_broadcast([P, LT, M]),
                                      ALU.mult).then_inc(hg_done, 1)
                if live(t - 2):
                    n = t - 2
                    dve.wait_ge(s_done, n + 1)
                    dve.wait_ge(ip_ready, FT * (n + 1))
                    for e in range(FT):
                        dve.scalar_tensor_tensor(B[:, e, :], ps_ip[:, e, :], col_raw[:, 3, e:e + 1],
                                                 S[:, e, :], ALU.add, ALU.mult
                                                 ).then_inc(b_done, 1)
                if live(t - 1):
                    n = t - 1
                    dve.wait_ge(hg_done, n + 1)
                    dve.tensor_tensor(tiles_of(h_all, n), hg[:],
                                      lnb_bc[:].unsqueeze(1).to_broadcast([P, LT, M]), ALU.add
                                      ).then_inc(h0_done, 1)
                    lone_wait(dve, h0_done, n + 1)
                    stats(1, [h_all[:, bass.ds(LT * n + lt, 1), :] for lt in range(LT)], None,
                          LT * n)
                if live(t - 2):
                    n = t - 2
                    dve.wait_ge(b_done, FT * (n + 1))
                    after(dve, attn_ready, n)
                    for e in range(FT):
                        dve.tensor_tensor_scan(HS[:, e, :], A[:, e, :], B[:, e, :], c_h[:, e:e + 1],
                                               ALU.mult, ALU.add).then_inc(scan_done, 1)
                if live(t - 1):
                    n = t - 1
                    dve.wait_ge(rstd_done[1], n + 1)
                    after(dve, uT_ps, n)
                    for lt in range(LT):
                        dve.tensor_scalar(U[:, lt:lt + 1, :], h_all[:, bass.ds(LT * n + lt, 1), :],
                                          mv[1][:, lt, 0:1], rstd[1][:, lt:lt + 1],
                                          ALU.subtract, ALU.mult).then_inc(u_ready, 1)
                if live(t):
                    n = t
                    for tt in range(LT):
                        dve.wait_ge(nd_ready, LT * n + tt + 1)
                        dve.reciprocal(rden[:, tt, :], ps_nd[:, tt, M:2 * M]).then_inc(recip_done, 1)
                        dve.scalar_tensor_tensor(t1[:, tt, :], tanh_q[:, tt, :], 1.0,
                                                 ps_nd[:, tt, 0:M], ALU.add, ALU.mult
                                                 ).then_inc(t1_done, 1)
                    dve.wait_ge(t1_done, LT * (n + 1))
                    dve.wait_ge(recip_done, LT * (n + 1))
                    after(dve, yT_ps, n)
                    dve.scalar_tensor_tensor(Y[:], t1[:], 0.5, rden[:], ALU.mult, ALU.mult
                                             ).then_inc(y_ready, 1)
                if live(t - 3):
                    n = t - 3
                    dve.wait_ge(lg_ready, n + 1)
                    dve.tensor_copy(tiles_of(logits, n), ps_lg).then_inc(lg_done, 1)

            return step

        mixer_memory.close()
        memory = ctx
        weight_set(1)
        G_SLOTS = 4
        FC_SLOTS = 4
        LAG = 3
        ROUTE_SUB, ROUTE_MASK, ROUTE_RANK = 6, 22, 37
        R = sb("R", [P, 2, M])
        XH = sb("XH", [P, FT, BLK], F32R)
        XL = sb("XL", [P, FT, BLK], F32R)
        g_act = sb("g_act", [P, G_SLOTS, BLK])
        GH = sb("GH", [P, HT, BLK], F32R)
        GL = sb("GL", [P, HT, BLK], F32R)
        yb = sb("yb", [P, 2, M])
        route_memory = ExitStack()
        memory = route_memory
        iota_i = sb("iota_i", [P, NE], I32)
        iota_m = sb("iota_m", [P, NE])
        dump_i = sb("dump_i", [P, 2], I32)
        dump_f = sb("dump_f", [P, 2])
        dump = sb("dump", [P, 2])
        valid = ident[:, 0:1]
        big = {k: sb(f"r_{k}", [P, TILES, NE]) for k in
               ("sub", "exp", "prob", "hit", "cand", "one0", "one1", "prob2", "mask", "incl", "pos",
                "tot", "sel")}
        small = {k: sb(f"s_{k}", [P, TILES]) for k in
                 ("max", "sum", "rec", "m0", "m1", "idx", "gsum", "grec")}
        slot_f = sb("slot_f", [P, TILES, 2])
        cnt_i = sb("cnt_i", [P, NE], I32)
        cnt_s = sb("cnt_s", [P, NE], I32)
        cnt = {k: sb(f"c_{k}", [P, NE]) for k in ("n", "at_least", "end", "start")}
        route_memory.close()
        memory = ctx
        DEEP = 4
        ya = [sb(f"ya{i}", [P, M]) for i in range(DEEP)]
        yc = [sb(f"yc{i}", [P, M]) for i in range(DEEP)]
        ysh = [sb(f"ysh{i}", [P, M]) for i in range(DEEP)]
        o1 = [sb(f"o1{i}", [P, M]) for i in range(DEEP)]
        o2 = [sb(f"o2{i}", [P, M]) for i in range(DEEP)]

        ps_fc = [ps_proj[:, 0, :], ps_proj[:, 2, :], ps_nd[:, 0, 0:BLK], ps_nd[:, 1, 0:BLK]]
        ps_y = [ps_h[:, 0, :], ps_ip[:, 0, :]]
        ps_rank = ps_ri.rearrange("p a b -> p (a b)")[:, 0:TILES * NE]
        ps_tot = ps_ip.rearrange("p a b -> p (a b)")[:, 0:TILES * NE]

        SCATTERS = 2 * TILES

        def experts(eng, block, start=None, finish=None):
            def run(g, i, nth, first, end):
                if start:
                    start(g, i, nth)
                if isinstance(g, int):
                    block(0, i)
                with eng.Fori(first, end) as b:
                    block(b, i)
                if finish:
                    finish(g)

            run(0, 0, 0, 1, SBLK)
            eng.wait_ge(bounds_ready, 1)
            with eng.Fori(0, NE // 2) as pair:
                for i in (1, 0):
                    g = pair * 2 + (2 - i)
                    first = eng.value_load(bounds[0:1, bass.ds(g, 1)], min_val=SBLK,
                                           max_val=MAX_BLK - 1)
                    end = eng.value_load(bounds[0:1, bass.ds(g + 1, 1)], min_val=SBLK + 1,
                                         max_val=MAX_BLK)
                    run(g, i, pair + (1 - i), first, end)

        def experts_sync(sp):
            def rows(buf, b):
                return buf[bass.ds(b * BLK, BLK), :].rearrange("(p a) m -> p a m", a=2)

            def load_rows(b):
                after(sp, pt_ready, b)
                sp.dma_start(R[:], rows(v_rows, b)).then_inc(rows_loaded, 16)

            def store_y(b):
                sp.wait_ge(y_done, 2 * b + 2)
                sp.dma_start(rows(y_rows, b), yb[:]).then_inc(y_stored, 16)

            sp.wait_ge(lg_done, NIMG)
            sp.wait_ge(consts, 8)
            sp.wait_ge(cls_dve, 12)
            sp.dma_start(v_rows[NT * P:NT * P + P, :], v_all[:, NT, :]).then_inc(rest_stored, 16)
            sp.dma_start(v_rows[NT * P + P:NT * P + 2 * P, :], zero_rows[:, 0, :]
                         ).then_inc(rest_stored, 16)
            sp.wait_ge(v_stored, 32 * NIMG)
            sp.wait_ge(rest_stored, 32)
            sp.wait_ge(y_zeroed, 16 * len(range(MIN_BLK * BLK, ROWS, BLK)))
            load_rows(0)
            load_rows(1)
            store_y(0)
            sp.wait_ge(bounds_ready, 1)
            for e in range(NE + 1):
                k = min(e + 2, NE + 1)
                end = sp.value_load(bounds[0:1, k:k + 1], min_val=SBLK + 1, max_val=MAX_BLK)
                last = end - 1 if e < NE else end
                sp.dma_start(rows(v_rows, last), zero_rows[:]).then_inc(tails_zeroed, 16)
            with sp.Fori(1, SBLK - 1) as b:
                load_rows(b + 1)
                store_y(b)
            sp.wait_ge(tails_zeroed, 16 * (NE + 1))
            sp.wait_ge(scattered, 16 * SCATTERS)
            end = sp.value_load(bounds[0:1, NE + 1:NE + 2], min_val=SBLK + 1, max_val=MAX_BLK)
            with sp.Fori(SBLK - 1, end) as b:
                load_rows(b + 1)
                store_y(b)

        def load_stage(pool, g):
            after(pool, w_split, g)
            pool.dma_start(stage1[:], expert_of(fc_w, g).rearrange("(k p) n -> p k n", p=P)
                           ).then_inc(staged, 16)
            pool.dma_start(stage2[:], expert_of(pj_w, g).rearrange("(j p) m -> p j m", p=P)
                           ).then_inc(staged, 16)

        def load_biases(pool, g, i):
            pool.dma_start(fcb[i][:], expert_of(fc_b, g)).then_inc(biases_loaded[i], 16)
            pool.dma_start(pjb[i][:], expert_of(pj_b, g).to_broadcast([P, M])).then_inc(biases_loaded[i], 16)

        def expert_of(w, g):
            if isinstance(g, int):
                return w[g]
            return w[bass.ds(g, 1)].rearrange("a c n -> (a c) n")

        HALF = FT * HID // 512
        CHUNKS = 2 * HALF

        def split_weights(pool, g, i, chunks=range(CHUNKS)):
            pool_wait(pool, staged, g * 32 + 32)
            for q in chunks:
                stage, high, low = (stage1, W1H, W1L) if q < HALF else (stage2, W2H, W2L)
                cols = slice((q % HALF) * 512, (q % HALF + 1) * 512)
                src, hi, lo = (b[:].rearrange("p a b -> p (a b)")[:, cols]
                               for b in (stage, high[i], low[i]))
                pool.tensor_copy(hi, src).then_inc(hi_split, 1)
                pool.wait_ge(hi_split, g * CHUNKS + (q + 1))
                last = pool.tensor_tensor(lo, src, hi.bitcast(F32), ALU.subtract)
                if q == CHUNKS - 1:
                    last.then_inc(w_split, 1)

        def experts_pool(pool):
            pool.wait_ge(lg_done, NIMG)
            pool.iota(iota_i[:], [[1, NE]], base=-NE, channel_multiplier=0).then_inc(route_pool, 1)
            pool.iota(dump_i[:], [[P, 2]], base=DUMP, channel_multiplier=1).then_inc(route_pool, 1)
            split_weights(pool, 1, 1)
            load_stage(pool, 2)
            pool.wait_ge(tails_zeroed, 16 * (NE + 1))
            pool.wait_ge(slots_ready, 1)
            for t in range(TILES):
                for k in range(2):
                    pool.indirect_dma_start(out=v_rows, out_offset=bass.IndirectOffsetOnAxis(
                        ap=slots[:, t, k:k + 1], axis=0), in_=v_all[:, t, :], in_offset=None
                    ).then_inc(scattered, 16)

            def next_weights(g, i, more=True):
                pool.wait_ge(expert_done, g - 1)
                load_biases(pool, g, i)
                split_weights(pool, g, i)
                if more:
                    load_stage(pool, g + 1)

            with pool.Fori(1, NE // 2) as pair:
                for i in range(2):
                    next_weights(pair * 2 + i, i)
            next_weights(NE, 0, more=False)

        def experts_tensor(pe):
            pe.wait_ge(route_dve, ROUTE_MASK)
            mask = big["mask"][:].rearrange("p t e -> p (t e)")
            pe.matmul(ps_rank, before[:], mask, start=True, stop=True)
            pe.matmul(ps_tot, ones_pp[:], mask, start=True, stop=True).then_inc(route_pe, 1)

            def transpose_rows(b):
                pe.wait_ge(rows_loaded, b * 16 + 16)
                after(pe, xl_ready, b)
                for a in range(2):
                    for f in range(FT):
                        last = pe.transpose(ps_t[:, f, a * P:(a + 1) * P],
                                            R[:, a, f * P:(f + 1) * P], ident[:])
                last.then_inc(pt_ready, 1)

            def fc(b, i, j):
                if j >= FC_SLOTS:
                    pe.wait_ge(gelu_done, b * HT + (j - FC_SLOTS + 1))
                parts = [(w, x, k) for w, x in ((W1H, XH), (W1L, XH), (W1H, XL)) for k in range(FT)]
                for q, (w, x, k) in enumerate(parts):
                    last = pe.matmul(ps_fc[j % FC_SLOTS], w[i][:, k, j * P:(j + 1) * P], x[:, k, :],
                                     start=(q == 0), stop=(q == len(parts) - 1))
                last.then_inc(fc_ready, 1)

            def project_hidden(b, i, j):
                pe.wait_ge(gl_done, b * HT + (j + 1))
                if j == 0:
                    after(pe, y_done, b * 2)
                for a in range(2):
                    parts = [(GH, W2H), (GH, W2L), (GL, W2H)]
                    for q, (gx, w) in enumerate(parts):
                        last = pe.matmul(ps_y[a], gx[:, j, a * P:(a + 1) * P], w[i][:, j, :],
                                         start=(j == 0 and q == 0), stop=(j == HT - 1 and q == 2))
                    if j == HT - 1:
                        last.then_inc(y_ps, 1)

            def start(g, i, nth):
                wait_apart(pe, w_split, g + 1)

            def block(b, i):
                pe.wait_ge(xl_ready, b + 1)
                for j in range(HT):
                    fc(b, i, j)
                    if j >= LAG:
                        project_hidden(b, i, j - LAG)
                transpose_rows(b + 1)
                for j in range(HT - LAG, HT):
                    project_hidden(b, i, j)

            pe.wait_ge(route_dve, ROUTE_RANK)
            transpose_rows(0)
            experts(pe, block, start)

        def experts_scalar(act):
            act.wait_ge(route_dve, ROUTE_SUB)
            act.activation(big["exp"][:], big["sub"][:], ACT.Exp).then_inc(route_act, 1)

            def high_x(b):
                act.wait_ge(pt_ready, b + 1)
                act.copy(XH[:], ps_t[:]).then_inc(xh_ready, 1)

            def start(g, i, nth):
                act.wait_ge(biases_loaded[i], nth * 32 + 32)

            def block(b, i):
                for j in range(HT):
                    act.wait_ge(fc_ready, b * HT + (j + 1))
                    if j >= G_SLOTS:
                        act.wait_ge(gl_done, b * HT + (j - G_SLOTS + 1))
                    act.activation(g_act[:, j % G_SLOTS, :], ps_fc[j % FC_SLOTS],
                                   ACT.Gelu_apprx_tanh, bias=fcb[i][:, j:j + 1]
                                   ).then_inc(gelu_done, 1)
                high_x(b + 1)

            high_x(0)
            experts(act, block, start)

        def route(dve):
            count = [0]

            def did(instruction):
                count[0] += 1
                instruction.then_inc(route_dve, 1)
                dve.wait_ge(route_dve, count[0])

            def over_e(a):
                return a[:].unsqueeze(2).to_broadcast([P, TILES, NE])

            def over_t(a):
                return a[:].unsqueeze(1).to_broadcast([P, TILES, NE])

            dve.wait_ge(route_pool, 2)
            did(dve.tensor_copy(iota_m[:], iota_i[:]))
            did(dve.tensor_copy(dump_f[:], dump_i[:]))
            did(dve.scalar_tensor_tensor(dump[:], dump_f[:], valid, dump_f[:], ALU.mult,
                                         ALU.subtract))
            did(dve.tensor_scalar(dump[:], dump[:], -1.0, None, ALU.mult))
            did(dve.tensor_reduce(small["max"][:], logits[:], AX.X, ALU.max))
            did(dve.tensor_tensor(big["sub"][:], logits[:], over_e(small["max"]), ALU.subtract))
            assert count[0] == ROUTE_SUB
            dve.wait_ge(route_act, 1)
            did(dve.tensor_reduce(small["sum"][:], big["exp"][:], AX.X, ALU.add))
            did(dve.reciprocal(small["rec"][:], small["sum"][:]))
            did(dve.tensor_tensor(big["prob"][:], big["exp"][:], over_e(small["rec"]), ALU.mult))
            prob = big["prob"]
            for k in range(2):
                one = big[f"one{k}"]
                did(dve.tensor_reduce(small[f"m{k}"][:], prob[:], AX.X, ALU.max))
                did(dve.tensor_tensor(big["hit"][:], prob[:], over_e(small[f"m{k}"]), ALU.is_equal))
                did(dve.tensor_tensor(big["cand"][:], big["hit"][:], over_t(iota_m), ALU.mult))
                did(dve.tensor_reduce(small["idx"][:], big["cand"][:], AX.X, ALU.min))
                did(dve.tensor_tensor(one[:], over_t(iota_m), over_e(small["idx"]), ALU.is_equal))
                if k == 0:
                    did(dve.scalar_tensor_tensor(big["prob2"][:], one[:], -2.0, prob[:], ALU.mult,
                                                 ALU.add))
                    prob = big["prob2"]
            did(dve.tensor_tensor(big["mask"][:], big["one0"][:], big["one1"][:], ALU.add))
            did(dve.tensor_scalar(big["mask"][:, NT, :], big["mask"][:, NT, :], valid, None,
                                  ALU.mult))
            assert count[0] == ROUTE_MASK
            did(dve.tensor_tensor(small["gsum"][:], small["m0"][:], small["m1"][:], ALU.add))
            did(dve.reciprocal(small["grec"][:], small["gsum"][:]))
            for k in range(2):
                did(dve.tensor_tensor(gates[:, :, k], small[f"m{k}"][:], small["grec"][:], ALU.mult))
            dve.wait_ge(route_pe, 1)
            tot, incl, pos = big["tot"], big["incl"], big["pos"]
            did(dve.tensor_copy(tot[:].rearrange("p t e -> p (t e)"), ps_tot))
            for e in range(NE):
                did(dve.tensor_tensor_scan(incl[:, :, e], ones_pp[:, 0:TILES], tot[:, :, e], 0.0,
                                           ALU.mult, ALU.add))
            did(dve.tensor_tensor(pos[:], incl[:], tot[:], ALU.subtract))
            did(dve.tensor_tensor(pos[:].rearrange("p t e -> p (t e)"),
                                  pos[:].rearrange("p t e -> p (t e)"), ps_rank, ALU.add))
            assert count[0] == ROUTE_RANK
            did(dve.tensor_scalar(cnt_i[:], incl[:, NT, :], float(BLK - 1), None, ALU.add))
            did(dve.tensor_scalar(cnt_s[:], cnt_i[:], BLK.bit_length() - 1, None,
                                  ALU.arith_shift_right))
            did(dve.tensor_copy(cnt["n"][:], cnt_s[:]))
            did(dve.tensor_scalar(cnt["at_least"][:], cnt["n"][:], 1.0, None, ALU.max))
            did(dve.tensor_tensor_scan(cnt["end"][:], ones_pp[:, 0:NE], cnt["at_least"][:],
                                       float(SBLK), ALU.mult, ALU.add))
            did(dve.tensor_tensor(cnt["start"][:], cnt["end"][:], cnt["at_least"][:], ALU.subtract))
            did(dve.memset(bounds[:, 0:1], 0))
            did(dve.tensor_copy(bounds[:, 1:2], cnt["start"][:, 0:1]))
            dve.tensor_copy(bounds[:, 2:NE + 2], cnt["end"][:]).then_inc(bounds_ready, 1)
            did(dve.tensor_scalar(cnt["start"][:], cnt["start"][:], float(BLK), None, ALU.mult))
            did(dve.tensor_tensor(pos[:], pos[:], over_t(cnt["start"]), ALU.add))
            for k in range(2):
                did(dve.tensor_tensor(big["sel"][:], big[f"one{k}"][:], pos[:], ALU.mult))
                did(dve.tensor_reduce(slot_f[:, :, k], big["sel"][:], AX.X, ALU.add))
            did(dve.scalar_tensor_tensor(slot_f[:, NT, :], slot_f[:, NT, :], valid, dump[:],
                                         ALU.mult, ALU.add))
            dve.tensor_copy(slots[:], slot_f[:]).then_inc(slots_ready, 1)

        def experts_vector(dve):
            route(dve)

            def low_x(b):
                dve.wait_ge(xh_ready, b + 1)
                dve.tensor_tensor(XL[:], ps_t[:], XH[:].bitcast(F32), ALU.subtract
                                  ).then_inc(xl_ready, 1)

            def low_g(b, j):
                dve.wait_ge(gh_done, b * HT + (j + 1))
                dve.tensor_tensor(GL[:, j, :], g_act[:, j % G_SLOTS, :], GH[:, j, :].bitcast(F32),
                                  ALU.subtract).then_inc(gl_done, 1)

            def start(g, i, nth):
                lone_wait(dve, biases_loaded[i], nth * 32 + 32)

            def block(b, i):
                for j in range(HT):
                    dve.wait_ge(gelu_done, b * HT + (j + 1))
                    dve.tensor_copy(GH[:, j, :], g_act[:, j % G_SLOTS, :]).then_inc(gh_done, 1)
                    if j:
                        low_g(b, j - 1)
                low_g(b, HT - 1)
                low_x(b + 1)
                for a in range(2):
                    dve.wait_ge(y_ps, b * 2 + (a + 1))
                    if a == 0:
                        after(dve, y_stored, b * 16)
                    dve.tensor_tensor(yb[:, a, :], ps_y[a], pjb[i][:], ALU.add).then_inc(y_done, 1)

            def finish(g):
                dve.memset(wait_carrier_d[:], 0.0).then_inc(expert_done, 1)

            low_x(0)
            experts(dve, block, start, finish)

        def combine_pool(pool):
            end = pool.value_load(bounds[0:1, NE + 1:NE + 2], min_val=SBLK + 1, max_val=MAX_BLK)
            pool_wait(pool, y_stored, end * 16)
            for t in range(TILES):
                if t >= DEEP:
                    pool.wait_ge(sum_done, t - DEEP + 1)
                for k, buf in enumerate((ya, yc)):
                    pool.indirect_dma_start(out=buf[t % DEEP][:], out_offset=None, in_=y_rows,
                                            in_offset=bass.IndirectOffsetOnAxis(
                                                ap=slots[:, t, k:k + 1], axis=0)
                                            ).then_inc(gathered[k][t % DEEP], 16)

        def combine_sync(sp):
            end = sp.value_load(bounds[0:1, NE + 1:NE + 2], min_val=SBLK + 1, max_val=MAX_BLK)
            sp.wait_ge(y_stored, end * 16)

            def store(t):
                sp.wait_ge(sum_done, t + 1)
                if t < NT:
                    n, lt = divmod(t, LT)
                    sp.dma_start(out[n, 1 + lt * P:1 + (lt + 1) * P, :], o2[t % DEEP][:]
                                 ).then_inc(out_stored[t % DEEP], 16)
                else:
                    sp.dma_start(out[:, 0, :].rearrange("(a n) m -> a n m", a=1),
                                 o2[t % DEEP][0:1, :].unsqueeze(1).to_broadcast([1, NIMG, M])
                                 ).then_inc(out_stored[t % DEEP], 16)

            for t in range(TILES):
                if t >= DEEP:
                    sp.wait_ge(sum_done, t - DEEP + 1)
                sp.dma_start(ysh[t % DEEP][:], y_rows[t * P:(t + 1) * P, :]).then_inc(ysh_loaded[t % DEEP], 16)
                if t >= 1:
                    store(t - 1)
            store(TILES - 1)
            for d in range(DEEP):
                sp.wait_ge(out_stored[d], 16 * len(range(d, TILES, DEEP)))

        def combine_vector(dve):
            for t in range(TILES):
                if True:
                    d = t % DEEP
                    p = P if t < NT else 1
                    dve.wait_ge(gathered[0][d], 16 * (t // DEEP + 1))
                    dve.scalar_tensor_tensor(o1[d][0:p, :], ya[d][0:p, :], gates[0:p, t, 0:1], h_all[0:p, t, :],
                                             ALU.mult, ALU.add).then_inc(first_added, 1)
                    dve.wait_ge(gathered[1][d], 16 * (t // DEEP + 1))
                    dve.wait_ge(first_added, t + 1)
                    dve.scalar_tensor_tensor(o1[d][0:p, :], yc[d][0:p, :], gates[0:p, t, 1:2], o1[d][0:p, :],
                                             ALU.mult, ALU.add).then_inc(combined_both, 1)
                    dve.wait_ge(combined_both, t + 1)
                    dve.wait_ge(ysh_loaded[d], 16 * (t // DEEP + 1))
                    if t >= DEEP:
                        dve.wait_ge(out_stored[d], 16 * (t // DEEP))
                    last = dve.tensor_tensor(o2[d][0:p, :], o1[d][0:p, :], ysh[d][0:p, :], ALU.add)
                    last.then_inc(sum_done, 1)

        block = ctx.enter_context(nc.Block())

        @block.sync
        def _(sp):
            steps(sp, mixer_sync(sp))
            experts_sync(sp)
            combine_sync(sp)

        @block.gpsimd
        def _(pool):
            steps(pool, mixer_pool(pool))
            experts_pool(pool)
            combine_pool(pool)

        @block.scalar
        def _(act):
            steps(act, mixer_scalar(act))
            experts_scalar(act)

        @block.vector
        def _(dve):
            steps(dve, mixer_vector(dve))
            experts_vector(dve)
            combine_vector(dve)

        @block.tensor
        def _(pe):
            steps(pe, mixer_tensor(pe))
            experts_tensor(pe)


def kernel(**inputs):
    import numpy as np
    import concourse.bacc as bacc
    from concourse import mybir as my
    from concourse.bass_utils import run_bass_kernel_spmd as run

    g = {k: np.asarray(v) for k, v in inputs.items()}
    x = g["x"]
    nimg, c, length, heads = x.shape
    d = g["L0_tok_Wq_w"].shape[0]
    m = heads * d
    w_proj = np.concatenate([np.concatenate([g[f"L0_tok_W{i}_w"].T, g[f"L0_tok_W{i}_b"][None]], 0)
                             for i in "qkv"], 1)
    w_resid = np.concatenate([np.broadcast_to(np.eye(c, dtype=x.dtype)[:, None, :], (c, heads, d)),
                              g["L0_tok_out_b"].reshape(1, heads, d)], 0)
    arrays = {
        "x": x.reshape(nimg, c, length * heads),
        "cls_tok": g["cls_tok"].reshape(1, m),
        "w_proj": w_proj, "w_resid": w_resid,
        "bias_t": g["L0_tok_w_bias"].T,
        "mask_t": np.ascontiguousarray(g["L0_tok_local_mask"].T).view(np.int32),
        "out_w": g["L0_tok_out_w"], "ln_g": g["L0_tok_ln_g"], "ln_b": g["L0_tok_ln_b"],
        "w_in": g["L0_attn_W_in"], "w_r": g["L0_attn_W_r"], "w_i": g["L0_attn_W_i"],
        "w_out": g["L0_attn_W_out"], "b_in": g["L0_attn_b_in"], "b_r": g["L0_attn_b_r"],
        "b_i": g["L0_attn_b_i"], "b_out": g["L0_attn_b_out"], "log_a": g["L0_attn_log_a"],
        "w_route": g["L0_ffn_Wr"],
        "fc_w": np.concatenate([g["L0_ffn_Wfc_s"][None], g["L0_ffn_Wfc"]], 0),
        "fc_b": np.concatenate([g["L0_ffn_bfc_s"][None], g["L0_ffn_bfc"]], 0)
        .reshape(-1, g["L0_ffn_bfc"].shape[1] // 128, 128).transpose(0, 2, 1),
        "pj_w": np.concatenate([g["L0_ffn_Wproj_s"][None], g["L0_ffn_Wproj"]], 0),
        "pj_b": np.concatenate([g["L0_ffn_bproj_s"][None], g["L0_ffn_bproj"]], 0)[:, None, :],
    }
    nc = bacc.Bacc("TRN2", target_bir_lowering=False, num_devices=1)
    args = []
    for name, a in list(arrays.items()):
        arrays[name] = a = np.ascontiguousarray(a)
        args.append(nc.dram_tensor(name, a.shape, my.dt.from_np(a.dtype), kind="ExternalInput").ap())
    out = nc.dram_tensor("out", (nimg, length + 1, m), my.dt.float32, kind="ExternalOutput").ap()
    vit_tower(nc, *args, out)
    r = run(nc, [arrays], core_ids=[0])
    return r.results[0]["out"]
```

```python
import concourse.bass as bass
from concourse import mybir
from contextlib import ExitStack


def vit_tower(nc, x, cls_tok, w_proj, w_resid, bias_t, mask_t, out_w, ln_g, ln_b, w_in, w_r, w_i,
              w_out, b_in, b_r, b_i, b_out, log_a, w_route, fc_w, fc_b, pj_w, pj_b, out):
    F32, F32R, I32, U32, U8 = (mybir.dt.float32, mybir.dt.float32r, mybir.dt.int32,
                               mybir.dt.uint32, mybir.dt.uint8)
    ALU, ACT, AX = mybir.AluOpType, mybir.ActivationFunctionType, mybir.AxisListType
    P = 128
    NIMG, C, LH = x.shape
    H = w_resid.shape[1]
    L = LH // H
    D = C
    M = H * D
    LT, FT = L // P, M // P
    KA = C + 1
    NE = w_route.shape[1]
    HID = fc_w.shape[2]
    HT = HID // P
    BLK = L
    TOK = NIMG * L + 1
    SEQ = L + 1
    CLS_ROW = NIMG * SEQ
    TAIL_ROW = CLS_ROW + 1
    LIST_BLKS = (TOK + BLK - 1) // BLK + 1
    LIST = LIST_BLKS * BLK
    DUMP = NE * LIST
    SBLK = NIMG + 1
    MIN_BLKS = 2
    MAX_BLK = 2 * TOK // BLK + MIN_BLKS * NE
    FIRST_E, GATE_DIFF, GATE2, OUT_ROW = M, M + 1, M + 2, M + 3
    W = M + 4
    EPS = 1e-5
    BIG = 3e38

    v_rows = nc.dram_tensor("v_rows", (DUMP + 2 * P, W), F32, kind="Internal").ap()

    ctx = ExitStack()
    with ctx:
        memory = ctx

        def sb(name, shape, dt=F32):
            return memory.enter_context(nc.sbuf_tensor(name, shape, dt))

        def sem(name):
            return ctx.enter_context(nc.semaphore(name))

        def ps(name, shape):
            return ctx.enter_context(nc.psum_tensor(name, shape, F32))

        ident = sb("ident", [P, P])
        ones_pp = sb("ones_pp", [P, P])
        before = sb("before", [P, P])
        minus_half = sb("minus_half", [P, 2])
        eps = sb("eps", [P, 2])
        carrier = {k: sb(f"carrier_{k}", [1, 1]) for k in ("dve", "end", "count", "pool", "start", "y", "set", "stage")}
        iota_i = sb("iota_i", [P, NE], I32)
        iota_m = sb("iota_m", [P, NE])
        list_i = sb("list_i", [P, NE], I32)
        list_f = sb("list_f", [P, NE])
        lines_i = sb("lines_i", [P, 3, 2], I32)
        lines_f = sb("lines_f", [P, 3, 2])
        block_i = sb("block_i", [P, MAX_BLK + 1], I32)
        block_f = sb("block_f", [P, MAX_BLK + 1])
        tail_rows = sb("tail_rows", [P, 2, W])
        zeros = sb("zeros", [P, 2, M])
        stage1 = sb("stage1", [P, FT, HID])
        stage2 = sb("stage2", [P, HT, M])
        W1H = [sb(f"w1h{i}", [P, FT, HID], F32R) for i in range(2)]
        W1L = [sb(f"w1l{i}", [P, FT, HID], F32R) for i in range(2)]
        W2H = [sb(f"w2h{i}", [P, HT, M], F32R) for i in range(2)]
        W2L = [sb(f"w2l{i}", [P, HT, M], F32R) for i in range(2)]
        fcb = [sb(f"fcb{i}", [P, HT]) for i in range(2)]
        pjb = [sb(f"pjb{i}", [P, M]) for i in range(2)]
        number = [sb(f"number{i}", [P, 1]) for i in range(2)]
        G_SLOTS = 4
        g_act = sb("g_act", [P, G_SLOTS, BLK])
        GH = sb("GH", [P, HT, BLK], F32R)
        GL = sb("GL", [P, HT, BLK], F32R)
        XH = [sb(f"xh{i}", [P, FT, BLK], F32R) for i in range(2)]
        XL = [sb(f"xl{i}", [P, FT, BLK], F32R) for i in range(2)]
        yb = sb("yb", [P, 2, M])
        run = sb("run", [P, NE])
        rlg = sb("rlg", [P, LT, NE])
        rlg2 = sb("rlg2", [P, LT, NE])
        rhit = sb("rhit", [P, LT, NE])
        rcand = sb("rcand", [P, LT, NE])
        ridx = sb("ridx", [P, 2, LT])
        rone = [sb(f"rone{i}", [P, LT, NE]) for i in range(2)]
        rmax = [sb(f"rmax{i}", [P, LT]) for i in range(2)]
        rmask = sb("rmask", [P, LT, NE])
        rdif = sb("rdif", [P, LT])
        rexp = sb("rexp", [P, LT])
        rden_g = sb("rden_g", [P, LT])
        rg1 = sb("rg1", [P, LT])
        rpos = sb("rpos", [P, LT, NE])
        rsel = [sb(f"rsel{i}", [P, LT, NE]) for i in range(2)]
        rslot = sb("rslot", [P, 2, LT])
        slots = [sb(f"slots{i}", [P, 2, LT], U32) for i in range(2)]
        cnt_i = sb("cnt_i", [P, NE], I32)
        cnt_s = sb("cnt_s", [P, NE], I32)
        ends_i = sb("ends_i", [P, NE], I32)
        cnt = {k: sb(f"c_{k}", [P, NE]) for k in ("size", "n", "blocks", "end", "start", "skip")}
        bounds = sb("bounds", [P, NE + 1], I32)
        where = sb("where", [P, MAX_BLK + 1])
        hop = sb("hop", [P, NE, MAX_BLK + 1])
        where_i = sb("where_i", [P, MAX_BLK + 1], I32)
        CXH = sb("CXH", [P, FT, 2], F32R)
        CXL = sb("CXL", [P, FT, 2], F32R)
        c_h1 = sb("c_h1", [1, M])
        c_y = sb("c_y", [1, M])
        mixer_memory = ExitStack()
        memory = mixer_memory
        wproj = sb("wproj", [KA, 3 * D])
        wresid = sb("wresid", [KA, H, D])
        ewT = sb("ewT", [P, LT, L])
        mask_sb = sb("mask_sb", [P, LT, L // 4], I32)
        outw_sb = sb("outw_sb", [P, FT, M])
        gates_h = [sb(f"gates_h{i}", [P, FT, M], F32R) for i in range(3)]
        gates_l = [sb(f"gates_l{i}", [P, FT, M], F32R) for i in range(3)]
        wout_sb = sb("wout_sb", [P, FT, M])
        route_sb = sb("route_sb", [P, FT, NE])
        route_h = sb("route_h", [P, FT, NE], F32R)
        route_l = sb("route_l", [P, FT, NE], F32R)
        lng_bc = sb("lng_bc", [P, M])
        lnb_bc = sb("lnb_bc", [P, M])
        bout_bc = sb("bout_bc", [P, M])
        col_raw = sb("col_raw", [P, 4, FT])
        bhalf = sb("bhalf", [P, 2, FT])
        a_clip = sb("a_clip", [P, 2, FT])
        a_exp = sb("a_exp", [P, 2, FT])
        a_rec = sb("a_rec", [P, FT])
        a_den = sb("a_den", [P, FT])
        a_half = sb("a_half", [P, FT])
        X = [sb(f"x{i}", [KA, LH]) for i in range(2)]
        E = sb("E", [P, LT, 2 * M])
        tanh_q = sb("tanh_q", [P, LT, M])
        rden = sb("rden", [P, LT, M])
        Y = sb("Y", [P, LT, M])
        YT = sb("YT", [P, FT, L])
        H0 = [sb(f"h0_{i}", [P, LT, M]) for i in range(2)]
        H1 = [sb(f"h1_{i}", [P, LT, M]) for i in range(2)]
        U = sb("U", [P, LT, M])
        V = [sb(f"v{i}", [P, LT, W]) for i in range(2)]
        UTH = sb("UTH", [P, FT, L], F32R)
        UTL = sb("UTL", [P, FT, L], F32R)
        TR = sb("TR", [P, FT, L])
        TI = sb("TI", [P, FT, L])
        A = sb("A", [P, FT, L])
        S = sb("S", [P, FT, L])
        HS = sb("HS", [P, FT, L])
        st = [sb(f"st{i}", [P, LT, 6]) for i in range(3)]
        mv = [sb(f"mv{i}", [P, LT, 2]) for i in range(3)]
        ve = [sb(f"ve{i}", [P, LT]) for i in range(3)]
        rstd = [sb(f"rstd{i}", [P, LT]) for i in range(3)]
        gates_raw = [b[:].rearrange("p a m -> p (a m)").rearrange("p (a m) -> p a m", a=FT)
                     for b in (TR, TI, A)]
        mask_f = S
        c_row = sb("c_row", [1, M])
        c_u = sb("c_u", [1, M])
        c_st = [sb(f"c_st{i}", [1, 6]) for i in range(2)]
        c_mv = [sb(f"c_mv{i}", [1, 2]) for i in range(2)]
        c_ve = [sb(f"c_ve{i}", [1, 2]) for i in range(2)]
        c_rs = [sb(f"c_rs{i}", [1, 2]) for i in range(2)]
        c_uh = sb("c_uh", [P, FT, 2], F32R)
        c_ul = sb("c_ul", [P, FT, 2], F32R)
        c_g = sb("c_g", [P, 2, FT])
        c_a = sb("c_a", [P, FT])
        c_om = sb("c_om", [P, FT])
        c_s = sb("c_s", [P, FT])
        c_h = sb("c_h", [P, FT])
        CV = sb("CV", [P, W])
        mixer_memory.close()
        expert_memory = ExitStack()
        memory = expert_memory
        R = sb("R", [P, 2, W])
        info = sb("info", [P, 2, 4])
        info_t = sb("info_t", [P, 2])
        gate = sb("gate", [P, 2])
        rows_to = sb("rows_to", [P, 2], U32)
        yt = sb("yt", [P, 2, M])
        expert_memory.close()
        memory = ctx
        ps_proj = ps("ps_proj", [P, H, 256])
        ps_nd = ps("ps_nd", [P, 2, 2 * M])
        ps_t = ps("ps_t", [P, FT, L])
        ps_h = ps("ps_h", [P, LT, M])
        ps_ri = ps("ps_ri", [P, 2, L])
        ps_ip = ps("ps_ip", [P, FT, L])
        ps_lg = ps_ri[:, 0, 0:LT * NE].rearrange("p (t e) -> p t e", e=NE)
        ps_rank = ps_ri[:, 0, 64:64 + LT * NE].rearrange("p (t e) -> p t e", e=NE)
        ps_tot = ps_ri[:, 0, 128:128 + NE]
        fc_loop = [ps_proj[:, 0, :], ps_proj[:, 2, :]]
        y_loop = [ps_nd[:, 0, 0:M], ps_nd[:, 1, 0:M]]
        fc_after = fc_loop + [ps_ri[:, 0, :], ps_ip[:, 0, :]]

        w_loaded, cls_loaded = sem("w_loaded"), sem("cls_loaded")
        x_loaded = [sem(f"x_loaded{i}") for i in range(2)]
        gate_w_loaded, gate_w_split = sem("gate_w_loaded"), sem("gate_w_split")
        consts, prep, prep_act = sem("consts"), sem("prep"), sem("prep_act")
        ones_in_x, base_stored = sem("ones_in_x"), sem("base_stored")
        proj_ready, exp_done, tq_done = sem("proj_ready"), sem("exp_done"), sem("tq_done")
        ekv_done, nd_ready, t1_done = sem("ekv_done"), sem("nd_ready"), sem("t1_done")
        recip_done, y_ready = sem("recip_done"), sem("y_ready")
        yT_ps, yT_sb, h_ready = sem("yT_ps"), sem("yT_sb"), sem("h_ready")
        raw = [sem(f"stats{i}") for i in range(3)]
        mv_done = [sem(f"mv_done{i}") for i in range(3)]
        ve_done = [sem(f"ve_done{i}") for i in range(3)]
        rstd_done = [sem(f"rstd_done{i}") for i in range(3)]
        hn_done, hg_done, h0_done, h0b_done = (sem("hn_done"), sem("hg_done"), sem("h0_done"),
                                               sem("h0b_done"))
        u_ready, uT_ps, uh_done, ul_done = sem("u_ready"), sem("uT_ps"), sem("uh_done"), sem("ul_done")
        ri_ready, ip_ready, tanh_done = sem("ri_ready"), sem("ip_ready"), sem("tanh_done")
        a_done, om_done, s_done = sem("a_done"), sem("om_done"), sem("s_done")
        b_done, scan_done, attn_ready = sem("b_done"), sem("scan_done"), sem("attn_ready")
        h1_done, v_ready, vT_ps = sem("h1_done"), sem("v_ready"), sem("vT_ps")
        vh_done, vl_done = sem("vh_done"), sem("vl_done")
        lg_ready, route_dve, route_act, rank_ready = (sem("lg_ready"), sem("route_dve"),
                                                      sem("route_act"), sem("rank_ready"))
        slots_ready = sem("slots_ready")
        scattered = [sem(f"scattered{i}") for i in range(2)]
        cls_scattered, cls_slots = sem("cls_scattered"), sem("cls_slots")
        cls_pe, cls_act, cls_dve, cls_pool = (sem("cls_pe"), sem("cls_act"), sem("cls_dve"),
                                              sem("cls_pool"))
        staged, high_loaded, w_split = sem("staged"), sem("high_loaded"), sem("w_split")
        biases_loaded = [sem(f"biases_loaded{i}") for i in range(2)]
        expert_done = sem("expert_done")
        bounds_ready, ends_ready, where_ready = sem("bounds_ready"), sem("ends_ready"), sem("where_ready")
        count_dve, tails_stored = sem("count_dve"), sem("tails_stored")
        rows_loaded, info_read, pt_ready, xh_ready, xl_ready = (
            sem("rows_loaded"), sem("info_read"), sem("pt_ready"), sem("xh_ready"), sem("xl_ready"))
        fc_ready, gelu_done, gh_done, gl_done = (sem("fc_ready"), sem("gelu_done"), sem("gh_done"),
                                                 sem("gl_done"))
        y_ps, y_done, yt_done, sum_done = sem("y_ps"), sem("y_done"), sem("yt_done"), sem("sum_done")
        info_done, added = sem("info_done"), sem("added")
        cls_base, cls_out = sem("cls_base"), sem("cls_out")
        lnb_loaded, lines, route_w = sem("lnb_loaded"), sem("lines"), sem("route_w")
        lg_done, mask_done, dif_done = sem("lg_done"), sem("mask_done"), sem("dif_done")
        seconds_stored = sem("seconds_stored")
        run_ready, sel_done = sem("run_ready"), sem("sel_done")
        carried = sem("carried")
        cls_row1, cls_s = sem("cls_row1"), sem("cls_s")

        DEPTH = 5
        PEEL = DEPTH + DEPTH % 2

        def steps(step):
            def over(eng):
                for t in range(PEEL):
                    step(t, t % 2)
                with eng.Fori(PEEL // 2, NIMG // 2) as pair:
                    step(pair * 2, 0)
                    step(pair * 2 + 1, 1)
                for t in range(NIMG, NIMG + DEPTH - 1):
                    step(t, t % 2)
            return over

        def live(n):
            return not isinstance(n, int) or 0 <= n < NIMG

        def after(eng, semaphore, value):
            if not isinstance(value, int) or value > 0:
                eng.wait_ge(semaphore, value)

        def at_most(value, limit):
            return min(value, limit) if isinstance(value, int) else value

        CONSTS = 14
        CLS_MASK, CLS_ROUTE, ROUTE = 15, 29, 19

        def dve_wait(dve, semaphore, value, use="dve"):
            dve.wait_ge(semaphore, value)
            if not isinstance(value, int):
                dve.memset(carrier[use][:], 0.0)

        def pool_wait(pool, semaphore, value, use="pool"):
            pool.wait_ge(semaphore, value)
            if not isinstance(value, int):
                return pool.tensor_tensor(carrier[use][:], minus_half[0:1, 0:1], minus_half[0:1, 0:1],
                                          ALU.add)

        def flat(buf):
            return buf[:].rearrange("p a b -> p (a b)")

        def over_lt(a):
            return a[:].unsqueeze(1).to_broadcast([P, LT, a.shape[1]])

        def over_e(a):
            return a.unsqueeze(2).to_broadcast([P, LT, NE])

        W_LOADS = 13
        GATE_W = (w_r, w_i, w_in)
        halves = ((0, 0), (1, 0), (0, 1))

        def store_base(sp, n):
            sp.wait_ge(sum_done, n + 1)
            dst = out[bass.ds(n * SEQ + 1, L), :].rearrange("(a p) m -> p a m", p=P)
            sp.dma_start(dst, yb[:]).then_inc(base_stored, 16)

        def mixer_sync(sp):
            def load_x(n, par):
                after(sp, h_ready, LT * (n - 1))
                sp.dma_start(X[par][0:C, :], x[n]).then_inc(x_loaded[par], 16)

            rows = "(t p) m -> p t m"
            sp.dma_start(c_row[:], cls_tok).then_inc(cls_loaded, 16)
            sp.dma_start(wproj[:], w_proj).then_inc(w_loaded, 16)
            load_x(0, 0)
            with nc.allow_non_contiguous_dma(reason="256 values as columns"):
                for i, src in enumerate((b_r, b_i, log_a, b_in)):
                    sp.dma_start(col_raw[:, i], src.rearrange("(t p) -> p t", p=P)
                                 ).then_inc(w_loaded, 16)
            for dst, src in ((mask_sb, mask_t), (ewT, bias_t)):
                sp.dma_start(dst[:], src.rearrange(rows, p=P)).then_inc(w_loaded, 16)
            for dst, src in zip(gates_raw, GATE_W):
                sp.dma_start(dst, src.rearrange(rows, p=P)).then_inc(gate_w_loaded, 16)
            load_x(1, 1)
            for dst, src in ((wout_sb, w_out), (outw_sb, out_w)):
                sp.dma_start(dst[:], src.rearrange(rows, p=P)).then_inc(w_loaded, 16)
            sp.dma_start(route_sb[:], w_route.rearrange(rows, p=P)).then_inc(w_loaded, 16)
            sp.dma_start(wresid[:], w_resid).then_inc(w_loaded, 16)
            for dst, src in ((lng_bc, ln_g), (bout_bc, b_out)):
                sp.dma_start(dst[:], src.rearrange("(a m) -> a m", a=1).to_broadcast([P, M])
                             ).then_inc(w_loaded, 16)
            sp.dma_start(lnb_bc[:], ln_b.rearrange("(a m) -> a m", a=1).to_broadcast([P, M])
                         ).then_inc(lnb_loaded, 16)
            sp.wait_ge(lines, 2)
            for e in range(NE):
                sp.dma_start(v_rows[e * LIST + BLK:e * LIST + 2 * BLK, :]
                             .rearrange("(p a) m -> p a m", a=2), tail_rows[:]
                             ).then_inc(seconds_stored, 16)

            def step(t, par):
                if live(t) and not (isinstance(t, int) and t < 2):
                    load_x(t, par)
                if live(t - 5):
                    store_base(sp, t - 5)

            return step

        def experts_sync(sp):
            def rows(b):
                return v_rows[bass.ds(b * BLK, BLK), :].rearrange("(p a) m -> p a m", a=2)

            def load_rows(b, source):
                after(sp, pt_ready, b)
                after(sp, info_read, b)
                sp.dma_start(R[:], rows(source)).then_inc(rows_loaded, 16)

            store_base(sp, NIMG - 1)
            sp.wait_ge(ends_ready, 1)
            for e in range(NE):
                end = sp.value_load(ends_i[0:1, e:e + 1], min_val=e * LIST, max_val=e * LIST + TOK)
                sp.dma_start(v_rows[bass.ds(end, BLK), :].rearrange("(p a) m -> p a m", a=2),
                             tail_rows[:]).then_inc(tails_stored, 16)
            sp.wait_ge(tails_stored, 16 * NE)
            sp.wait_ge(cls_scattered, 32)
            for i in range(2):
                sp.wait_ge(scattered[i], 16 * 2 * LT * (NIMG // 2))
            load_rows(0, 0)
            sp.wait_ge(cls_base, 1)
            sp.dma_start(out[CLS_ROW:CLS_ROW + 1, :], c_y[:]).then_inc(base_stored, 16)
            sp.wait_ge(where_ready, 1)
            end = sp.value_load(bounds[0:1, NE:NE + 1], min_val=MIN_BLKS * NE,
                                max_val=MAX_BLK)
            with sp.Fori(1, end) as b:
                source = sp.value_load(where_i[0:1, bass.ds(b, 1)], min_val=0,
                                       max_val=NE * LIST_BLKS - 1)
                load_rows(b, source)
            sp.wait_ge(pt_ready, end)
            sp.wait_ge(info_read, end)
            sp.dma_start(R[:], rows(0)).then_inc(rows_loaded, 16)
            sp.wait_ge(added, end * 32 + 32)
            sp.wait_ge(rows_loaded, end * 16 + 16)
            sp.dma_start(c_y[:], out[CLS_ROW:CLS_ROW + 1, :]).then_inc(cls_out, 16)
            sp.wait_ge(cls_out, 16)
            first_rows = out[0:NIMG * SEQ, :].rearrange("(n s) m -> n s m", s=SEQ)[:, 0, :]
            sp.dma_start(first_rows.rearrange("(a n) m -> a n m", a=1),
                         c_y[:].unsqueeze(1).to_broadcast([1, NIMG, M])).then_inc(cls_out, 16)
            sp.wait_ge(cls_out, 32)
            sp.wait_ge(base_stored, 16 * (NIMG + 1))


        def expert_of(w, g):
            if isinstance(g, int):
                return w[g]
            return w[bass.ds(g, 1)].rearrange("a c n -> (a c) n")

        def fc_of(g):
            return expert_of(fc_w, g).rearrange("(k p) n -> p k n", p=P)

        def pj_of(g):
            return expert_of(pj_w, g).rearrange("(j p) m -> p j m", p=P)

        def load_stage(pool, g):
            if not isinstance(g, int) or g > 0:
                pool_wait(pool, w_split, g, "stage")
            pool.dma_start(stage1[:], fc_of(g)).then_inc(staged, 16)
            pool.dma_start(stage2[:], pj_of(g)).then_inc(staged, 16)

        def load_high(pool, g, i):
            if not isinstance(g, int) or g > 1:
                pool_wait(pool, expert_done, g - 1, "set")
            pool.dma_start(W1H[i][:], fc_of(g)).then_inc(high_loaded, 16)
            pool.dma_start(W2H[i][:], pj_of(g)).then_inc(high_loaded, 16)
            pool.dma_start(fcb[i][:], expert_of(fc_b, g)).then_inc(biases_loaded[i], 16)
            pool.dma_start(pjb[i][:], expert_of(pj_b, g).to_broadcast([P, M])
                           ).then_inc(biases_loaded[i], 16)

        PARTS = 4

        def split_low(pool, g, i, part=None):
            if part in (None, 0):
                pool.wait_ge(staged, g * 32 + 32)
                pool.wait_ge(high_loaded, g * 32 + 32)
            for q in range(PARTS) if part is None else (part,):
                stage, high, low = ((stage1, W1H, W1L), (stage2, W2H, W2L))[q * 2 // PARTS]
                n = 2 * FT * HID // PARTS
                cols = slice((q % (PARTS // 2)) * n, (q % (PARTS // 2) + 1) * n)
                last = pool.tensor_tensor(flat(low[i])[:, cols], flat(stage)[:, cols],
                                          flat(high[i])[:, cols].bitcast(F32), ALU.subtract)
            if part in (None, PARTS - 1):
                last.then_inc(w_split, 1)

        def inv_std(pool, i, n):
            pool.wait_ge(mv_done[i], LT * (n + 1))
            pool.tensor_tensor(ve[i][:], mv[i][:, :, 1], eps[:], ALU.add).then_inc(ve_done[i], 1)
            pool.wait_ge(ve_done[i], n + 1)
            after(pool, [hn_done, u_ready, v_ready][i], LT * n)
            pool.tensor_tensor(rstd[i][:], ve[i][:], minus_half[:], ALU.pow
                               ).then_inc(rstd_done[i], 1)

        def scatter(pool, source, where_to, semaphore):
            pool.indirect_dma_start(out=v_rows, out_offset=bass.IndirectOffsetOnAxis(
                ap=where_to, axis=0), in_=source, in_offset=None).then_inc(semaphore, 16)

        def mixer_pool(pool):
            pool.memset(minus_half[:], -0.5).then_inc(consts, 1)
            pool.memset(eps[:], EPS).then_inc(consts, 1)
            pool.memset(ones_pp[:], 1.0).then_inc(consts, 1)
            pool.memset(ident[:], 0.0).then_inc(consts, 1)
            pool.memset(zeros[:], 0.0).then_inc(consts, 1)
            pool.memset(tail_rows[:], 0.0).then_inc(consts, 1)
            pool.memset(CV[:], 0.0).then_inc(consts, 1)
            pool.wait_ge(consts, 7)
            pool.affine_select(out=ident[:], in_=ident[:], compare_op=ALU.not_equal, fill=1.0,
                               base=0, pattern=[[-1, P]], channel_multiplier=1).then_inc(consts, 1)
            pool.affine_select(out=before[:], in_=ones_pp[:], compare_op=ALU.is_gt, fill=0.0,
                               base=0, pattern=[[1, P]], channel_multiplier=-1).then_inc(consts, 1)
            pool.iota(iota_i[:], [[1, NE]], base=-NE, channel_multiplier=0).then_inc(consts, 1)
            pool.iota(list_i[:], [[LIST, NE]], base=0, channel_multiplier=0).then_inc(consts, 1)
            pool.iota(block_i[:], [[1, MAX_BLK + 1]], base=0, channel_multiplier=0
                      ).then_inc(consts, 1)
            pool.iota(lines_i[:, 0], [[P, 2]], base=DUMP, channel_multiplier=1)
            pool.iota(lines_i[:, 1], [[P, 2]], base=TAIL_ROW, channel_multiplier=1
                      ).then_inc(consts, 1)
            pool.iota(lines_i[:, 2], [[P, 2]], base=1, channel_multiplier=1).then_inc(consts, 1)
            load_high(pool, 0, 0)
            load_stage(pool, 0)
            pool.wait_ge(consts, CONSTS)

            for a in range(2):
                pool.dma_start(out[TAIL_ROW + a * P:TAIL_ROW + (a + 1) * P, :], zeros[:, a, :]
                               ).then_inc(added, 16)

            def cls_inv_std(i, count):
                pool.wait_ge(cls_dve, count)
                pool.tensor_tensor(c_ve[i][:, 0:1], c_mv[i][:, 1:2], eps[0:1, 0:1], ALU.add
                                   ).then_inc(cls_pool, 1)
                pool.wait_ge(cls_pool, 2 * i + 1)
                pool.tensor_tensor(c_rs[i][:, 0:1], c_ve[i][:, 0:1], minus_half[0:1, 0:1], ALU.pow
                                   ).then_inc(cls_pool, 1)

            cls_inv_std(0, 2)

            def step(t, par):
                if live(t - 3):
                    inv_std(pool, 2, t - 3)
                if live(t - 1):
                    n = t - 1
                    h0 = H0[1 - par]
                    inv_std(pool, 0, n)
                    if isinstance(n, int) and n == 0:
                        pool.wait_ge(w_loaded, 16 * W_LOADS)
                        pool.wait_ge(lnb_loaded, 16)
                    for i, (bc, semaphore, done) in enumerate((
                            (lng_bc, (hn_done, LT * (n + 1)), hg_done),
                            (lnb_bc, (hg_done, n + 1), h0_done))):
                        pool.wait_ge(*semaphore)
                        pool.tensor_tensor(h0[:], h0[:], over_lt(bc), (ALU.mult, ALU.add)[i]
                                           ).then_inc(done, 1)
                    inv_std(pool, 1, n)
                    pool.wait_ge(u_ready, LT * (n + 1))
                    pool.tensor_tensor(h0[:], h0[:], over_lt(bout_bc), ALU.add
                                       ).then_inc(h0b_done, 1)
                if isinstance(t, int) and t == 1:
                    cls_inv_std(1, 9)
                if isinstance(t, int) and t == 2:
                    split_low(pool, 0, 0)
                    load_high(pool, 1, 1)
                    load_stage(pool, 1)
                if isinstance(t, int) and t == 3:
                    pool.wait_ge(seconds_stored, 16 * NE)
                    pool.wait_ge(cls_slots, 1)
                    for k in range(2):
                        scatter(pool, CV[:], slots[1][:, k, 0:1], cls_scattered)
                    split_low(pool, 1, 1)
                if live(t - 4):
                    n = t - 4
                    pool_wait(pool, slots_ready, n + 1)
                    for k in range(2):
                        for lt in range(LT):
                            scatter(pool, V[par][:, lt, :], slots[par][:, k, lt:lt + 1],
                                    scattered[par])

            return step

        def experts_pool(pool):
            load_stage(pool, 2)

            def add_rows(b):
                pool.wait_ge(carried, b * 2 + 1)
                pool_wait(pool, added, b * 32 + 32).then_inc(carried, 1)
                pool.wait_ge(carried, b * 2 + 2)
                pool_wait(pool, y_done, b * 2 + (2 * SBLK + 2), "y").then_inc(carried, 1)
                for a in range(2):
                    pool.indirect_dma_start(
                        out=out, out_offset=bass.IndirectOffsetOnAxis(ap=rows_to[:, a:a + 1],
                                                                      axis=0),
                        in_=yb[:, a, :], in_offset=None, compute_op=ALU.add).then_inc(added, 16)

            def expert(g, i, first, end, prefetch):
                if prefetch:
                    load_high(pool, g + 1, 1 - i)
                add_rows(first)
                if prefetch:
                    split_low(pool, g + 1, 1 - i)
                if prefetch == 2:
                    load_stage(pool, g + 2)
                with pool.Fori(first + 1, end) as b:
                    add_rows(b)

            def limits(g):
                first = pool.value_load(bounds[0:1, bass.ds(g - 1, 1)], min_val=0,
                                        max_val=MAX_BLK - MIN_BLKS)
                end = pool.value_load(bounds[0:1, bass.ds(g, 1)], min_val=MIN_BLKS,
                                      max_val=MAX_BLK)
                return first, end

            pool.wait_ge(bounds_ready, 1)
            pool.wait_ge(base_stored, 16 * (NIMG + 1))
            pool.tensor_tensor(carrier["start"][:], minus_half[0:1, 0:1], minus_half[0:1, 0:1],
                               ALU.add).then_inc(carried, 1)
            with pool.Fori(0, NE // 2 - 1) as pair:
                for i in (1, 0):
                    g = pair * 2 + (2 - i)
                    expert(g, i, *limits(g), 2)
            expert(NE - 1, 1, *limits(NE - 1), 1)
            expert(NE, 0, *limits(NE), 0)

        def split_product(pe, dst, w, cols, x, width=None):
            parts = [(a, b, k) for a, b in halves for k in range(FT)]
            for q, (a, b, k) in enumerate(parts):
                rhs = x[b][:, k, :] if width is None else x[b][:, k, 0:width]
                last = pe.matmul(dst, w[a][:, k, cols], rhs, start=(q == 0),
                                 stop=(q == len(parts) - 1))
            return last

        def fc(pe, b, i, j, xs, banks):
            if j >= len(banks):
                pe.wait_ge(gelu_done, b * HT + (j - len(banks) + 1))
            split_product(pe, banks[j % len(banks)], (W1H[i], W1L[i]), slice(j * P, (j + 1) * P), xs
                          ).then_inc(fc_ready, 1)

        def project_hidden(pe, b, i, j, banks):
            pe.wait_ge(gl_done, b * HT + (j + 1))
            for a in range(2):
                for q, (g, w) in enumerate(((GH, W2H), (GH, W2L), (GL, W2H))):
                    last = pe.matmul(banks[a], g[:, j, a * P:(a + 1) * P], w[i][:, j, :],
                                     start=(j == 0 and q == 0), stop=(j == HT - 1 and q == 2))
                if j == HT - 1:
                    last.then_inc(y_ps, 1)

        LAG = 3

        def mixer_tensor(pe):
            def columns(row, dst):
                for k in range(FT):
                    for c in range(2):
                        last = pe.matmul(dst[:, 2 * k + c:2 * k + c + 1],
                                         row[0:1, k * P:(k + 1) * P], ones_pp[0:1, 0:1],
                                         start=True, stop=True)
                return last

            def cls_a():
                pe.wait_ge(consts, CONSTS)
                pe.wait_ge(cls_dve, 3)
                columns(c_u, ps_ip[:, 0, :]).then_inc(cls_pe, 1)
                pe.wait_ge(gate_w_split, 6)
                pe.wait_ge(cls_dve, 4)
                for i in range(3):
                    for e in range(FT):
                        dst = ps_ri[:, i // 2, ((i % 2) * FT + e) * 2:((i % 2) * FT + e) * 2 + 2]
                        last = split_product(pe, dst, (gates_h[i], gates_l[i]),
                                             slice(e * P, (e + 1) * P), (c_uh, c_ul))
                last.then_inc(cls_pe, 1)

            def cls_b():
                pe.wait_ge(cls_dve, 7)
                pe.wait_ge(hn_done, LT)
                for k in range(FT):
                    last = pe.matmul(ps_h[0:1, 0, :], c_h[:, k:k + 1], wout_sb[:, k, :],
                                     start=(k == 0), stop=(k == FT - 1))
                last.then_inc(cls_pe, 1)

            def cls_c():
                pe.wait_ge(cls_dve, 10)
                pe.wait_ge(b_done, FT)
                columns(CV, ps_ip[:, 0, :]).then_inc(cls_pe, 1)
                pe.wait_ge(cls_dve, 11)
                pe.wait_ge(prep, 8)
                pe.wait_ge(tanh_done, FT)
                for q, (a, b, k) in enumerate([(a, b, k) for a, b in halves for k in range(FT)]):
                    last = pe.matmul(ps_lg[0:2, 0, :], (CXH, CXL)[b][:, k, :],
                                     (route_h, route_l)[a][:, k, :], start=(q == 0),
                                     stop=(q == 3 * FT - 1))
                last.then_inc(cls_pe, 1)

            def cls_d():
                pe.wait_ge(route_dve, CLS_MASK)
                pe.wait_ge(tanh_done, 2 * FT)
                pe.matmul(ps_tot, ones_pp[:], rmask[:, 0, :], start=True, stop=True
                          ).then_inc(cls_pe, 1)

            def head_view(par, lt, h):
                return X[par].rearrange("c (l h) -> c l h", h=H)[:, lt * P:(lt + 1) * P, h]

            def project(n, par, lt):
                pe.wait_ge(x_loaded[par], 8 * (n - par) + 16)
                after(pe, ekv_done, LT * n + lt)
                if lt == 0 and live(n - 5):
                    pe.wait_ge(gelu_done, HT * (n - 4))
                for h in range(H):
                    last = pe.matmul(ps_proj[:, h, 0:3 * D], head_view(par, lt, h), wproj[:],
                                     start=True, stop=True)
                last.then_inc(proj_ready, 1)

            def transposes(src):
                for lt in range(LT):
                    for f in range(FT):
                        last = pe.transpose(ps_t[:, f, lt * P:(lt + 1) * P],
                                            src[:, lt, f * P:(f + 1) * P], ident[:])
                return last

            def gate_pair(n, e):
                if e == 0:
                    pe.wait_ge(ul_done, n + 1)
                    if live(n - 2):
                        pe.wait_ge(run_ready, n)
                    elif n == 0:
                        pe.wait_ge(cls_dve, 7)
                        pe.wait_ge(cls_act, 2)
                    else:
                        pe.wait_ge(route_dve, 2)
                after(pe, tanh_done, FT * n + e)
                for i in range(2):
                    last = split_product(pe, ps_ri[:, i, :], (gates_h[i], gates_l[i]),
                                         slice(e * P, (e + 1) * P), (UTH, UTL))
                last.then_inc(ri_ready, 1)

            def input_gate(n, e):
                if e == 0:
                    after(pe, b_done, FT * n)
                    if isinstance(n, int) and n == 1:
                        pe.wait_ge(cls_dve, 11)
                split_product(pe, ps_ip[:, e, :], (gates_h[2], gates_l[2]),
                              slice(e * P, (e + 1) * P), (UTH, UTL)).then_inc(ip_ready, 1)

            def transpose_u(n):
                pe.wait_ge(u_ready, LT * (n + 1))
                after(pe, vl_done, n - 1)
                transposes(U).then_inc(uT_ps, 1)

            def ranks(n):
                pe.wait_ge(mask_done, n + 1)
                for lt in range(LT):
                    for k in range(lt + 1):
                        pe.matmul(ps_rank[:, lt, :], (before if k == lt else ones_pp)[:],
                                  rmask[:, k, :], start=(k == 0), stop=(k == lt))
                for k in range(LT):
                    last = pe.matmul(ps_tot, ones_pp[:], rmask[:, k, :], start=(k == 0),
                                     stop=(k == LT - 1))
                last.then_inc(rank_ready, 1)

            pe.wait_ge(w_loaded, 16 * W_LOADS)
            pe.wait_ge(ones_in_x, 2)

            def step(t, par):
                if live(t - 3):
                    n = t - 3
                    pe.wait_ge(scan_done, FT * (n + 1))
                    pe.wait_ge(hn_done, at_most(LT * (n + 2), LT * NIMG))
                    for lt in range(LT):
                        for k in range(FT):
                            last = pe.matmul(ps_h[:, lt, :], HS[:, k, lt * P:(lt + 1) * P],
                                             wout_sb[:, k, :], start=(k == 0), stop=(k == FT - 1))
                    last.then_inc(attn_ready, 1)
                if live(t):
                    project(t, par, 0)
                if live(t - 1):
                    n = t - 1
                    pe.wait_ge(y_ready, n + 1)
                    after(pe, ul_done, n)
                    transposes(Y).then_inc(yT_ps, 1)
                if live(t):
                    project(t, par, 1)
                if live(t - 4):
                    n = t - 4
                    pe.wait_ge(vl_done, n + 1)
                    pe.wait_ge(run_ready, n + 1)
                    pe.wait_ge(tanh_done, at_most(FT * (n + 2), FT * NIMG))
                    for lt in range(LT):
                        for q, (a, b, k) in enumerate([(a, b, k) for a, b in halves
                                                       for k in range(FT)]):
                            last = pe.matmul(ps_lg[:, lt, :],
                                             (XH, XL)[b][par][:, k, lt * P:(lt + 1) * P],
                                             (route_h, route_l)[a][:, k, :], start=(q == 0),
                                             stop=(q == 3 * FT - 1))
                    last.then_inc(lg_ready, 1)
                if live(t - 1):
                    n = t - 1
                    pe.wait_ge(yT_sb, n + 1)
                    after(pe, h1_done, n - 1)
                    if isinstance(n, int) and n == 1:
                        pe.wait_ge(cls_row1, 1)
                    for lt in range(LT):
                        for f in range(FT):
                            pe.matmul(ps_h[:, lt, :], YT[:, f, lt * P:(lt + 1) * P],
                                      outw_sb[:, f, :], start=(f == 0), stop=False)
                        for h in range(H):
                            last = pe.matmul(ps_h[:, lt, h * D:(h + 1) * D],
                                             head_view(1 - par, lt, h), wresid[:, h, :],
                                             start=False, stop=(h == H - 1))
                        last.then_inc(h_ready, 1)
                if live(t):
                    n = t
                    if isinstance(n, int) and n == 0:
                        pe.wait_ge(prep_act, 1)
                    pe.wait_ge(ekv_done, LT * (n + 1))
                    after(pe, t1_done, LT * n)
                    after(pe, y_done, 2 * (n - 4))
                    for tt in range(LT):
                        for s in range(LT):
                            last = pe.matmul(ps_nd[:, tt, :], ewT[:, s, tt * P:(tt + 1) * P],
                                             E[:, s, :], start=(s == 0), stop=(s == LT - 1))
                        last.then_inc(nd_ready, 1)
                if live(t - 3):
                    n = t - 3
                    pe.wait_ge(v_ready, LT * (n + 1))
                    pe.wait_ge(yT_sb, at_most(n + 3, NIMG))
                    if isinstance(t, int) and t > NIMG:
                        pe.wait_ge(ul_done, NIMG)
                        pe.wait_ge(vl_done, n)
                    transposes(V[1 - par]).then_inc(vT_ps, 1)

                others = {}
                if live(t - 2):
                    others[3] = lambda: gate_pair(t - 2, 0)
                    others[6] = lambda: input_gate(t - 2, 0)
                    others[8] = lambda: gate_pair(t - 2, 1)
                    others[9] = lambda: input_gate(t - 2, 1)
                if live(t - 1):
                    others[12] = lambda: transpose_u(t - 1)
                if live(t - 4):
                    others[1] = lambda: ranks(t - 4)
                n = t - 4
                parts = []
                for j in range(HT + LAG):
                    if j < HT:
                        parts.append((fc, j, fc_loop))
                    if j >= LAG:
                        parts.append((project_hidden, j - LAG, y_loop))
                for q, (part, j, banks) in enumerate(parts):
                    if live(n):
                        if q == 0 and isinstance(n, int) and n == 0:
                            pe.wait_ge(w_split, 1)
                        if q == 0 and not live(t):
                            pe.wait_ge(gelu_done, HT * n)
                        if part is fc:
                            fc(pe, n, 0, j, (XH[par], XL[par]), banks)
                        else:
                            if j == 0 and live(t):
                                pe.wait_ge(t1_done, LT * (t + 1))
                            elif j == 0:
                                after(pe, y_done, 2 * n)
                            project_hidden(pe, n, 0, j, banks)
                    if q in others:
                        others[q]()
                if isinstance(t, int) and t == 0:
                    cls_a()
                if isinstance(t, int) and t == 1:
                    cls_b()
                if isinstance(t, int) and t == 2:
                    cls_c()
                if isinstance(t, int) and t == 3:
                    cls_d()

            return step

        def experts_tensor(pe):
            b = NIMG
            for j in range(HT):
                if j >= len(fc_loop):
                    pe.wait_ge(gelu_done, b * HT + (j - len(fc_loop) + 1))
                split_product(pe, fc_loop[j % 2][:, 0:2], (W1H[0], W1L[0]),
                              slice(j * P, (j + 1) * P), (CXH, CXL)).then_inc(fc_ready, 1)
            pe.wait_ge(gl_done, b * HT + HT)
            pe.wait_ge(y_done, 2 * b)
            for j in range(HT):
                for q, (g, w) in enumerate(((GH, W2H), (GH, W2L), (GL, W2H))):
                    last = pe.matmul(y_loop[0][0:2, :], g[:, j, 0:2], w[0][:, j, :],
                                     start=(j == 0 and q == 0), stop=(j == HT - 1 and q == 2))
            last.then_inc(y_ps, 2)

            def transpose_rows(b):
                pe.wait_ge(rows_loaded, b * 16 + 16)
                after(pe, xl_ready, b)
                for a in range(2):
                    for f in range(FT):
                        last = pe.transpose(ps_t[:, f, a * P:(a + 1) * P],
                                            R[:, a, f * P:(f + 1) * P], ident[:])
                last.then_inc(pt_ready, 1)

            def block(b, i, g):
                pe.wait_ge(w_split, g + 1)
                pe.wait_ge(xl_ready, b + 1)
                for j in range(HT):
                    fc(pe, b + SBLK, i, j, (XH[0], XL[0]), fc_after)
                    if j >= LAG:
                        if j == LAG:
                            pe.wait_ge(y_done, b * 2 + 2 * SBLK)
                        project_hidden(pe, b + SBLK, i, j - LAG, y_loop)
                transpose_rows(b + 1)
                for j in range(HT - LAG, HT):
                    project_hidden(pe, b + SBLK, i, j, y_loop)

            pe.wait_ge(vl_done, NIMG)
            transpose_rows(0)
            pe.wait_ge(b_done, FT * NIMG)
            experts(pe, block)

        def experts(eng, block, start=None, finish=None):
            eng.wait_ge(bounds_ready, 1)
            with eng.Fori(0, NE // 2) as pair:
                for i in (1, 0):
                    g = pair * 2 + (2 - i)
                    first = eng.value_load(bounds[0:1, bass.ds(g - 1, 1)], min_val=0,
                                           max_val=MAX_BLK - MIN_BLKS)
                    end = eng.value_load(bounds[0:1, bass.ds(g, 1)], min_val=MIN_BLKS,
                                         max_val=MAX_BLK)
                    if start:
                        start(g, i, pair + (1 - i))
                    with eng.Fori(first, end) as b:
                        block(b, i, g)
                    if finish:
                        finish(g, i)

        def gelu(act, b, i, j, banks, width=BLK):
            act.wait_ge(fc_ready, b * HT + (j + 1))
            if j >= G_SLOTS:
                act.wait_ge(gl_done, b * HT + (j - G_SLOTS + 1))
            act.activation(g_act[:, j % G_SLOTS, 0:width], banks[j % len(banks)][:, 0:width],
                           ACT.Gelu_apprx_tanh, bias=fcb[i][:, j:j + 1]).then_inc(gelu_done, 1)

        def mixer_scalar(act):
            def exp_and_tanh(n, lt):
                act.wait_ge(proj_ready, LT * n + lt + 1)
                after(act, nd_ready, LT * n)
                act.activation(E[:, lt, M:2 * M].rearrange("p (h d) -> p h d", h=H),
                               ps_proj[:, :, D:2 * D], ACT.Exp).then_inc(exp_done, 1)
                after(act, t1_done, LT * n)
                act.activation(tanh_q[:, lt, :].rearrange("p (h d) -> p h d", h=H),
                               ps_proj[:, :, 0:D], ACT.Tanh, scale=0.5).then_inc(tq_done, 1)

            def high_g(n, j):
                act.wait_ge(gelu_done, n * HT + (j + 1))
                act.copy(GH[:, j, :], g_act[:, j % G_SLOTS, :]).then_inc(gh_done, 1)

            def tanh_gates(n, e):
                act.wait_ge(ri_ready, FT * n + e + 1)
                after(act, s_done, n)
                if isinstance(n, int) and n == 0:
                    act.wait_ge(gate_w_split, 6)
                act.activation(TR[:, e, :], ps_ri[:, 0, :], ACT.Tanh, bias=bhalf[:, 0, e:e + 1],
                               scale=0.5)
                act.activation(TI[:, e, :], ps_ri[:, 1, :], ACT.Tanh, bias=bhalf[:, 1, e:e + 1],
                               scale=0.5).then_inc(tanh_done, 1)

            act.wait_ge(prep, 2)
            act.activation(ewT[:], ewT[:], ACT.Exp).then_inc(prep_act, 1)
            act.wait_ge(prep, 4)
            act.activation(a_exp[:, 0], a_clip[:, 0], ACT.Exp)
            act.activation(a_exp[:, 1], a_clip[:, 1], ACT.Exp, scale=-1.0).then_inc(prep_act, 1)

            def step(t, par):
                if live(t):
                    exp_and_tanh(t, 0)
                if live(t - 1):
                    act.wait_ge(yT_ps, t)
                    act.copy(YT[:], ps_t[:]).then_inc(yT_sb, 1)
                if live(t):
                    exp_and_tanh(t, 1)
                if live(t - 4):
                    n = t - 4
                    act.wait_ge(dif_done, n + 2)
                    act.activation(rexp[:], rdif[:], ACT.Exp).then_inc(route_act, 1)
                if live(t - 3):
                    n = t - 3
                    act.wait_ge(vT_ps, n + 1)
                    after(act, fc_ready, HT * (n - 1))
                    act.copy(XH[1 - par][:], ps_t[:]).then_inc(vh_done, 1)
                n = t - 4
                for j in range(HT + 1):
                    if live(n):
                        if isinstance(n, int) and n == 0 and j == 0:
                            act.wait_ge(biases_loaded[0], 32)
                        if j < HT:
                            gelu(act, n, 0, j, fc_loop)
                        if j:
                            high_g(n, j - 1)
                    if live(t - 2) and j in (3, 5):
                        tanh_gates(t - 2, j // 5)
                    if live(t - 1) and j == 7:
                        act.wait_ge(uT_ps, t)
                        after(act, ip_ready, FT * (t - 1))
                        act.copy(UTH[:], ps_t[:]).then_inc(uh_done, 1)
                if isinstance(t, int) and t == 0:
                    act.wait_ge(cls_pe, 1)
                    act.copy(c_uh[:].rearrange("p k c -> p (k c)"), ps_ip[:, 0, 0:2 * FT]
                             ).then_inc(cls_act, 1)
                    act.wait_ge(cls_pe, 2)
                    act.wait_ge(prep, 3)
                    for i in range(2):
                        for e in range(FT):
                            c = (i * FT + e) * 2
                            last = act.activation(c_g[:, i, e:e + 1], ps_ri[:, 0, c:c + 1],
                                                  ACT.Tanh, bias=bhalf[:, i, e:e + 1], scale=0.5)
                    last.then_inc(cls_act, 1)
                if isinstance(t, int) and t == 2:
                    act.wait_ge(cls_pe, 4)
                    act.copy(CXH[:].rearrange("p k c -> p (k c)"), ps_ip[:, 0, 0:2 * FT]
                             ).then_inc(cls_act, 1)
                    act.wait_ge(dif_done, 1)
                    act.activation(rexp[:], rdif[:], ACT.Exp).then_inc(route_act, 1)

            return step

        def experts_scalar(act):
            for j in range(HT):
                gelu(act, NIMG, 0, j, fc_loop, 2)

            def high_x(b):
                act.wait_ge(pt_ready, b + 1)
                act.copy(XH[0][:], ps_t[:]).then_inc(xh_ready, 1)

            def start(g, i, nth):
                act.wait_ge(biases_loaded[i], nth * 32 + 32)

            def block(b, i, g):
                for j in range(HT):
                    gelu(act, b + SBLK, i, j, fc_after)
                high_x(b + 1)

            high_x(0)
            experts(act, block, start)

        def low_g(dve, b, j, width=BLK):
            dve.wait_ge(gh_done, b * HT + (j + 1))
            dve.tensor_tensor(GL[:, j, 0:width], g_act[:, j % G_SLOTS, 0:width],
                              GH[:, j, 0:width].bitcast(F32), ALU.subtract).then_inc(gl_done, 1)

        def mixer_vector(dve):
            seen = [0]

            def routed(n, instruction, k):
                instruction.then_inc(route_dve, 1)
                dve.wait_ge(route_dve, ROUTE * n + (CLS_ROUTE + k))

            def stats(i, srcs, n):
                for lt, src in enumerate(srcs):
                    dve.bn_stats(st[i][:, lt, :], src).then_inc(raw[i], 1)
                dve_wait(dve, raw[i], LT * (n + 1))
                for lt in range(LT):
                    dve.bn_aggr(mv[i][:, lt, :], st[i][:, lt, :]).then_inc(mv_done[i], 1)

            def norm(i, dst, src, lt):
                return dve.tensor_scalar(dst, src, mv[i][:, lt, 0:1], rstd[i][:, lt:lt + 1],
                                         ALU.subtract, ALU.mult)

            def choose(chain, valid=None):
                source = rlg
                for k in range(2):
                    chain(dve.tensor_reduce(rmax[k][:], source[:], AX.X, ALU.max))
                    chain(dve.tensor_tensor(rhit[:], source[:], over_e(rmax[k][:]), ALU.is_equal))
                    chain(dve.tensor_tensor(rcand[:], rhit[:], over_lt(iota_m), ALU.mult))
                    chain(dve.tensor_reduce(ridx[:, k, :], rcand[:], AX.X, ALU.min))
                    chain(dve.tensor_tensor(rone[k][:], over_lt(iota_m), over_e(ridx[:, k, :]),
                                            ALU.is_equal))
                    if k == 0:
                        chain(dve.scalar_tensor_tensor(rlg2[:], rone[0][:], -BIG, rlg[:], ALU.mult,
                                                       ALU.add))
                        source = rlg2

            def gates_of(v_cols, chain):
                chain(dve.tensor_scalar(rden_g[:], rexp[:], 1.0, None, ALU.add))
                chain(dve.reciprocal(rg1[:], rden_g[:]))
                chain(dve.tensor_tensor(v_cols[:, :, 2], rexp[:, 0:v_cols.shape[1]],
                                        rg1[:, 0:v_cols.shape[1]], ALU.mult))
                chain(dve.tensor_tensor(v_cols[:, :, 1], rg1[:, 0:v_cols.shape[1]],
                                        v_cols[:, :, 2], ALU.subtract))

            for i in range(2):
                dve.memset(X[i][C:KA, :], 1.0).then_inc(ones_in_x, 1)
            dve.wait_ge(cls_loaded, 16)
            dve.bn_stats(c_st[0][:], c_row[:]).then_inc(cls_dve, 1)
            dve.wait_ge(cls_dve, 1)
            dve.bn_aggr(c_mv[0][:], c_st[0][:]).then_inc(cls_dve, 1)
            dve.wait_ge(w_loaded, 16 * W_LOADS)
            dve.tensor_copy(mask_f[:], mask_sb[:].bitcast(U8)).then_inc(prep, 1)
            dve.wait_ge(prep, 1)
            dve.tensor_tensor(ewT[:], ewT[:], mask_f[:], ALU.mult).then_inc(prep, 1)
            dve.tensor_scalar(bhalf[:], col_raw[:, 0:2], 0.5, None, ALU.mult).then_inc(prep, 1)
            for i, op in enumerate((ALU.min, ALU.max)):
                last = dve.tensor_scalar(a_clip[:, i], col_raw[:, 2], 0.0, None, op)
            last.then_inc(prep, 1)
            dve.wait_ge(cls_pool, 2)
            dve.tensor_scalar(c_u[:], c_row[:], c_mv[0][:, 0:1], c_rs[0][:, 0:1],
                              ALU.subtract, ALU.mult).then_inc(cls_dve, 1)
            dve.wait_ge(prep_act, 2)
            dve.tensor_tensor(a_den[:], a_exp[:, 0], a_exp[:, 1], ALU.add).then_inc(prep, 1)
            dve.wait_ge(prep, 5)
            dve.reciprocal(a_rec[:], a_den[:]).then_inc(prep, 1)
            dve.wait_ge(prep, 6)
            dve.scalar_tensor_tensor(a_half[:], a_exp[:, 0], 0.5, a_rec[:], ALU.mult, ALU.mult
                                     ).then_inc(prep, 1)
            for i in range(3):
                dve.wait_ge(gate_w_loaded, 48)
                dve.tensor_copy(gates_h[i][:], gates_raw[i]).then_inc(gate_w_split, 1)
            dve.wait_ge(gate_w_split, 3)
            for i in range(3):
                dve.tensor_tensor(gates_l[i][:], gates_raw[i], gates_h[i][:].bitcast(F32),
                                  ALU.subtract).then_inc(gate_w_split, 1)
            dve.tensor_copy(route_h[:], route_sb[:]).then_inc(route_w, 1)
            dve.wait_ge(route_w, 1)
            dve.tensor_tensor(route_l[:], route_sb[:], route_h[:].bitcast(F32), ALU.subtract
                              ).then_inc(prep, 1)
            dve.wait_ge(consts, CONSTS)
            dve.tensor_copy(iota_m[:], iota_i[:])
            dve.tensor_copy(list_f[:], list_i[:])
            dve.tensor_copy(block_f[:], block_i[:])
            dve.tensor_copy(lines_f[:], lines_i[:]).then_inc(lines, 1)
            dve.memset(number[1][:], float(-NE))
            dve.memset(number[0][:], float(1 - NE))
            dve.wait_ge(lines, 1)
            dve.tensor_copy(tail_rows[:, :, OUT_ROW], lines_f[:, 1]).then_inc(lines, 1)
            for i in range(2):
                dve.tensor_scalar(V[i][:, :, OUT_ROW], lines_f[:, 2], float((i - 2) * SEQ), None,
                                  ALU.add).then_inc(lines, 1)

            def cls_a():
                dve.wait_ge(cls_act, 1)
                dve.tensor_tensor(c_ul[:].rearrange("p k c -> p (k c)"), ps_ip[:, 0, 0:2 * FT],
                                  c_uh[:].rearrange("p k c -> p (k c)").bitcast(F32), ALU.subtract
                                  ).then_inc(cls_dve, 1)
                dve.wait_ge(cls_act, 2)
                dve.wait_ge(prep, 8)
                dve.scalar_tensor_tensor(c_a[:], c_g[:, 0], 1.0, a_half[:], ALU.add, ALU.mult
                                         ).then_inc(cls_dve, 1)
                dve.wait_ge(cls_dve, 5)
                dve.tensor_scalar(c_om[:], c_a[:], -0.5, 0.5, ALU.mult, ALU.add).then_inc(cls_dve, 1)
                dve.wait_ge(cls_dve, 6)
                dve.scalar_tensor_tensor(c_s[:], c_g[:, 1], 1.0, c_om[:], ALU.add, ALU.mult
                                         ).then_inc(cls_s, 1)
                dve.wait_ge(cls_s, 1)
                for e in range(FT):
                    last = dve.scalar_tensor_tensor(c_h[:, e:e + 1], ps_ri[:, 1, 2 * e:2 * e + 1],
                                                    col_raw[:, 3, e:e + 1], c_s[:, e:e + 1],
                                                    ALU.add, ALU.mult)
                last.then_inc(cls_dve, 1)

            def cls_b():
                dve.wait_ge(cls_pe, 3)
                dve.tensor_tensor(c_h1[:], c_row[:], ps_h[0:1, 0, :], ALU.add).then_inc(cls_row1, 1)
                dve.wait_ge(cls_row1, 1)
                dve.tensor_tensor(c_h1[:], c_h1[:], bout_bc[0:1, :], ALU.add).then_inc(cls_row1, 1)
                dve.wait_ge(cls_row1, 2)
                dve.bn_stats(c_st[1][:], c_h1[:]).then_inc(cls_dve, 1)
                dve.wait_ge(cls_dve, 8)
                dve.bn_aggr(c_mv[1][:], c_st[1][:]).then_inc(cls_dve, 1)
                dve.wait_ge(cls_pool, 4)
                dve.tensor_scalar(CV[0:1, 0:M], c_h1[:], c_mv[1][:, 0:1], c_rs[1][:, 0:1],
                                  ALU.subtract, ALU.mult).then_inc(cls_dve, 1)

            def cls_c():
                count = [0]

                def chain(instruction):
                    count[0] += 1
                    instruction.then_inc(route_dve, 1)
                    dve.wait_ge(route_dve, count[0])

                valid = ident[:, 0:1]
                dve.wait_ge(cls_act, 3)
                dve.tensor_tensor(CXL[:].rearrange("p k c -> p (k c)"), ps_ip[:, 0, 0:2 * FT],
                                  CXH[:].rearrange("p k c -> p (k c)").bitcast(F32), ALU.subtract
                                  ).then_inc(cls_dve, 1)
                chain(dve.memset(rlg[:], 0.0))
                dve.wait_ge(cls_pe, 5)
                chain(dve.tensor_copy(rlg[0:1, 0, :], ps_lg[0:1, 0, :]))
                choose(chain)
                chain(dve.tensor_tensor(rmask[:], rone[0][:], rone[1][:], ALU.add))
                chain(dve.tensor_scalar(rmask[:], rmask[:], valid, None, ALU.mult))
                assert count[0] == CLS_MASK, count
                dve.tensor_tensor(rdif[:], rmax[1][:], rmax[0][:], ALU.subtract
                                  ).then_inc(dif_done, 1)
                dve.wait_ge(route_act, 1)
                cv = CV[:].rearrange("p (a w) -> p a w", a=1)
                chain(dve.tensor_copy(CV[0:1, FIRST_E:FIRST_E + 1], ridx[0:1, 0, 0:1]))
                chain(dve.tensor_scalar(rden_g[:], rexp[:], 1.0, None, ALU.add))
                chain(dve.reciprocal(rg1[:], rden_g[:]))
                chain(dve.tensor_tensor(CV[0:1, GATE2:GATE2 + 1], rexp[0:1, 0:1], rg1[0:1, 0:1],
                                        ALU.mult))
                chain(dve.tensor_tensor(CV[0:1, GATE_DIFF:GATE_DIFF + 1], rg1[0:1, 0:1],
                                        CV[0:1, GATE2:GATE2 + 1], ALU.subtract))
                chain(dve.memset(CV[0:1, OUT_ROW:OUT_ROW + 1], float(CLS_ROW)))
                for k in range(2):
                    chain(dve.tensor_tensor(rsel[k][:], rone[k][:], over_lt(list_f), ALU.mult))
                    chain(dve.tensor_reduce(rslot[:, k, :], rsel[k][:], AX.X, ALU.add))
                    chain(dve.tensor_tensor(rsel[k][:, 0, 0:1], rslot[:, k, 0:1],
                                            lines_f[:, 0, k:k + 1], ALU.subtract))
                    chain(dve.scalar_tensor_tensor(rslot[:, k, 0:1], rsel[k][:, 0, 0:1], valid,
                                                   lines_f[:, 0, k:k + 1], ALU.mult, ALU.add))
                dve.tensor_copy(slots[1][:], rslot[:]).then_inc(cls_slots, 1)
                assert count[0] == CLS_ROUTE, count

            def cls_d():
                dve.wait_ge(cls_pe, 6)
                dve.tensor_tensor(run[:], list_f[:], ps_tot, ALU.add).then_inc(run_ready, 1)

            def ekv(n, lt):
                dve.wait_ge(tq_done, LT * n + lt + 1)
                dve.tensor_tensor(E[:, lt, 0:M].rearrange("p (h d) -> p h d", h=H),
                                  ps_proj[:, :, 2 * D:3 * D],
                                  E[:, lt, M:2 * M].rearrange("p (h d) -> p h d", h=H), ALU.mult
                                  ).then_inc(ekv_done, 1)

            def numerator(n, tt):
                dve.wait_ge(nd_ready, LT * n + tt + 1)
                dve.reciprocal(rden[:, tt, :], ps_nd[:, tt, M:2 * M]).then_inc(recip_done, 1)
                if tt == 0:
                    after(dve, yT_ps, n)
                dve.scalar_tensor_tensor(Y[:, tt, :], tanh_q[:, tt, :], 1.0, ps_nd[:, tt, 0:M],
                                         ALU.add, ALU.mult).then_inc(t1_done, 1)

            def shared(n, js):
                if live(n):
                    for j in js:
                        low_g(dve, n, j)

            def step(t, par):
                if live(t - 3):
                    n = t - 3
                    h1, h0 = H1[1 - par], H0[1 - par]
                    dve.wait_ge(attn_ready, n + 1)
                    dve.wait_ge(h0b_done, n + 1)
                    after(dve, sum_done, n - 1)
                    dve.tensor_tensor(h1[:], h0[:], ps_h[:], ALU.add).then_inc(h1_done, 1)
                    dve_wait(dve, h1_done, n + 1)
                    stats(2, [h1[:, lt, :] for lt in range(LT)], n)
                if live(t):
                    ekv(t, 0)
                if live(t - 3):
                    n = t - 3
                    v = V[1 - par]
                    dve.wait_ge(rstd_done[2], n + 1)
                    if live(n - 2):
                        dve.wait_ge(scattered[1 - par], 16 * LT * (n - (1 - par)))
                    for lt in range(LT):
                        norm(2, v[:, lt, 0:M], h1[:, lt, :], lt).then_inc(v_ready, 1)
                if live(t):
                    ekv(t, 1)
                if live(t - 4):
                    n = t - 4
                    dve.wait_ge(lg_ready, n + 1)
                    k = [0]

                    def chain(instruction):
                        k[0] += 1
                        routed(n, instruction, k[0])

                    dve.tensor_copy(rlg[:], ps_lg).then_inc(lg_done, 1)
                    dve.wait_ge(lg_done, n + 1)
                    choose(chain)
                    dve.tensor_tensor(rmask[:], rone[0][:], rone[1][:], ALU.add
                                      ).then_inc(mask_done, 1)
                    dve.tensor_tensor(rdif[:], rmax[1][:], rmax[0][:], ALU.subtract
                                      ).then_inc(dif_done, 1)
                if live(t - 1):
                    n = t - 1
                    dve.wait_ge(h_ready, LT * (n + 1))
                    stats(0, [ps_h[:, lt, :] for lt in range(LT)], n)
                if live(t):
                    numerator(t, 0)
                if live(t - 1):
                    n = t - 1
                    h0 = H0[1 - par]
                    dve.wait_ge(rstd_done[0], n + 1)
                    for lt in range(LT):
                        norm(0, h0[:, lt, :], ps_h[:, lt, :], lt).then_inc(hn_done, 1)
                if live(t - 3):
                    n = t - 3
                    dve.wait_ge(vh_done, n + 1)
                    dve.tensor_tensor(XL[1 - par][:], ps_t[:], XH[1 - par][:].bitcast(F32),
                                      ALU.subtract).then_inc(vl_done, 1)
                if live(t - 4):
                    n = t - 4
                    v = V[par]
                    dve.wait_ge(route_act, n + 2)
                    chain(dve.tensor_copy(v[:, :, FIRST_E], ridx[:, 0, :]))
                    gates_of(v[:, :, M:M + 3], chain)
                    dve.wait_ge(rank_ready, n + 1)
                    chain(dve.tensor_tensor(rpos[:], ps_rank, over_lt(run), ALU.add))
                    dve.tensor_tensor(run[:], run[:], ps_tot, ALU.add).then_inc(run_ready, 1)
                shared(t - 4, range(0, 1))
                if live(t):
                    numerator(t, 1)
                    dve.wait_ge(t1_done, LT * (t + 1))
                    dve.wait_ge(recip_done, LT * (t + 1))
                    dve.scalar_tensor_tensor(Y[:], Y[:], 0.5, rden[:], ALU.mult, ALU.mult
                                             ).then_inc(y_ready, 1)
                if live(t - 4):
                    v = V[par]
                    if isinstance(n, int) and n == 0:
                        dve.wait_ge(lines, 4)
                    chain(dve.tensor_scalar(v[:, :, OUT_ROW], v[:, :, OUT_ROW], float(2 * SEQ), None,
                                            ALU.add))
                    for k2 in range(2):
                        dve.tensor_tensor(rsel[k2][:], rone[k2][:], rpos[:], ALU.mult
                                          ).then_inc(sel_done, 1)
                    dve.wait_ge(sel_done, 2 * (n + 1))
                    for k2 in range(2):
                        last = dve.tensor_reduce(rslot[:, k2, :], rsel[k2][:], AX.X, ALU.add)
                    chain(last)
                    assert k[0] == ROUTE, k
                    if isinstance(n, int) and n == 1:
                        dve.wait_ge(cls_scattered, 32)
                    dve.tensor_copy(slots[par][:], rslot[:]).then_inc(slots_ready, 1)
                if live(t - 1):
                    n = t - 1
                    dve_wait(dve, h0_done, n + 1)
                    stats(1, [H0[1 - par][:, lt, :] for lt in range(LT)], n)
                shared(t - 4, range(1, 3))
                if live(t - 1):
                    n = t - 1
                    dve.wait_ge(rstd_done[1], n + 1)
                    after(dve, uT_ps, n)
                    for lt in range(LT):
                        norm(1, U[:, lt, :], H0[1 - par][:, lt, :], lt).then_inc(u_ready, 1)
                shared(t - 4, range(3, 4))
                if live(t - 2):
                    n = t - 2
                    dve.wait_ge(tanh_done, FT * (n + 1))
                    for e in range(FT):
                        dve.tensor_scalar(A[:, e, :], TR[:, e, :], 1.0, a_half[:, e:e + 1],
                                          ALU.add, ALU.mult).then_inc(a_done, 1)
                shared(t - 4, range(4, 5))
                if live(t - 2):
                    dve.wait_ge(a_done, FT * (n + 1))
                    dve.tensor_scalar(S[:], A[:], -0.5, 0.5, ALU.mult, ALU.add).then_inc(om_done, 1)
                    dve.wait_ge(om_done, n + 1)
                    dve.scalar_tensor_tensor(S[:], TI[:], 1.0, S[:], ALU.add, ALU.mult
                                             ).then_inc(s_done, 1)
                shared(t - 4, range(5, 6))
                if live(t - 2):
                    n = t - 2
                    dve.wait_ge(s_done, n + 1)
                    dve.wait_ge(ip_ready, FT * (n + 1))
                    for e in range(FT):
                        dve.scalar_tensor_tensor(S[:, e, :], ps_ip[:, e, :], col_raw[:, 3, e:e + 1],
                                                 S[:, e, :], ALU.add, ALU.mult
                                                 ).then_inc(b_done, 1)
                shared(t - 4, range(6, 7))
                if live(t - 2):
                    n = t - 2
                    dve.wait_ge(b_done, FT * (n + 1))
                    after(dve, attn_ready, n)
                    for e in range(FT):
                        dve.tensor_tensor_scan(HS[:, e, :], A[:, e, :], S[:, e, :], c_h[:, e:e + 1],
                                               ALU.mult, ALU.add).then_inc(scan_done, 1)
                shared(t - 4, range(7, 8))
                if live(t - 1):
                    n = t - 1
                    dve.wait_ge(uh_done, n + 1)
                    dve.tensor_tensor(UTL[:], ps_t[:], UTH[:].bitcast(F32), ALU.subtract
                                      ).then_inc(ul_done, 1)
                if live(t - 4):
                    n = t - 4
                    for a in range(2):
                        dve.wait_ge(y_ps, 2 * n + a + 1)
                        if a == 0:
                            after(dve, base_stored, 16 * n)
                        dve.tensor_tensor(yb[:, a, :], y_loop[a], pjb[0][:], ALU.add
                                          ).then_inc(y_done, 1)
                    dve.wait_ge(y_done, 2 * (n + 1))
                    dve.tensor_tensor(yb[:], yb[:], H1[par][:], ALU.add).then_inc(sum_done, 1)
                if isinstance(t, int) and t == 0:
                    cls_a()
                if isinstance(t, int) and t == 1:
                    cls_b()
                if isinstance(t, int) and t == 2:
                    cls_c()
                if isinstance(t, int) and t == 3:
                    cls_d()
                    dve.wait_ge(biases_loaded[0], 32)

            return step

        def experts_vector(dve):
            count = [0]

            def chain(instruction):
                count[0] += 1
                instruction.then_inc(count_dve, 1)
                dve.wait_ge(count_dve, count[0])

            dve.wait_ge(run_ready, NIMG + 1)
            dve.tensor_copy(ends_i[:], run[:]).then_inc(ends_ready, 1)
            chain(dve.tensor_tensor(cnt["size"][:], run[:], list_f[:], ALU.subtract))
            chain(dve.tensor_scalar(cnt_i[:], cnt["size"][:], float(BLK - 1), None, ALU.add))
            chain(dve.tensor_scalar(cnt_s[:], cnt_i[:], BLK.bit_length() - 1, None,
                                    ALU.arith_shift_right))
            chain(dve.tensor_copy(cnt["n"][:], cnt_s[:]))
            chain(dve.tensor_scalar(cnt["blocks"][:], cnt["n"][:], float(MIN_BLKS), None, ALU.max))
            chain(dve.tensor_tensor_scan(cnt["end"][:], ones_pp[:, 0:NE], cnt["blocks"][:],
                                         0.0, ALU.mult, ALU.add))
            dve.memset(bounds[:, 0:1], 0)
            dve.tensor_copy(bounds[:, 1:NE + 1], cnt["end"][:]).then_inc(bounds_ready, 1)
            dve.tensor_scalar(cnt["skip"][:], cnt["blocks"][:], -1.0, float(LIST_BLKS),
                              ALU.mult, ALU.add)
            dve.tensor_copy(hop[:, NE - 1, :], block_f[:])
            chain(dve.memset(carrier["count"][:], 0.0))
            for e in range(NE - 1):
                last = dve.tensor_scalar(hop[:, e, :], block_f[:], cnt["end"][:, e:e + 1],
                                         cnt["skip"][:, e:e + 1], ALU.is_ge, ALU.mult)
            chain(last)
            chain(dve.tensor_reduce(where[:], hop[:].rearrange("p e b -> p b e"), AX.X, ALU.add))
            dve.tensor_copy(where_i[:], where[:]).then_inc(where_ready, 1)

            b = NIMG
            for j in range(HT):
                dve.wait_ge(gelu_done, b * HT + (j + 1))
                dve.tensor_copy(GH[:, j, 0:2], g_act[:, j % G_SLOTS, 0:2]).then_inc(gh_done, 1)
                low_g(dve, b, j, 2)
            dve.wait_ge(y_ps, 2 * b + 2)
            for a in range(2):
                cols = slice(a * P, (a + 1) * P)
                dve.tensor_tensor(c_y[:, cols], y_loop[0][0:1, cols], pjb[0][0:1, cols], ALU.add
                                  ).then_inc(y_done, 1)
            dve.wait_ge(y_done, 2 * b + 2)
            dve.tensor_tensor(c_y[:], c_y[:], c_h1[:], ALU.add).then_inc(cls_base, 1)
            dve.memset(carrier["end"][:], 0.0).then_inc(expert_done, 1)
            dve.wait_ge(base_stored, 16 * NIMG)

            def next_x(b):
                dve.wait_ge(rows_loaded, b * 16 + 16)
                dve.tensor_copy(info[:], R[:, :, M:W]).then_inc(info_read, 1)
                dve.wait_ge(xh_ready, b + 1)
                dve.tensor_tensor(XL[0][:], ps_t[:], XH[0][:].bitcast(F32), ALU.subtract
                                  ).then_inc(xl_ready, 1)

            def start(g, i, nth):
                dve_wait(dve, biases_loaded[i], nth * 32 + 32)
                dve_wait(dve, expert_done, g, "end")

            def block(b, i, g):
                for j in range(HT):
                    dve.wait_ge(gelu_done, (b + SBLK) * HT + (j + 1))
                    dve.tensor_copy(GH[:, j, :], g_act[:, j % G_SLOTS, :]).then_inc(gh_done, 1)
                    if j:
                        low_g(dve, b + SBLK, j - 1)
                low_g(dve, b + SBLK, HT - 1)
                if True:
                    dve.wait_ge(info_read, b + 1)
                    dve.tensor_scalar(info_t[:], info[:, :, 0], number[i][:], None, ALU.is_equal
                                      ).then_inc(info_done, 1)
                    dve.wait_ge(added, b * 32 + 32)
                    dve.tensor_copy(rows_to[:], info[:, :, 3])
                    dve.wait_ge(info_done, b * 3 + 1)
                    dve.tensor_tensor(info_t[:], info_t[:], info[:, :, 1], ALU.mult
                                      ).then_inc(info_done, 1)
                    dve.wait_ge(info_done, b * 3 + 2)
                    dve.tensor_tensor(gate[:], info_t[:], info[:, :, 2], ALU.add
                                      ).then_inc(info_done, 1)
                dve.wait_ge(info_done, b * 3 + 3)
                next_x(b + 1)
                for a in range(2):
                    dve.wait_ge(y_ps, b * 2 + (2 * SBLK + a + 1))
                    dve.tensor_tensor(yt[:, a, :], y_loop[a], pjb[i][:], ALU.add
                                      ).then_inc(yt_done, 1)
                dve.wait_ge(yt_done, b * 2 + 2)
                for a in range(2):
                    dve.tensor_scalar(yb[:, a, :], yt[:, a, :], gate[:, a:a + 1], None, ALU.mult
                                      ).then_inc(y_done, 1)

            def finish(g, i):
                dve.tensor_scalar(number[i][:], number[i][:], 2.0, None, ALU.add
                                  ).then_inc(expert_done, 1)

            next_x(0)
            experts(dve, block, start, finish)

        block = ctx.enter_context(nc.Block())

        @block.sync
        def _(sp):
            steps(mixer_sync(sp))(sp)
            experts_sync(sp)

        @block.gpsimd
        def _(pool):
            steps(mixer_pool(pool))(pool)
            experts_pool(pool)

        @block.scalar
        def _(act):
            steps(mixer_scalar(act))(act)
            experts_scalar(act)

        @block.vector
        def _(dve):
            steps(mixer_vector(dve))(dve)
            experts_vector(dve)

        @block.tensor
        def _(pe):
            steps(mixer_tensor(pe))(pe)
            experts_tensor(pe)




def kernel(**inputs):
    import numpy as np
    import concourse.bacc as bacc
    from concourse import mybir as my
    from concourse.bass_utils import run_bass_kernel_spmd as run

    g = {k: np.asarray(v) for k, v in inputs.items()}
    x = g["x"]
    nimg, c, length, heads = x.shape
    d = g["L0_tok_Wq_w"].shape[0]
    m = heads * d
    w_proj = np.concatenate([np.concatenate([g[f"L0_tok_W{i}_w"].T, g[f"L0_tok_W{i}_b"][None]], 0)
                             for i in "qkv"], 1)
    w_resid = np.concatenate([np.broadcast_to(np.eye(c, dtype=x.dtype)[:, None, :], (c, heads, d)),
                              g["L0_tok_out_b"].reshape(1, heads, d)], 0)
    arrays = {
        "x": x.reshape(nimg, c, length * heads),
        "cls_tok": g["cls_tok"].reshape(1, m),
        "w_proj": w_proj, "w_resid": w_resid,
        "bias_t": g["L0_tok_w_bias"].T,
        "mask_t": np.ascontiguousarray(g["L0_tok_local_mask"].T).view(np.int32),
        "out_w": g["L0_tok_out_w"], "ln_g": g["L0_tok_ln_g"], "ln_b": g["L0_tok_ln_b"],
        "w_in": g["L0_attn_W_in"], "w_r": g["L0_attn_W_r"], "w_i": g["L0_attn_W_i"],
        "w_out": g["L0_attn_W_out"], "b_in": g["L0_attn_b_in"], "b_r": g["L0_attn_b_r"],
        "b_i": g["L0_attn_b_i"], "b_out": g["L0_attn_b_out"], "log_a": g["L0_attn_log_a"],
        "w_route": g["L0_ffn_Wr"],
        "fc_w": np.concatenate([g["L0_ffn_Wfc_s"][None], g["L0_ffn_Wfc"]], 0),
        "fc_b": np.concatenate([g["L0_ffn_bfc_s"][None], g["L0_ffn_bfc"]], 0)
        .reshape(-1, g["L0_ffn_bfc"].shape[1] // 128, 128).transpose(0, 2, 1),
        "pj_w": np.concatenate([g["L0_ffn_Wproj_s"][None], g["L0_ffn_Wproj"]], 0),
        "pj_b": np.concatenate([g["L0_ffn_bproj_s"][None], g["L0_ffn_bproj"]], 0)[:, None, :],
    }
    nc = bacc.Bacc("TRN2", target_bir_lowering=False, num_devices=1)
    args = []
    for name, a in list(arrays.items()):
        arrays[name] = a = np.ascontiguousarray(a)
        args.append(nc.dram_tensor(name, a.shape, my.dt.from_np(a.dtype), kind="ExternalInput").ap())
    rows = nimg * (length + 1)
    out = nc.dram_tensor("out", (rows + 1 + 256, m), my.dt.float32, kind="ExternalOutput").ap()
    vit_tower(nc, *args, out)
    r = run(nc, [arrays], core_ids=[0])
    return np.asarray(r.results[0]["out"])[:rows].reshape(nimg, length + 1, m)
```

```python
import concourse.bass as bass
from concourse import mybir
from contextlib import ExitStack


def vit_tower(nc, x, cls_tok, w_proj, bias_t, mask_t, out_w, ln_g, ln_b, w_in, w_r, w_i,
              w_out, b_in, b_r, b_i, b_out, log_a, w_route, fc_w, fc_b, pj_w, pj_b, out):
    F32, F32R, I32, U32, U8 = (mybir.dt.float32, mybir.dt.float32r, mybir.dt.int32,
                               mybir.dt.uint32, mybir.dt.uint8)
    ALU, ACT, AX = mybir.AluOpType, mybir.ActivationFunctionType, mybir.AxisListType
    P = 128
    NIMG, C, LH = x.shape
    H = w_proj.shape[1]
    L = LH // H
    D = C
    M = H * D
    LT, FT = L // P, M // P
    KA = C + 1
    NE = w_route.shape[1]
    HID = fc_w.shape[2]
    HT = HID // P
    BLK = L
    TOK = NIMG * L + 1
    SEQ = L + 1
    CLS_ROW = NIMG * SEQ
    TAIL_ROW = CLS_ROW + 1
    LIST_BLKS = (TOK + BLK - 1) // BLK + 1
    LIST = LIST_BLKS * BLK
    DUMP = NE * LIST
    SBLK = NIMG + 1
    MIN_BLKS = 2
    MAX_BLK = 2 * TOK // BLK + MIN_BLKS * NE
    FIRST_E, GATE_DIFF, GATE2, OUT_ROW = M, M + 1, M + 2, M + 3
    W = M + 4
    EPS = 1e-5
    BIG = 3e38

    v_rows = nc.dram_tensor("v_rows", (DUMP + 2 * P, W), F32, kind="Internal").ap()

    ctx = ExitStack()
    with ctx:
        memory = ctx

        def sb(name, shape, dt=F32):
            return memory.enter_context(nc.sbuf_tensor(name, shape, dt))

        def sem(name):
            return ctx.enter_context(nc.semaphore(name))

        def ps(name, shape):
            return ctx.enter_context(nc.psum_tensor(name, shape, F32))

        ident = sb("ident", [P, P])
        ones_pp = sb("ones_pp", [P, P])
        before = sb("before", [P, P])
        minus_half = sb("minus_half", [P, 2])
        eps = sb("eps", [P, 2])
        carrier = {k: sb(f"carrier_{k}", [1, 1]) for k in
                   ("dve", "end", "count", "pool", "start", "y", "set", "stage")}
        iota_i = sb("iota_i", [P, NE], I32)
        iota_m = sb("iota_m", [P, NE])
        list_i = sb("list_i", [P, NE], I32)
        list_f = sb("list_f", [P, NE])
        lines_i = sb("lines_i", [P, 3, 2], I32)
        lines_f = sb("lines_f", [P, 3, 2])
        block_i = sb("block_i", [P, MAX_BLK + 1], I32)
        block_f = sb("block_f", [P, MAX_BLK + 1])
        tail_rows = sb("tail_rows", [P, 2, W])
        zeros = sb("zeros", [P, 2, M])
        stage1 = sb("stage1", [P, FT, HID])
        stage2 = sb("stage2", [P, HT, M])
        W1H = [sb(f"w1h{i}", [P, FT, HID], F32R) for i in range(2)]
        W1L = [sb(f"w1l{i}", [P, FT, HID], F32R) for i in range(2)]
        W2H = [sb(f"w2h{i}", [P, HT, M], F32R) for i in range(2)]
        W2L = [sb(f"w2l{i}", [P, HT, M], F32R) for i in range(2)]
        fcb = [sb(f"fcb{i}", [P, HT]) for i in range(2)]
        pjb = [sb(f"pjb{i}", [P, M]) for i in range(2)]
        number = [sb(f"number{i}", [P, 1]) for i in range(2)]
        G_SLOTS = 4
        g_act = sb("g_act", [P, G_SLOTS, BLK])
        GH = sb("GH", [P, HT, BLK], F32R)
        GL = sb("GL", [P, HT, BLK], F32R)
        XH = [sb(f"xh{i}", [P, FT, BLK], F32R) for i in range(2)]
        XL = [sb(f"xl{i}", [P, FT, BLK], F32R) for i in range(2)]
        yb = sb("yb", [P, 2, M])
        run = sb("run", [P, NE])
        rlg = sb("rlg", [P, LT, NE])
        rlg2 = sb("rlg2", [P, LT, NE])
        rhit = sb("rhit", [P, LT, NE])
        rcand = sb("rcand", [P, LT, NE])
        ridx = sb("ridx", [P, 2, LT])
        rone = [sb(f"rone{i}", [P, LT, NE]) for i in range(2)]
        rmax = [sb(f"rmax{i}", [P, LT]) for i in range(2)]
        rmask = sb("rmask", [P, LT, NE], F32R)
        ones_r = sb("ones_r", [P, P], F32R)
        before_r = sb("before_r", [P, P], F32R)
        rdif = sb("rdif", [P, LT])
        rtanh = sb("rtanh", [P, LT])
        rpos = sb("rpos", [P, LT, NE])
        rsel = [sb(f"rsel{i}", [P, LT, NE]) for i in range(2)]
        rslot = sb("rslot", [P, 2, LT])
        slots = [sb(f"slots{i}", [P, 2, LT], U32) for i in range(2)]
        cnt_i = sb("cnt_i", [P, NE], I32)
        cnt_s = sb("cnt_s", [P, NE], I32)
        ends_i = sb("ends_i", [P, NE], I32)
        cnt = {k: sb(f"c_{k}", [P, NE]) for k in ("size", "n", "blocks", "end", "start", "skip")}
        bounds = sb("bounds", [P, NE + 1], I32)
        where = sb("where", [P, MAX_BLK + 1])
        hop = sb("hop", [P, NE, MAX_BLK + 1])
        where_i = sb("where_i", [P, MAX_BLK + 1], I32)
        CXH = sb("CXH", [P, FT, 2], F32R)
        CXL = sb("CXL", [P, FT, 2], F32R)
        c_h1 = sb("c_h1", [1, M])
        c_y = sb("c_y", [1, M])
        mixer_memory = ExitStack()
        memory = mixer_memory
        wproj = sb("wproj", [KA, H, 4 * D])
        ewT = sb("ewT", [P, LT, L])
        mask_sb = sb("mask_sb", [P, LT, L // 4], I32)
        outw_sb = sb("outw_sb", [P, FT, M])
        gates_h = [sb(f"gates_h{i}", [P, FT, M], F32R) for i in range(3)]
        gates_l = [sb(f"gates_l{i}", [P, FT, M], F32R) for i in range(3)]
        wout_sb = sb("wout_sb", [P, FT, M])
        route_sb = sb("route_sb", [P, FT, NE])
        route_hl = sb("route_hl", [P, FT, 2 * NE], F32R)
        lng_bc = sb("lng_bc", [P, M])
        lnb_bc = sb("lnb_bc", [P, M])
        bout_bc = sb("bout_bc", [P, M])
        col_raw = sb("col_raw", [P, 4, FT])
        bhalf = sb("bhalf", [P, 2, FT])
        a_clip = sb("a_clip", [P, 2, FT])
        a_exp = sb("a_exp", [P, 2, FT])
        a_rec = sb("a_rec", [P, FT])
        a_den = sb("a_den", [P, FT])
        a_half = sb("a_half", [P, FT])
        X = [sb(f"x{i}", [KA, LH]) for i in range(2)]
        E = sb("E", [P, LT, 2 * M])
        tanh_q = sb("tanh_q", [P, LT, M])
        XR = [sb(f"xr{i}", [P, LT, M]) for i in range(2)]
        rden = sb("rden", [P, LT, M])
        Y = sb("Y", [P, LT, M])
        YT = sb("YT", [P, FT, L])
        H0 = [sb(f"h0_{i}", [P, LT, M]) for i in range(2)]
        H1 = [sb(f"h1_{i}", [P, LT, M]) for i in range(2)]
        U = sb("U", [P, LT, M])
        V = [sb(f"v{i}", [P, LT, W]) for i in range(2)]
        UTH = sb("UTH", [P, FT, L], F32R)
        UTL = sb("UTL", [P, FT, L], F32R)
        TR = sb("TR", [P, FT, L])
        TI = sb("TI", [P, FT, L])
        A = sb("A", [P, FT, L])
        S = sb("S", [P, FT, L])
        HS = sb("HS", [P, FT, L])
        st = [sb(f"st{i}", [P, LT, 6]) for i in range(3)]
        mv = [sb(f"mv{i}", [P, LT, 2]) for i in range(3)]
        ve = [sb(f"ve{i}", [P, LT]) for i in range(3)]
        rstd = [sb(f"rstd{i}", [P, LT]) for i in range(3)]
        gates_raw = [b[:].rearrange("p a m -> p (a m)").rearrange("p (a m) -> p a m", a=FT)
                     for b in (TR, TI, A)]
        mask_f = S
        c_row = sb("c_row", [1, M])
        c_u = sb("c_u", [1, M])
        c_st = [sb(f"c_st{i}", [1, 6]) for i in range(2)]
        c_mv = [sb(f"c_mv{i}", [1, 2]) for i in range(2)]
        c_ve = [sb(f"c_ve{i}", [1, 2]) for i in range(2)]
        c_rs = [sb(f"c_rs{i}", [1, 2]) for i in range(2)]
        c_uh = sb("c_uh", [P, FT, 2], F32R)
        c_ul = sb("c_ul", [P, FT, 2], F32R)
        c_g = sb("c_g", [P, 2, FT])
        c_a = sb("c_a", [P, FT])
        c_om = sb("c_om", [P, FT])
        c_s = sb("c_s", [P, FT])
        c_h = sb("c_h", [P, FT])
        CV = sb("CV", [P, W])
        mixer_memory.close()
        expert_memory = ExitStack()
        memory = expert_memory
        R = sb("R", [P, 2, W])
        info = sb("info", [P, 2, 4])
        info_t = sb("info_t", [P, 2])
        gate = sb("gate", [P, 2])
        rows_to = sb("rows_to", [P, 2], U32)
        yt = sb("yt", [P, 2, M])
        expert_memory.close()
        memory = ctx
        ps_proj = ps("ps_proj", [P, H, 256])
        ps_nd = ps("ps_nd", [P, 2, 2 * M])
        ps_t = ps("ps_t", [P, FT, L])
        ps_h = ps("ps_h", [P, LT, M])
        ps_ri = ps("ps_ri", [P, 2, L])
        ps_ip = ps("ps_ip", [P, FT, L])
        ps_lg = ps_ri[:, 0, 0:2 * LT * NE].rearrange("p (t e) -> p t e", e=2 * NE)
        ps_rank = ps_ri[:, 0, 64:64 + LT * NE].rearrange("p (t e) -> p t e", e=NE)
        ps_tot = ps_ri[:, 0, 128:128 + NE]
        fc_loop = [ps_proj[:, 0, :], ps_proj[:, 2, :]]
        y_loop = [ps_nd[:, 0, 0:M], ps_nd[:, 1, 0:M]]
        fc_after = fc_loop + [ps_ri[:, 0, :], ps_ip[:, 0, :]]

        w_loaded, cls_loaded = sem("w_loaded"), sem("cls_loaded")
        proj_loaded, prep_loaded = sem("proj_loaded"), sem("prep_loaded")
        x_loaded = [sem(f"x_loaded{i}") for i in range(2)]
        gate_w_loaded, gate_w_split = sem("gate_w_loaded"), sem("gate_w_split")
        consts, prep, prep_act = sem("consts"), sem("prep"), sem("prep_act")
        ones_in_x, base_stored = sem("ones_in_x"), sem("base_stored")
        proj_ready, exp_done, tq_done = sem("proj_ready"), sem("exp_done"), sem("tq_done")
        ekv_done, nd_ready, t1_done = sem("ekv_done"), sem("nd_ready"), sem("t1_done")
        recip_done, y_ready = sem("recip_done"), sem("y_ready")
        yT_ps, yT_sb, h_ready = sem("yT_ps"), sem("yT_sb"), sem("h_ready")
        raw = [sem(f"stats{i}") for i in range(3)]
        mv_done = [sem(f"mv_done{i}") for i in range(3)]
        ve_done = [sem(f"ve_done{i}") for i in range(3)]
        rstd_done = [sem(f"rstd_done{i}") for i in range(3)]
        hn_done, hg_done, h0_done, h0b_done = (sem("hn_done"), sem("hg_done"), sem("h0_done"),
                                               sem("h0b_done"))
        u_ready, uT_ps, uh_done, ul_done = sem("u_ready"), sem("uT_ps"), sem("uh_done"), sem("ul_done")
        ri_ready, ip_ready, tanh_done = sem("ri_ready"), sem("ip_ready"), sem("tanh_done")
        a_done, om_done, s_done = sem("a_done"), sem("om_done"), sem("s_done")
        b_done, scan_done, attn_ready = sem("b_done"), sem("scan_done"), sem("attn_ready")
        h1_done, v_ready, vT_ps = sem("h1_done"), sem("v_ready"), sem("vT_ps")
        vh_done, vl_done = sem("vh_done"), sem("vl_done")
        lg_ready, route_dve, route_act, rank_ready = (sem("lg_ready"), sem("route_dve"),
                                                      sem("route_act"), sem("rank_ready"))
        slots_ready = sem("slots_ready")
        scattered = [sem(f"scattered{i}") for i in range(2)]
        cls_scattered, cls_slots = sem("cls_scattered"), sem("cls_slots")
        cls_pe, cls_act, cls_dve, cls_pool = (sem("cls_pe"), sem("cls_act"), sem("cls_dve"),
                                              sem("cls_pool"))
        staged, high_loaded, w_split = sem("staged"), sem("high_loaded"), sem("w_split")
        biases_loaded = [sem(f"biases_loaded{i}") for i in range(2)]
        expert_done = sem("expert_done")
        bounds_ready, ends_ready, where_ready = sem("bounds_ready"), sem("ends_ready"), sem("where_ready")
        count_dve, tails_stored = sem("count_dve"), sem("tails_stored")
        rows_loaded, info_read, pt_ready, xh_ready, xl_ready = (
            sem("rows_loaded"), sem("info_read"), sem("pt_ready"), sem("xh_ready"), sem("xl_ready"))
        fc_ready, gelu_done, gh_done, gl_done = (sem("fc_ready"), sem("gelu_done"), sem("gh_done"),
                                                 sem("gl_done"))
        y_ps, y_done, yt_done, sum_done = sem("y_ps"), sem("y_done"), sem("yt_done"), sem("sum_done")
        info_done, added = sem("info_done"), sem("added")
        cls_base, cls_stored, cls_out = sem("cls_base"), sem("cls_stored"), sem("cls_out")
        lnb_loaded, lines, route_w = sem("lnb_loaded"), sem("lines"), sem("route_w")
        lg_copied, lg_done, mask_done, dif_done = (sem("lg_copied"), sem("lg_done"),
                                                   sem("mask_done"), sem("dif_done"))
        seconds_stored = sem("seconds_stored")
        run_ready, sel_done = sem("run_ready"), sem("sel_done")
        carried, hx_done = sem("carried"), sem("hx_done")
        cls_row1, cls_s = sem("cls_row1"), sem("cls_s")

        DEPTH = 5
        PEEL = DEPTH + DEPTH % 2

        def steps(step):
            def over(eng):
                for t in range(PEEL):
                    step(t, t % 2)
                with eng.Fori(PEEL // 2, NIMG // 2) as pair:
                    step(pair * 2, 0)
                    step(pair * 2 + 1, 1)
                for t in range(NIMG, NIMG + DEPTH - 1):
                    step(t, t % 2)
            return over

        def live(n):
            return not isinstance(n, int) or 0 <= n < NIMG

        def after(eng, semaphore, value):
            if not isinstance(value, int) or value > 0:
                eng.wait_ge(semaphore, value)

        def at_most(value, limit):
            return min(value, limit) if isinstance(value, int) else value

        CONSTS = 14
        CLS_MASK, CLS_ROUTE, ROUTE = 16, 28, 16

        def dve_wait(dve, semaphore, value, use="dve"):
            dve.wait_ge(semaphore, value)
            if not isinstance(value, int):
                dve.memset(carrier[use][:], 0.0)

        def pool_wait(pool, semaphore, value, use="pool"):
            pool.wait_ge(semaphore, value)
            if not isinstance(value, int):
                half = minus_half[0:1, 0:1]
                return pool.tensor_tensor(carrier[use][:], half, half, ALU.add)

        def flat(buf):
            return buf[:].rearrange("p a b -> p (a b)")

        def over_lt(a):
            return a[:].unsqueeze(1).to_broadcast([P, LT, a.shape[1]])

        def over_e(a):
            return a.unsqueeze(2).to_broadcast([P, LT, NE])

        W_LOADS = 5
        GATE_W = (w_r, w_i, w_in)
        halves = ((0, 0), (1, 0), (0, 1))

        def store_base(sp, n):
            sp.wait_ge(sum_done, n + 1)
            dst = out[bass.ds(n * SEQ + 1, L), :].rearrange("(a p) m -> p a m", p=P)
            sp.dma_start(dst, yb[:]).then_inc(base_stored, 16)

        def mixer_sync(sp):
            def load_x(n, par):
                after(sp, proj_ready, LT * (n - 1))
                sp.dma_start(X[par][0:C, :], x[n]).then_inc(x_loaded[par], 16)

            rows = "(t p) m -> p t m"
            sp.dma_start(c_row[:], cls_tok).then_inc(cls_loaded, 16)
            sp.dma_start(wproj[:], w_proj).then_inc(proj_loaded, 16)
            load_x(0, 0)
            with nc.allow_non_contiguous_dma(reason="256 values as columns"):
                for i, src in enumerate((b_r, b_i, log_a, b_in)):
                    sp.dma_start(col_raw[:, i], src.rearrange("(t p) -> p t", p=P)
                                 ).then_inc(prep_loaded, 16)
            for dst, src in ((mask_sb, mask_t), (ewT, bias_t)):
                sp.dma_start(dst[:], src.rearrange(rows, p=P)).then_inc(prep_loaded, 16)
            for dst, src in zip(gates_raw, GATE_W):
                sp.dma_start(dst, src.rearrange(rows, p=P)).then_inc(gate_w_loaded, 16)
            load_x(1, 1)
            for dst, src in ((wout_sb, w_out), (outw_sb, out_w)):
                sp.dma_start(dst[:], src.rearrange(rows, p=P)).then_inc(w_loaded, 16)
            sp.dma_start(route_sb[:], w_route.rearrange(rows, p=P)).then_inc(w_loaded, 16)
            for dst, src in ((lng_bc, ln_g), (bout_bc, b_out)):
                sp.dma_start(dst[:], src.rearrange("(a m) -> a m", a=1).to_broadcast([P, M])
                             ).then_inc(w_loaded, 16)
            sp.dma_start(lnb_bc[:], ln_b.rearrange("(a m) -> a m", a=1).to_broadcast([P, M])
                         ).then_inc(lnb_loaded, 16)
            sp.wait_ge(lines, 2)
            for e in range(NE):
                sp.dma_start(v_rows[e * LIST + BLK:e * LIST + 2 * BLK, :]
                             .rearrange("(p a) m -> p a m", a=2), tail_rows[:]
                             ).then_inc(seconds_stored, 16)

            def step(t, par):
                if live(t) and not (isinstance(t, int) and t < 2):
                    load_x(t, par)
                if live(t - 5):
                    store_base(sp, t - 5)

            return step

        def experts_sync(sp):
            def rows(b):
                return v_rows[bass.ds(b * BLK, BLK), :].rearrange("(p a) m -> p a m", a=2)

            def load_rows(b, source):
                after(sp, pt_ready, b)
                after(sp, info_read, b)
                sp.dma_start(R[:], rows(source)).then_inc(rows_loaded, 16)

            sp.wait_ge(ends_ready, 1)
            for e in range(NE):
                end = sp.value_load(ends_i[0:1, e:e + 1], min_val=e * LIST, max_val=e * LIST + TOK)
                sp.dma_start(v_rows[bass.ds(end, BLK), :].rearrange("(p a) m -> p a m", a=2),
                             tail_rows[:]).then_inc(tails_stored, 16)
            sp.wait_ge(tails_stored, 16 * NE)
            sp.wait_ge(cls_scattered, 32)
            for i in range(2):
                sp.wait_ge(scattered[i], 16 * 2 * LT * (NIMG // 2))
            load_rows(0, 0)
            store_base(sp, NIMG - 1)
            sp.wait_ge(cls_base, 1)
            sp.dma_start(out[CLS_ROW:CLS_ROW + 1, :], c_y[:]).then_inc(cls_stored, 16)
            sp.wait_ge(where_ready, 1)
            end = sp.value_load(bounds[0:1, NE:NE + 1], min_val=MIN_BLKS * NE,
                                max_val=MAX_BLK)
            with sp.Fori(1, end) as b:
                source = sp.value_load(where_i[0:1, bass.ds(b, 1)], min_val=0,
                                       max_val=NE * LIST_BLKS - 1)
                load_rows(b, source)
            sp.wait_ge(pt_ready, end)
            sp.wait_ge(info_read, end)
            sp.dma_start(R[:], rows(0)).then_inc(rows_loaded, 16)
            sp.wait_ge(added, end * 32 + 32)
            sp.wait_ge(rows_loaded, end * 16 + 16)
            sp.dma_start(c_y[:], out[CLS_ROW:CLS_ROW + 1, :]).then_inc(cls_out, 16)
            sp.wait_ge(cls_out, 16)
            first_rows = out[0:NIMG * SEQ, :].rearrange("(n s) m -> n s m", s=SEQ)[:, 0, :]
            sp.dma_start(first_rows.rearrange("(a n) m -> a n m", a=1),
                         c_y[:].unsqueeze(1).to_broadcast([1, NIMG, M])).then_inc(cls_out, 16)
            sp.wait_ge(cls_out, 32)
            sp.wait_ge(base_stored, 16 * NIMG)

        def expert_of(w, g):
            if isinstance(g, int):
                return w[g]
            return w[bass.ds(g, 1)].rearrange("a c n -> (a c) n")

        def fc_of(g):
            return expert_of(fc_w, g).rearrange("(k p) n -> p k n", p=P)

        def pj_of(g):
            return expert_of(pj_w, g).rearrange("(j p) m -> p j m", p=P)

        def load_stage(pool, g):
            if not isinstance(g, int) or g > 0:
                pool_wait(pool, w_split, g, "stage")
            pool.dma_start(stage1[:], fc_of(g)).then_inc(staged, 16)
            pool.dma_start(stage2[:], pj_of(g)).then_inc(staged, 16)

        def load_high(pool, g, i):
            if not isinstance(g, int) or g > 1:
                pool_wait(pool, expert_done, g - 1, "set")
            pool.dma_start(W1H[i][:], fc_of(g)).then_inc(high_loaded, 16)
            pool.dma_start(W2H[i][:], pj_of(g)).then_inc(high_loaded, 16)
            pool.dma_start(fcb[i][:], expert_of(fc_b, g)).then_inc(biases_loaded[i], 16)
            pool.dma_start(pjb[i][:], expert_of(pj_b, g).to_broadcast([P, M])
                           ).then_inc(biases_loaded[i], 16)

        PARTS = 4

        def split_low(pool, g, i, part=None):
            if part in (None, 0):
                pool.wait_ge(staged, g * 32 + 32)
                pool.wait_ge(high_loaded, g * 32 + 32)
            for q in range(PARTS) if part is None else (part,):
                stage, high, low = ((stage1, W1H, W1L), (stage2, W2H, W2L))[q * 2 // PARTS]
                n = 2 * FT * HID // PARTS
                cols = slice((q % (PARTS // 2)) * n, (q % (PARTS // 2) + 1) * n)
                last = pool.tensor_tensor(flat(low[i])[:, cols], flat(stage)[:, cols],
                                          flat(high[i])[:, cols].bitcast(F32), ALU.subtract)
            if part in (None, PARTS - 1):
                last.then_inc(w_split, 1)

        def inv_std(pool, i, n):
            pool.wait_ge(mv_done[i], LT * (n + 1))
            pool.tensor_tensor(ve[i][:], mv[i][:, :, 1], eps[:], ALU.add).then_inc(ve_done[i], 1)
            pool.wait_ge(ve_done[i], n + 1)
            after(pool, [hn_done, u_ready, v_ready][i], LT * n)
            pool.tensor_tensor(rstd[i][:], ve[i][:], minus_half[:], ALU.pow
                               ).then_inc(rstd_done[i], 1)

        def scatter(pool, source, where_to, semaphore):
            pool.indirect_dma_start(out=v_rows, out_offset=bass.IndirectOffsetOnAxis(
                ap=where_to, axis=0), in_=source, in_offset=None).then_inc(semaphore, 16)

        def mixer_pool(pool):
            pool.memset(minus_half[:], -0.5).then_inc(consts, 1)
            pool.memset(eps[:], EPS).then_inc(consts, 1)
            pool.memset(ones_pp[:], 1.0).then_inc(consts, 1)
            pool.memset(ident[:], 0.0).then_inc(consts, 1)
            pool.memset(zeros[:], 0.0).then_inc(consts, 1)
            pool.memset(tail_rows[:], 0.0).then_inc(consts, 1)
            pool.memset(CV[:], 0.0).then_inc(consts, 1)
            pool.wait_ge(consts, 7)
            pool.affine_select(out=ident[:], in_=ident[:], compare_op=ALU.not_equal, fill=1.0,
                               base=0, pattern=[[-1, P]], channel_multiplier=1).then_inc(consts, 1)
            pool.affine_select(out=before[:], in_=ones_pp[:], compare_op=ALU.is_gt, fill=0.0,
                               base=0, pattern=[[1, P]], channel_multiplier=-1).then_inc(consts, 1)
            pool.iota(iota_i[:], [[1, NE]], base=-NE, channel_multiplier=0).then_inc(consts, 1)
            pool.iota(list_i[:], [[LIST, NE]], base=0, channel_multiplier=0).then_inc(consts, 1)
            pool.iota(block_i[:], [[1, MAX_BLK + 1]], base=0, channel_multiplier=0
                      ).then_inc(consts, 1)
            pool.iota(lines_i[:, 0], [[P, 2]], base=DUMP, channel_multiplier=1)
            pool.iota(lines_i[:, 1], [[P, 2]], base=TAIL_ROW, channel_multiplier=1
                      ).then_inc(consts, 1)
            pool.iota(lines_i[:, 2], [[P, 2]], base=1, channel_multiplier=1).then_inc(consts, 1)
            pool.wait_ge(consts, CONSTS)

            for a in range(2):
                pool.dma_start(out[TAIL_ROW + a * P:TAIL_ROW + (a + 1) * P, :], zeros[:, a, :]
                               ).then_inc(added, 16)

            def cls_inv_std(i, count):
                pool.wait_ge(cls_dve, count)
                pool.tensor_tensor(c_ve[i][:, 0:1], c_mv[i][:, 1:2], eps[0:1, 0:1], ALU.add
                                   ).then_inc(cls_pool, 1)
                pool.wait_ge(cls_pool, 2 * i + 1)
                pool.tensor_tensor(c_rs[i][:, 0:1], c_ve[i][:, 0:1], minus_half[0:1, 0:1], ALU.pow
                                   ).then_inc(cls_pool, 1)

            cls_inv_std(0, 2)
            pool.wait_ge(gate_w_loaded, 48)
            load_high(pool, 0, 0)
            load_stage(pool, 0)
            pool.wait_ge(gate_w_split, 3)
            for i in range(3):
                pool.tensor_tensor(gates_l[i][:], gates_raw[i], gates_h[i][:].bitcast(F32),
                                   ALU.subtract).then_inc(gate_w_split, 1)

            def step(t, par):
                if live(t - 3):
                    inv_std(pool, 2, t - 3)
                if live(t - 1):
                    n = t - 1
                    h0 = H0[1 - par]
                    inv_std(pool, 0, n)
                    if isinstance(n, int) and n == 0:
                        pool.wait_ge(w_loaded, 16 * W_LOADS)
                        pool.wait_ge(lnb_loaded, 16)
                    for i, (bc, semaphore, done) in enumerate((
                            (lng_bc, (hn_done, LT * (n + 1)), hg_done),
                            (lnb_bc, (hg_done, n + 1), h0_done))):
                        pool.wait_ge(*semaphore)
                        pool.tensor_tensor(h0[:], h0[:], over_lt(bc), (ALU.mult, ALU.add)[i]
                                           ).then_inc(done, 1)
                    inv_std(pool, 1, n)
                    pool.wait_ge(u_ready, LT * (n + 1))
                    pool.tensor_tensor(h0[:], h0[:], over_lt(bout_bc), ALU.add
                                       ).then_inc(h0b_done, 1)
                if isinstance(t, int) and t == 1:
                    cls_inv_std(1, 9)
                for g, part in {1: ((0, 0), (0, 1)), 2: ((0, 2),), 3: ((0, 3),),
                                4: ((1, 0), (1, 1)), 5: ((1, 2), (1, 3))
                                }.get(t if isinstance(t, int) else None, ()):
                    split_low(pool, g, g, part)
                if isinstance(t, int) and t == 3:
                    pool.wait_ge(seconds_stored, 16 * NE)
                    pool.wait_ge(cls_slots, 1)
                    for k in range(2):
                        scatter(pool, CV[:], slots[1][:, k, 0:1], cls_scattered)
                    load_high(pool, 1, 1)
                    load_stage(pool, 1)
                if live(t - 4):
                    n = t - 4
                    pool_wait(pool, slots_ready, n + 1)
                    for k in range(2):
                        for lt in range(LT):
                            scatter(pool, V[par][:, lt, :], slots[par][:, k, lt:lt + 1],
                                    scattered[par])

            return step

        def experts_pool(pool):
            load_stage(pool, 2)

            def add_rows(b):
                pool.wait_ge(carried, b * 2 + 1)
                pool_wait(pool, added, b * 32 + 32).then_inc(carried, 1)
                pool.wait_ge(carried, b * 2 + 2)
                pool_wait(pool, y_done, b * 2 + (2 * SBLK + 2), "y").then_inc(carried, 1)
                for a in range(2):
                    pool.indirect_dma_start(
                        out=out, out_offset=bass.IndirectOffsetOnAxis(ap=rows_to[:, a:a + 1],
                                                                      axis=0),
                        in_=yb[:, a, :], in_offset=None, compute_op=ALU.add).then_inc(added, 16)

            def expert(g, i, first, end, prefetch):
                if prefetch:
                    load_high(pool, g + 1, 1 - i)
                add_rows(first)
                if prefetch:
                    split_low(pool, g + 1, 1 - i)
                if prefetch == 2:
                    load_stage(pool, g + 2)
                with pool.Fori(first + 1, end) as b:
                    add_rows(b)

            def limits(g):
                first = pool.value_load(bounds[0:1, bass.ds(g - 1, 1)], min_val=0,
                                        max_val=MAX_BLK - MIN_BLKS)
                end = pool.value_load(bounds[0:1, bass.ds(g, 1)], min_val=MIN_BLKS,
                                      max_val=MAX_BLK)
                return first, end

            pool.wait_ge(bounds_ready, 1)
            pool.wait_ge(cls_stored, 16)
            pool.wait_ge(base_stored, 16 * NIMG)
            pool.tensor_tensor(carrier["start"][:], minus_half[0:1, 0:1], minus_half[0:1, 0:1],
                               ALU.add).then_inc(carried, 1)
            with pool.Fori(0, NE // 2 - 1) as pair:
                for i in (1, 0):
                    g = pair * 2 + (2 - i)
                    expert(g, i, *limits(g), 2)
            expert(NE - 1, 1, *limits(NE - 1), 1)
            expert(NE, 0, *limits(NE), 0)

        def split_product(pe, dst, w, cols, x, width=None):
            parts = [(a, b, k) for a, b in halves for k in range(FT)]
            for q, (a, b, k) in enumerate(parts):
                rhs = x[b][:, k, :] if width is None else x[b][:, k, 0:width]
                last = pe.matmul(dst, w[a][:, k, cols], rhs, start=(q == 0),
                                 stop=(q == len(parts) - 1))
            return last

        def fc(pe, b, i, j, xs, banks):
            if j >= len(banks):
                pe.wait_ge(gelu_done, b * HT + (j - len(banks) + 1))
            split_product(pe, banks[j % len(banks)], (W1H[i], W1L[i]), slice(j * P, (j + 1) * P), xs
                          ).then_inc(fc_ready, 1)

        def project_hidden(pe, b, i, j, banks):
            pe.wait_ge(gl_done, b * HT + (j + 1))
            for a in range(2):
                for q, (g, w) in enumerate(((GH, W2H), (GH, W2L), (GL, W2H))):
                    last = pe.matmul(banks[a], g[:, j, a * P:(a + 1) * P], w[i][:, j, :],
                                     start=(j == 0 and q == 0), stop=(j == HT - 1 and q == 2))
                if j == HT - 1:
                    last.then_inc(y_ps, 1)

        LAG = 3

        def mixer_tensor(pe):
            def columns(row, dst):
                for k in range(FT):
                    for c in range(2):
                        last = pe.matmul(dst[:, 2 * k + c:2 * k + c + 1],
                                         row[0:1, k * P:(k + 1) * P], ones_pp[0:1, 0:1],
                                         start=True, stop=True)
                return last

            def cls_a():
                pe.wait_ge(consts, CONSTS)
                pe.wait_ge(cls_dve, 3)
                columns(c_u, ps_ip[:, 0, :]).then_inc(cls_pe, 1)
                pe.wait_ge(gate_w_split, 6)
                pe.wait_ge(cls_dve, 4)
                for i in range(3):
                    for e in range(FT):
                        dst = ps_ri[:, i // 2, ((i % 2) * FT + e) * 2:((i % 2) * FT + e) * 2 + 2]
                        last = split_product(pe, dst, (gates_h[i], gates_l[i]),
                                             slice(e * P, (e + 1) * P), (c_uh, c_ul))
                last.then_inc(cls_pe, 1)

            def cls_b():
                pe.wait_ge(cls_dve, 7)
                pe.wait_ge(hx_done, 1)
                for k in range(FT):
                    last = pe.matmul(ps_h[0:1, 0, :], c_h[:, k:k + 1], wout_sb[:, k, :],
                                     start=(k == 0), stop=(k == FT - 1))
                last.then_inc(cls_pe, 1)

            def cls_c():
                pe.wait_ge(cls_dve, 10)
                pe.wait_ge(b_done, FT)
                columns(CV, ps_ip[:, 0, :]).then_inc(cls_pe, 1)
                pe.wait_ge(cls_dve, 11)
                pe.wait_ge(prep, 8)
                pe.wait_ge(tanh_done, FT)
                for q, (b, k) in enumerate([(b, k) for b in range(2) for k in range(FT)]):
                    last = pe.matmul(ps_lg[0:2, 0, :], (CXH, CXL)[b][:, k, :], route_hl[:, k, :],
                                     start=(q == 0), stop=(q == 2 * FT - 1))
                last.then_inc(cls_pe, 1)

            def cls_d():
                pe.wait_ge(route_dve, CLS_MASK)
                pe.wait_ge(tanh_done, 2 * FT)
                pe.matmul(ps_tot, ones_r[:], rmask[:, 0, :], start=True, stop=True
                          ).then_inc(cls_pe, 1)

            def head_view(par, lt, h):
                return X[par].rearrange("c (l h) -> c l h", h=H)[:, lt * P:(lt + 1) * P, h]

            def project(n, par, lt):
                pe.wait_ge(x_loaded[par], 8 * (n - par) + 16)
                after(pe, ekv_done, LT * n + lt)
                if lt == 0 and live(n - 5):
                    pe.wait_ge(gelu_done, HT * (n - 4))
                for h in range(H):
                    last = pe.matmul(ps_proj[:, h, :], head_view(par, lt, h), wproj[:, h, :],
                                     start=True, stop=True)
                last.then_inc(proj_ready, 1)

            def transposes(src):
                for lt in range(LT):
                    for f in range(FT):
                        last = pe.transpose(ps_t[:, f, lt * P:(lt + 1) * P],
                                            src[:, lt, f * P:(f + 1) * P], ident[:])
                return last

            def gate_pair(n, e):
                if e == 0:
                    pe.wait_ge(ul_done, n + 1)
                    if live(n - 2):
                        pe.wait_ge(run_ready, n)
                    elif n == 0:
                        pe.wait_ge(cls_dve, 7)
                        pe.wait_ge(cls_act, 2)
                    else:
                        pe.wait_ge(route_dve, 3)
                after(pe, tanh_done, FT * n + e)
                for i in range(2):
                    last = split_product(pe, ps_ri[:, i, :], (gates_h[i], gates_l[i]),
                                         slice(e * P, (e + 1) * P), (UTH, UTL))
                last.then_inc(ri_ready, 1)

            def input_gate(n, e):
                if e == 0:
                    after(pe, b_done, FT * n)
                    if isinstance(n, int) and n == 1:
                        pe.wait_ge(cls_dve, 11)
                split_product(pe, ps_ip[:, e, :], (gates_h[2], gates_l[2]),
                              slice(e * P, (e + 1) * P), (UTH, UTL)).then_inc(ip_ready, 1)

            def transpose_v(n, t, par):
                pe.wait_ge(v_ready, LT * (n + 1))
                pe.wait_ge(yT_sb, at_most(n + 3, NIMG))
                if isinstance(t, int) and t > NIMG:
                    pe.wait_ge(ul_done, NIMG)
                    pe.wait_ge(vl_done, n)
                transposes(V[1 - par]).then_inc(vT_ps, 1)

            def transpose_u(n):
                pe.wait_ge(u_ready, LT * (n + 1))
                after(pe, vl_done, n - 1)
                transposes(U).then_inc(uT_ps, 1)

            def ranks(n):
                pe.wait_ge(mask_done, n + 1)
                for lt in range(LT):
                    for k in range(lt + 1):
                        pe.matmul(ps_rank[:, lt, :], (before_r if k == lt else ones_r)[:],
                                  rmask[:, k, :], start=(k == 0), stop=(k == lt))
                for k in range(LT):
                    last = pe.matmul(ps_tot, ones_r[:], rmask[:, k, :], start=(k == 0),
                                     stop=(k == LT - 1))
                last.then_inc(rank_ready, 1)

            pe.wait_ge(proj_loaded, 16)
            pe.wait_ge(ones_in_x, 2)

            def step(t, par):
                if live(t):
                    project(t, par, 0)
                if live(t - 1):
                    n = t - 1
                    if isinstance(n, int) and n == 0:
                        pe.wait_ge(consts, CONSTS)
                    pe.wait_ge(y_ready, n + 1)
                    after(pe, ul_done, n)
                    transposes(Y).then_inc(yT_ps, 1)
                if live(t - 4):
                    n = t - 4
                    pe.wait_ge(vl_done, n + 1)
                    pe.wait_ge(run_ready, n + 1)
                    pe.wait_ge(tanh_done, at_most(FT * (n + 2), FT * NIMG))
                    for lt in range(LT):
                        for q, (b, k) in enumerate([(b, k) for b in range(2) for k in range(FT)]):
                            last = pe.matmul(ps_lg[:, lt, :],
                                             (XH, XL)[b][par][:, k, lt * P:(lt + 1) * P],
                                             route_hl[:, k, :], start=(q == 0),
                                             stop=(q == 2 * FT - 1))
                    last.then_inc(lg_ready, 1)
                if live(t - 3):
                    n = t - 3
                    pe.wait_ge(scan_done, FT * (n + 1))
                    pe.wait_ge(hx_done, at_most(n + 2, NIMG))
                    for lt in range(LT):
                        for k in range(FT):
                            last = pe.matmul(ps_h[:, lt, :], HS[:, k, lt * P:(lt + 1) * P],
                                             wout_sb[:, k, :], start=(k == 0), stop=(k == FT - 1))
                    last.then_inc(attn_ready, 1)
                if live(t):
                    project(t, par, 1)
                if live(t - 1):
                    n = t - 1
                    if isinstance(n, int) and n == 0:
                        pe.wait_ge(w_loaded, 16 * W_LOADS)
                    pe.wait_ge(yT_sb, n + 1)
                    after(pe, h1_done, n - 1)
                    if isinstance(n, int) and n == 1:
                        pe.wait_ge(cls_row1, 1)
                    for lt in range(LT):
                        for f in range(FT):
                            last = pe.matmul(ps_h[:, lt, :], YT[:, f, lt * P:(lt + 1) * P],
                                             outw_sb[:, f, :], start=(f == 0),
                                             stop=(f == FT - 1))
                        last.then_inc(h_ready, 1)
                if live(t):
                    n = t
                    if isinstance(n, int) and n == 0:
                        pe.wait_ge(prep_act, 1)
                    pe.wait_ge(ekv_done, LT * (n + 1))
                    after(pe, t1_done, LT * n)
                    after(pe, y_done, 2 * (n - 4))
                    for tt in range(LT):
                        for s in range(LT):
                            last = pe.matmul(ps_nd[:, tt, :], ewT[:, s, tt * P:(tt + 1) * P],
                                             E[:, s, :], start=(s == 0), stop=(s == LT - 1))
                        last.then_inc(nd_ready, 1)
                n = t - 4
                for j in range(HT + LAG):
                    if j < HT and live(n):
                        if j == 0 and isinstance(n, int) and n == 0:
                            pe.wait_ge(w_split, 1)
                        if j == 0 and not live(t):
                            pe.wait_ge(gelu_done, HT * n)
                        fc(pe, n, 0, j, (XH[par], XL[par]), fc_loop)
                    if j == 1 and live(n):
                        ranks(n)
                    if j == 3 and live(t - 2):
                        gate_pair(t - 2, 0)
                        input_gate(t - 2, 0)
                    if j == 5 and live(t - 3):
                        transpose_v(t - 3, t, par)
                    if j == 6 and live(t - 2):
                        input_gate(t - 2, 1)
                    if j >= LAG and live(n):
                        if j == LAG and live(t):
                            pe.wait_ge(t1_done, LT * (t + 1))
                        elif j == LAG:
                            after(pe, y_done, 2 * n)
                        project_hidden(pe, n, 0, j - LAG, y_loop)
                    if j == 5 and live(t - 2):
                        gate_pair(t - 2, 1)
                    if j == 6 and isinstance(t, int) and t == 1:
                        cls_a()
                    if j == 7 and live(t - 1):
                        transpose_u(t - 1)
                if isinstance(t, int) and t == 1:
                    cls_b()
                if isinstance(t, int) and t == 2:
                    cls_c()
                if isinstance(t, int) and t == 3:
                    cls_d()

            return step

        def experts_tensor(pe):
            def transpose_rows(b):
                pe.wait_ge(rows_loaded, b * 16 + 16)
                after(pe, xl_ready, b)
                for a in range(2):
                    for f in range(FT):
                        last = pe.transpose(ps_t[:, f, a * P:(a + 1) * P],
                                            R[:, a, f * P:(f + 1) * P], ident[:])
                last.then_inc(pt_ready, 1)

            def block(b, i, g):
                pe.wait_ge(w_split, g + 1)
                pe.wait_ge(xl_ready, b + 1)
                for j in range(HT):
                    fc(pe, b + SBLK, i, j, (XH[0], XL[0]), fc_after)
                    if j >= LAG:
                        if j == LAG:
                            pe.wait_ge(y_done, b * 2 + 2 * SBLK)
                        project_hidden(pe, b + SBLK, i, j - LAG, y_loop)
                transpose_rows(b + 1)
                for j in range(HT - LAG, HT):
                    project_hidden(pe, b + SBLK, i, j, y_loop)

            b = NIMG
            for j in range(HT):
                if j >= len(fc_loop):
                    pe.wait_ge(gelu_done, b * HT + (j - len(fc_loop) + 1))
                split_product(pe, fc_loop[j % 2][:, 0:2], (W1H[0], W1L[0]),
                              slice(j * P, (j + 1) * P), (CXH, CXL)).then_inc(fc_ready, 1)
            pe.wait_ge(vl_done, NIMG)
            transpose_rows(0)
            pe.wait_ge(gl_done, b * HT + HT)
            pe.wait_ge(y_done, 2 * b)
            for j in range(HT):
                for q, (g, w) in enumerate(((GH, W2H), (GH, W2L), (GL, W2H))):
                    last = pe.matmul(y_loop[0][0:2, :], g[:, j, 0:2], w[0][:, j, :],
                                     start=(j == 0 and q == 0), stop=(j == HT - 1 and q == 2))
            last.then_inc(y_ps, 2)
            pe.wait_ge(b_done, FT * NIMG)
            experts(pe, block)

        def experts(eng, block, start=None, finish=None):
            eng.wait_ge(bounds_ready, 1)
            with eng.Fori(0, NE // 2) as pair:
                for i in (1, 0):
                    g = pair * 2 + (2 - i)
                    first = eng.value_load(bounds[0:1, bass.ds(g - 1, 1)], min_val=0,
                                           max_val=MAX_BLK - MIN_BLKS)
                    end = eng.value_load(bounds[0:1, bass.ds(g, 1)], min_val=MIN_BLKS,
                                         max_val=MAX_BLK)
                    if start:
                        start(g, i, pair + (1 - i))
                    with eng.Fori(first, end) as b:
                        block(b, i, g)
                    if finish:
                        finish(g, i)

        def gelu(act, b, i, j, banks, width=BLK):
            act.wait_ge(fc_ready, b * HT + (j + 1))
            if j >= G_SLOTS:
                act.wait_ge(gl_done, b * HT + (j - G_SLOTS + 1))
            act.activation(g_act[:, j % G_SLOTS, 0:width], banks[j % len(banks)][:, 0:width],
                           ACT.Gelu_apprx_tanh, bias=fcb[i][:, j:j + 1]).then_inc(gelu_done, 1)

        def mixer_scalar(act):
            def exp_and_tanh(n, par, lt):
                act.wait_ge(proj_ready, LT * n + lt + 1)
                after(act, nd_ready, LT * n)
                act.activation(E[:, lt, M:2 * M].rearrange("p (h d) -> p h d", h=H),
                               ps_proj[:, :, D:2 * D], ACT.Exp).then_inc(exp_done, 1)
                after(act, t1_done, LT * n)
                act.activation(tanh_q[:, lt, :].rearrange("p (h d) -> p h d", h=H),
                               ps_proj[:, :, 0:D], ACT.Tanh, scale=0.5)
                after(act, hx_done, n - 1)
                act.copy(XR[par][:, lt, :].rearrange("p (h d) -> p h d", h=H),
                         ps_proj[:, :, 3 * D:4 * D]).then_inc(tq_done, 1)

            def cls_a():
                act.wait_ge(cls_pe, 1)
                act.copy(c_uh[:].rearrange("p k c -> p (k c)"), ps_ip[:, 0, 0:2 * FT]
                         ).then_inc(cls_act, 1)
                act.wait_ge(cls_pe, 2)
                act.wait_ge(prep, 3)
                for i in range(2):
                    for e in range(FT):
                        c = (i * FT + e) * 2
                        last = act.activation(c_g[:, i, e:e + 1], ps_ri[:, 0, c:c + 1],
                                              ACT.Tanh, bias=bhalf[:, i, e:e + 1], scale=0.5)
                last.then_inc(cls_act, 1)

            def tanh_route(n):
                act.wait_ge(dif_done, n + 2)
                act.activation(rtanh[:], rdif[:], ACT.Tanh, scale=0.5).then_inc(route_act, 1)

            def high_g(n, j):
                act.wait_ge(gelu_done, n * HT + (j + 1))
                act.copy(GH[:, j, :], g_act[:, j % G_SLOTS, :]).then_inc(gh_done, 1)

            def tanh_gates(n, e):
                act.wait_ge(ri_ready, FT * n + e + 1)
                after(act, s_done, n)
                if isinstance(n, int) and n == 0:
                    act.wait_ge(gate_w_split, 6)
                act.activation(TR[:, e, :], ps_ri[:, 0, :], ACT.Tanh, bias=bhalf[:, 0, e:e + 1],
                               scale=0.5)
                act.activation(TI[:, e, :], ps_ri[:, 1, :], ACT.Tanh, bias=bhalf[:, 1, e:e + 1],
                               scale=0.5).then_inc(tanh_done, 1)

            def step(t, par):
                if live(t):
                    exp_and_tanh(t, par, 0)
                if live(t - 1):
                    act.wait_ge(yT_ps, t)
                    act.copy(YT[:], ps_t[:]).then_inc(yT_sb, 1)
                if isinstance(t, int) and t == 0:
                    act.wait_ge(prep, 2)
                    act.activation(ewT[:], ewT[:], ACT.Exp).then_inc(prep_act, 1)
                    act.wait_ge(prep, 4)
                    act.activation(a_exp[:, 0], a_clip[:, 0], ACT.Exp)
                    act.activation(a_exp[:, 1], a_clip[:, 1], ACT.Exp, scale=-1.0
                                   ).then_inc(prep_act, 1)
                if live(t):
                    exp_and_tanh(t, par, 1)
                if isinstance(t, int) and t == 0:
                    act.wait_ge(gate_w_loaded, 48)
                    for i in range(3):
                        act.copy(gates_h[i][:], gates_raw[i]).then_inc(gate_w_split, 1)
                if live(t - 4) and live(t):
                    tanh_route(t - 4)
                n = t - 4
                for j in range(HT + 1):
                    if live(n):
                        if isinstance(n, int) and n == 0 and j == 0:
                            act.wait_ge(biases_loaded[0], 32)
                        if j < HT:
                            gelu(act, n, 0, j, fc_loop)
                        if j == 0 and not live(t):
                            tanh_route(n)
                        if j:
                            high_g(n, j - 1)
                    if live(t - 3) and j == 5:
                        act.wait_ge(vT_ps, t - 2)
                        after(act, fc_ready, HT * (t - 4))
                        act.copy(XH[1 - par][:], ps_t[:]).then_inc(vh_done, 1)
                    if live(t - 2) and j in (3, 5):
                        tanh_gates(t - 2, j // 5)
                    if isinstance(t, int) and t == 1 and j == 6:
                        cls_a()
                    if live(t - 1) and j == 7:
                        act.wait_ge(uT_ps, t)
                        after(act, ip_ready, FT * (t - 1))
                        act.copy(UTH[:], ps_t[:]).then_inc(uh_done, 1)
                if isinstance(t, int) and t == 2:
                    act.wait_ge(cls_pe, 4)
                    act.copy(CXH[:].rearrange("p k c -> p (k c)"), ps_ip[:, 0, 0:2 * FT]
                             ).then_inc(cls_act, 1)
                    tanh_route(-1)

            return step

        def experts_scalar(act):
            for j in range(HT):
                gelu(act, NIMG, 0, j, fc_loop, 2)

            def high_x(b):
                act.wait_ge(pt_ready, b + 1)
                act.copy(XH[0][:], ps_t[:]).then_inc(xh_ready, 1)

            def start(g, i, nth):
                act.wait_ge(biases_loaded[i], nth * 32 + 32)

            def block(b, i, g):
                for j in range(HT):
                    gelu(act, b + SBLK, i, j, fc_after)
                high_x(b + 1)

            high_x(0)
            experts(act, block, start)

        def low_g(dve, b, j, width=BLK):
            dve.wait_ge(gh_done, b * HT + (j + 1))
            dve.tensor_tensor(GL[:, j, 0:width], g_act[:, j % G_SLOTS, 0:width],
                              GH[:, j, 0:width].bitcast(F32), ALU.subtract).then_inc(gl_done, 1)

        def mixer_vector(dve):
            def routed(n, instruction, k):
                instruction.then_inc(route_dve, 1)
                dve.wait_ge(route_dve, ROUTE * n + (CLS_ROUTE + k))

            def stats(i, srcs, n):
                for lt, src in enumerate(srcs):
                    dve.bn_stats(st[i][:, lt, :], src).then_inc(raw[i], 1)
                dve_wait(dve, raw[i], LT * (n + 1))
                for lt in range(LT):
                    dve.bn_aggr(mv[i][:, lt, :], st[i][:, lt, :]).then_inc(mv_done[i], 1)

            def norm(i, dst, src, lt):
                return dve.tensor_scalar(dst, src, mv[i][:, lt, 0:1], rstd[i][:, lt:lt + 1],
                                         ALU.subtract, ALU.mult)

            def choose(chain, valid=None):
                source = rlg
                for k in range(2):
                    chain(dve.tensor_reduce(rmax[k][:], source[:], AX.X, ALU.max))
                    chain(dve.tensor_tensor(rhit[:], source[:], over_e(rmax[k][:]), ALU.is_equal))
                    chain(dve.tensor_tensor(rcand[:], rhit[:], over_lt(iota_m), ALU.mult))
                    chain(dve.tensor_reduce(ridx[:, k, :], rcand[:], AX.X, ALU.min))
                    chain(dve.tensor_tensor(rone[k][:], over_lt(iota_m), over_e(ridx[:, k, :]),
                                            ALU.is_equal))
                    if k == 0:
                        chain(dve.scalar_tensor_tensor(rlg2[:], rone[0][:], -BIG, rlg[:], ALU.mult,
                                                       ALU.add))
                        source = rlg2

            for i in range(2):
                dve.memset(X[i][C:KA, :], 1.0).then_inc(ones_in_x, 1)
            dve.wait_ge(cls_loaded, 16)
            dve.bn_stats(c_st[0][:], c_row[:]).then_inc(cls_dve, 1)
            dve.wait_ge(cls_dve, 1)
            dve.bn_aggr(c_mv[0][:], c_st[0][:]).then_inc(cls_dve, 1)
            dve.wait_ge(prep_loaded, 16 * 6)
            dve.tensor_copy(mask_f[:], mask_sb[:].bitcast(U8)).then_inc(prep, 1)
            dve.wait_ge(prep, 1)
            dve.tensor_tensor(ewT[:], ewT[:], mask_f[:], ALU.mult).then_inc(prep, 1)
            dve.tensor_scalar(bhalf[:], col_raw[:, 0:2], 0.5, None, ALU.mult).then_inc(prep, 1)
            for i, op in enumerate((ALU.min, ALU.max)):
                last = dve.tensor_scalar(a_clip[:, i], col_raw[:, 2], 0.0, None, op)
            last.then_inc(prep, 1)
            def constants():
                dve.wait_ge(cls_pool, 2)
                dve.tensor_scalar(c_u[:], c_row[:], c_mv[0][:, 0:1], c_rs[0][:, 0:1],
                                  ALU.subtract, ALU.mult).then_inc(cls_dve, 1)
                dve.wait_ge(prep_act, 2)
                dve.tensor_tensor(a_den[:], a_exp[:, 0], a_exp[:, 1], ALU.add).then_inc(prep, 1)
                dve.wait_ge(prep, 5)
                dve.reciprocal(a_rec[:], a_den[:]).then_inc(prep, 1)
                dve.wait_ge(prep, 6)
                dve.scalar_tensor_tensor(a_half[:], a_exp[:, 0], 0.5, a_rec[:], ALU.mult, ALU.mult
                                         ).then_inc(prep, 1)
                route_h = route_hl[:, :, 0:NE]
                dve.wait_ge(w_loaded, 16 * W_LOADS)
                dve.tensor_copy(route_h, route_sb[:]).then_inc(route_w, 1)
                dve.wait_ge(route_w, 1)
                dve.tensor_tensor(route_hl[:, :, NE:2 * NE], route_sb[:], route_h.bitcast(F32),
                                  ALU.subtract
                                  ).then_inc(prep, 1)
                dve.wait_ge(consts, CONSTS)
                dve.tensor_copy(iota_m[:], iota_i[:])
                dve.tensor_copy(ones_r[:], ones_pp[:])
                dve.tensor_copy(before_r[:], before[:])
                dve.tensor_copy(list_f[:], list_i[:])
                dve.tensor_copy(block_f[:], block_i[:])
                dve.tensor_copy(lines_f[:], lines_i[:]).then_inc(lines, 1)
                dve.memset(number[1][:], float(-NE))
                dve.memset(number[0][:], float(1 - NE))
                dve.wait_ge(lines, 1)
                dve.tensor_copy(tail_rows[:, :, OUT_ROW], lines_f[:, 1]).then_inc(lines, 1)
                for i in range(2):
                    dve.tensor_scalar(V[i][:, :, OUT_ROW], lines_f[:, 2], float((i - 2) * SEQ),
                                      None, ALU.add).then_inc(lines, 1)

            def cls_low():
                dve.wait_ge(cls_act, 1)
                dve.tensor_tensor(c_ul[:].rearrange("p k c -> p (k c)"), ps_ip[:, 0, 0:2 * FT],
                                  c_uh[:].rearrange("p k c -> p (k c)").bitcast(F32), ALU.subtract
                                  ).then_inc(cls_dve, 1)

            def cls_a():
                dve.wait_ge(cls_act, 2)
                dve.wait_ge(prep, 8)
                dve.scalar_tensor_tensor(c_a[:], c_g[:, 0], 1.0, a_half[:], ALU.add, ALU.mult
                                         ).then_inc(cls_dve, 1)
                dve.wait_ge(cls_dve, 5)
                dve.tensor_scalar(c_om[:], c_a[:], -0.5, 0.5, ALU.mult, ALU.add).then_inc(cls_dve, 1)
                dve.wait_ge(cls_dve, 6)
                dve.scalar_tensor_tensor(c_s[:], c_g[:, 1], 1.0, c_om[:], ALU.add, ALU.mult
                                         ).then_inc(cls_s, 1)
                dve.wait_ge(cls_s, 1)
                for e in range(FT):
                    last = dve.scalar_tensor_tensor(c_h[:, e:e + 1], ps_ri[:, 1, 2 * e:2 * e + 1],
                                                    col_raw[:, 3, e:e + 1], c_s[:, e:e + 1],
                                                    ALU.add, ALU.mult)
                last.then_inc(cls_dve, 1)

            def cls_b():
                dve.wait_ge(cls_pe, 3)
                dve.tensor_tensor(c_h1[:], c_row[:], ps_h[0:1, 0, :], ALU.add).then_inc(cls_row1, 1)
                dve.wait_ge(cls_row1, 1)
                dve.tensor_tensor(c_h1[:], c_h1[:], bout_bc[0:1, :], ALU.add).then_inc(cls_row1, 1)
                dve.wait_ge(cls_row1, 2)
                dve.bn_stats(c_st[1][:], c_h1[:]).then_inc(cls_dve, 1)
                dve.wait_ge(cls_dve, 8)
                dve.bn_aggr(c_mv[1][:], c_st[1][:]).then_inc(cls_dve, 1)
                dve.wait_ge(cls_pool, 4)
                dve.tensor_scalar(CV[0:1, 0:M], c_h1[:], c_mv[1][:, 0:1], c_rs[1][:, 0:1],
                                  ALU.subtract, ALU.mult).then_inc(cls_dve, 1)

            def cls_c():
                count = [0]

                def chain(instruction):
                    count[0] += 1
                    instruction.then_inc(route_dve, 1)
                    dve.wait_ge(route_dve, count[0])

                valid = ident[:, 0:1]
                dve.wait_ge(cls_act, 3)
                dve.tensor_tensor(CXL[:].rearrange("p k c -> p (k c)"), ps_ip[:, 0, 0:2 * FT],
                                  CXH[:].rearrange("p k c -> p (k c)").bitcast(F32), ALU.subtract
                                  ).then_inc(cls_dve, 1)
                chain(dve.memset(rlg[:], 0.0))
                dve.wait_ge(cls_pe, 5)
                chain(dve.tensor_copy(rlg[0:1, 0, :], ps_lg[0:1, 0, 0:NE]))
                chain(dve.tensor_tensor(rlg[0:1, 0, :], rlg[0:1, 0, :], ps_lg[0:1, 0, NE:2 * NE],
                                        ALU.add))
                choose(chain)
                chain(dve.tensor_tensor(rhit[:], rone[0][:], rone[1][:], ALU.add))
                chain(dve.tensor_scalar(rmask[:], rhit[:], valid, None, ALU.mult))
                assert count[0] == CLS_MASK, count
                dve.tensor_tensor(rdif[:], rmax[1][:], rmax[0][:], ALU.subtract
                                  ).then_inc(dif_done, 1)
                dve.wait_ge(route_act, 1)
                chain(dve.tensor_copy(CV[0:1, FIRST_E:FIRST_E + 1], ridx[0:1, 0, 0:1]))
                chain(dve.tensor_scalar(CV[0:1, GATE_DIFF:GATE_DIFF + 1], rtanh[0:1, 0:1], -1.0, None,
                                        ALU.mult))
                chain(dve.tensor_scalar(CV[0:1, GATE2:GATE2 + 1], rtanh[0:1, 0:1], 0.5, 0.5,
                                        ALU.mult, ALU.add))
                chain(dve.memset(CV[0:1, OUT_ROW:OUT_ROW + 1], float(CLS_ROW)))
                for k in range(2):
                    chain(dve.tensor_tensor(rsel[k][:], rone[k][:], over_lt(list_f), ALU.mult))
                    chain(dve.tensor_reduce(rslot[:, k, :], rsel[k][:], AX.X, ALU.add))
                    chain(dve.tensor_tensor(rsel[k][:, 0, 0:1], rslot[:, k, 0:1],
                                            lines_f[:, 0, k:k + 1], ALU.subtract))
                    chain(dve.scalar_tensor_tensor(rslot[:, k, 0:1], rsel[k][:, 0, 0:1], valid,
                                                   lines_f[:, 0, k:k + 1], ALU.mult, ALU.add))
                dve.tensor_copy(slots[1][:], rslot[:]).then_inc(cls_slots, 1)
                assert count[0] == CLS_ROUTE, count

            def cls_d():
                dve.wait_ge(cls_pe, 6)
                dve.tensor_tensor(run[:], list_f[:], ps_tot, ALU.add).then_inc(run_ready, 1)

            def ekv(n, lt):
                dve.wait_ge(tq_done, LT * n + lt + 1)
                dve.tensor_tensor(E[:, lt, 0:M].rearrange("p (h d) -> p h d", h=H),
                                  ps_proj[:, :, 2 * D:3 * D],
                                  E[:, lt, M:2 * M].rearrange("p (h d) -> p h d", h=H), ALU.mult
                                  ).then_inc(ekv_done, 1)

            def numerator(n, tt):
                dve.wait_ge(nd_ready, LT * n + tt + 1)
                dve.reciprocal(rden[:, tt, :], ps_nd[:, tt, M:2 * M]).then_inc(recip_done, 1)
                if tt == 0:
                    after(dve, yT_ps, n)
                dve.scalar_tensor_tensor(Y[:, tt, :], tanh_q[:, tt, :], 1.0, ps_nd[:, tt, 0:M],
                                         ALU.add, ALU.mult).then_inc(t1_done, 1)

            def shared(n, js):
                if live(n):
                    for j in js:
                        low_g(dve, n, j)

            def step(t, par):
                if live(t):
                    ekv(t, 0)
                if live(t - 4):
                    n = t - 4
                    dve.wait_ge(lg_ready, n + 1)
                    k = [0]

                    def chain(instruction):
                        k[0] += 1
                        routed(n, instruction, k[0])

                    dve.tensor_copy(rlg2[:], ps_lg[:, :, 0:NE]).then_inc(lg_copied, 1)
                    dve.wait_ge(lg_copied, n + 1)
                    dve.tensor_tensor(rlg[:], rlg2[:], ps_lg[:, :, NE:2 * NE], ALU.add
                                      ).then_inc(lg_done, 1)
                    dve.wait_ge(lg_done, n + 1)
                    choose(chain)
                    dve.tensor_tensor(rmask[:], rone[0][:], rone[1][:], ALU.add
                                      ).then_inc(mask_done, 1)
                    dve.tensor_tensor(rdif[:], rmax[1][:], rmax[0][:], ALU.subtract
                                      ).then_inc(dif_done, 1)
                if live(t - 3):
                    n = t - 3
                    h1, h0 = H1[1 - par], H0[1 - par]
                    dve.wait_ge(attn_ready, n + 1)
                    dve.wait_ge(h0b_done, n + 1)
                    after(dve, sum_done, n - 1)
                    dve.tensor_tensor(h1[:], h0[:], ps_h[:], ALU.add).then_inc(h1_done, 1)
                    dve_wait(dve, h1_done, n + 1)
                    stats(2, [h1[:, lt, :] for lt in range(LT)], n)
                if live(t):
                    ekv(t, 1)
                if live(t - 3):
                    n = t - 3
                    v = V[1 - par]
                    dve.wait_ge(rstd_done[2], n + 1)
                    if live(n - 2):
                        dve.wait_ge(scattered[1 - par], 16 * LT * (n - (1 - par)))
                    for lt in range(LT):
                        norm(2, v[:, lt, 0:M], h1[:, lt, :], lt).then_inc(v_ready, 1)
                if live(t - 1):
                    n = t - 1
                    dve.wait_ge(h_ready, LT * (n + 1))
                    h0 = H0[1 - par]
                    dve.tensor_tensor(h0[:], XR[1 - par][:], ps_h[:], ALU.add).then_inc(hx_done, 1)
                    dve_wait(dve, hx_done, n + 1)
                    stats(0, [h0[:, lt, :] for lt in range(LT)], n)
                if live(t):
                    numerator(t, 0)
                if live(t - 1):
                    n = t - 1
                    h0 = H0[1 - par]
                    dve.wait_ge(rstd_done[0], n + 1)
                    for lt in range(LT):
                        norm(0, h0[:, lt, :], h0[:, lt, :], lt).then_inc(hn_done, 1)
                if live(t - 4):
                    n = t - 4
                    v = V[par]
                    dve.wait_ge(route_act, n + 2)
                    chain(dve.tensor_copy(v[:, :, FIRST_E], ridx[:, 0, :]))
                    dve.tensor_scalar(v[:, :, GATE_DIFF], rtanh[:], -1.0, None, ALU.mult)
                    chain(dve.tensor_scalar(v[:, :, GATE2], rtanh[:], 0.5, 0.5, ALU.mult, ALU.add))
                    dve.wait_ge(rank_ready, n + 1)
                    chain(dve.tensor_tensor(rpos[:], ps_rank, over_lt(run), ALU.add))
                    dve.tensor_tensor(run[:], run[:], ps_tot, ALU.add).then_inc(run_ready, 1)
                    if isinstance(n, int) and n == NIMG - 1:
                        dve.wait_ge(run_ready, NIMG + 1)
                        dve.tensor_copy(ends_i[:], run[:]).then_inc(ends_ready, 1)
                shared(t - 4, range(0, 1))
                if live(t):
                    numerator(t, 1)
                    dve.wait_ge(t1_done, LT * (t + 1))
                    dve.wait_ge(recip_done, LT * (t + 1))
                    dve.scalar_tensor_tensor(Y[:], Y[:], 0.5, rden[:], ALU.mult, ALU.mult
                                             ).then_inc(y_ready, 1)
                if isinstance(t, int) and t == 1:
                    cls_low()
                shared(t - 4, range(1, 2))
                if live(t - 4):
                    v = V[par]
                    if isinstance(n, int) and n == 0:
                        dve.wait_ge(lines, 4)
                    chain(dve.tensor_scalar(v[:, :, OUT_ROW], v[:, :, OUT_ROW], float(2 * SEQ), None,
                                            ALU.add))
                    for k2 in range(2):
                        dve.tensor_tensor(rsel[k2][:], rone[k2][:], rpos[:], ALU.mult
                                          ).then_inc(sel_done, 1)
                    dve.wait_ge(sel_done, 2 * (n + 1))
                    for k2 in range(2):
                        last = dve.tensor_reduce(rslot[:, k2, :], rsel[k2][:], AX.X, ALU.add)
                    chain(last)
                    assert k[0] == ROUTE, k
                    if isinstance(n, int) and n == 1:
                        dve.wait_ge(cls_scattered, 32)
                    dve.tensor_copy(slots[par][:], rslot[:]).then_inc(slots_ready, 1)
                if live(t - 1):
                    n = t - 1
                    dve_wait(dve, h0_done, n + 1)
                    stats(1, [H0[1 - par][:, lt, :] for lt in range(LT)], n)
                shared(t - 4, range(2, 3))
                if live(t - 1):
                    n = t - 1
                    dve.wait_ge(rstd_done[1], n + 1)
                    after(dve, uT_ps, n)
                    for lt in range(LT):
                        norm(1, U[:, lt, :], H0[1 - par][:, lt, :], lt).then_inc(u_ready, 1)
                shared(t - 4, range(3, 4))
                if live(t - 3):
                    n = t - 3
                    dve.wait_ge(vh_done, n + 1)
                    dve.tensor_tensor(XL[1 - par][:], ps_t[:], XH[1 - par][:].bitcast(F32),
                                      ALU.subtract).then_inc(vl_done, 1)
                if live(t - 2):
                    n = t - 2
                    dve.wait_ge(tanh_done, FT * (n + 1))
                    if isinstance(n, int) and n == 0:
                        dve.wait_ge(gate_w_split, 6)
                    for e in range(FT):
                        dve.tensor_scalar(A[:, e, :], TR[:, e, :], 1.0, a_half[:, e:e + 1],
                                          ALU.add, ALU.mult).then_inc(a_done, 1)
                shared(t - 4, range(4, 5))
                if live(t - 2):
                    dve.wait_ge(a_done, FT * (n + 1))
                    dve.tensor_scalar(S[:], A[:], -0.5, 0.5, ALU.mult, ALU.add).then_inc(om_done, 1)
                    dve.wait_ge(om_done, n + 1)
                    dve.scalar_tensor_tensor(S[:], TI[:], 1.0, S[:], ALU.add, ALU.mult
                                             ).then_inc(s_done, 1)
                shared(t - 4, range(5, 6))
                if live(t - 2):
                    n = t - 2
                    dve.wait_ge(s_done, n + 1)
                    dve.wait_ge(ip_ready, FT * (n + 1))
                    for e in range(FT):
                        dve.scalar_tensor_tensor(S[:, e, :], ps_ip[:, e, :], col_raw[:, 3, e:e + 1],
                                                 S[:, e, :], ALU.add, ALU.mult
                                                 ).then_inc(b_done, 1)
                shared(t - 4, range(6, 7))
                if live(t - 2):
                    n = t - 2
                    dve.wait_ge(b_done, FT * (n + 1))
                    after(dve, attn_ready, n)
                    for e in range(FT):
                        dve.tensor_tensor_scan(HS[:, e, :], A[:, e, :], S[:, e, :], c_h[:, e:e + 1],
                                               ALU.mult, ALU.add).then_inc(scan_done, 1)
                shared(t - 4, range(7, 8))
                if live(t - 1):
                    n = t - 1
                    dve.wait_ge(uh_done, n + 1)
                    dve.tensor_tensor(UTL[:], ps_t[:], UTH[:].bitcast(F32), ALU.subtract
                                      ).then_inc(ul_done, 1)
                if live(t - 4):
                    n = t - 4
                    for a in range(2):
                        dve.wait_ge(y_ps, 2 * n + a + 1)
                        if a == 0:
                            after(dve, base_stored, 16 * n)
                        dve.tensor_tensor(yb[:, a, :], y_loop[a], pjb[0][:], ALU.add
                                          ).then_inc(y_done, 1)
                    dve.wait_ge(y_done, 2 * (n + 1))
                    dve.tensor_tensor(yb[:], yb[:], H1[par][:], ALU.add).then_inc(sum_done, 1)
                if isinstance(t, int) and t == 0:
                    constants()
                if isinstance(t, int) and t == 1:
                    cls_a()
                    cls_b()
                if isinstance(t, int) and t == 2:
                    cls_c()
                if isinstance(t, int) and t == 3:
                    cls_d()
                    dve.wait_ge(biases_loaded[0], 32)

            return step

        def experts_vector(dve):
            count = [0]

            def chain(instruction):
                count[0] += 1
                instruction.then_inc(count_dve, 1)
                dve.wait_ge(count_dve, count[0])

            dve.wait_ge(run_ready, NIMG + 1)
            chain(dve.tensor_tensor(cnt["size"][:], run[:], list_f[:], ALU.subtract))
            chain(dve.tensor_scalar(cnt_i[:], cnt["size"][:], float(BLK - 1), None, ALU.add))
            chain(dve.tensor_scalar(cnt_s[:], cnt_i[:], BLK.bit_length() - 1, None,
                                    ALU.arith_shift_right))
            chain(dve.tensor_copy(cnt["n"][:], cnt_s[:]))
            chain(dve.tensor_scalar(cnt["blocks"][:], cnt["n"][:], float(MIN_BLKS), None, ALU.max))
            chain(dve.tensor_tensor_scan(cnt["end"][:], ones_pp[:, 0:NE], cnt["blocks"][:],
                                         0.0, ALU.mult, ALU.add))
            dve.memset(bounds[:, 0:1], 0)
            dve.tensor_copy(bounds[:, 1:NE + 1], cnt["end"][:]).then_inc(bounds_ready, 1)
            dve.tensor_scalar(cnt["skip"][:], cnt["blocks"][:], -1.0, float(LIST_BLKS),
                              ALU.mult, ALU.add)
            dve.tensor_copy(hop[:, NE - 1, :], block_f[:])
            chain(dve.memset(carrier["count"][:], 0.0))
            for e in range(NE - 1):
                last = dve.tensor_scalar(hop[:, e, :], block_f[:], cnt["end"][:, e:e + 1],
                                         cnt["skip"][:, e:e + 1], ALU.is_ge, ALU.mult)
            chain(last)
            chain(dve.tensor_reduce(where[:], hop[:].rearrange("p e b -> p b e"), AX.X, ALU.add))
            dve.tensor_copy(where_i[:], where[:]).then_inc(where_ready, 1)

            def next_info(b):
                dve.wait_ge(rows_loaded, b * 16 + 16)
                dve.tensor_copy(info[:], R[:, :, M:W]).then_inc(info_read, 1)

            def next_x(b):
                dve.wait_ge(xh_ready, b + 1)
                dve.tensor_tensor(XL[0][:], ps_t[:], XH[0][:].bitcast(F32), ALU.subtract
                                  ).then_inc(xl_ready, 1)

            b = NIMG
            for j in range(HT):
                dve.wait_ge(gelu_done, b * HT + (j + 1))
                dve.tensor_copy(GH[:, j, 0:2], g_act[:, j % G_SLOTS, 0:2]).then_inc(gh_done, 1)
                low_g(dve, b, j, 2)
            next_info(0)
            next_x(0)
            dve.wait_ge(y_ps, 2 * b + 2)
            for a in range(2):
                cols = slice(a * P, (a + 1) * P)
                dve.tensor_tensor(c_y[:, cols], y_loop[0][0:1, cols], pjb[0][0:1, cols], ALU.add
                                  ).then_inc(y_done, 1)
            dve.wait_ge(y_done, 2 * b + 2)
            dve.tensor_tensor(c_y[:], c_y[:], c_h1[:], ALU.add).then_inc(cls_base, 1)
            dve.memset(carrier["end"][:], 0.0).then_inc(expert_done, 1)
            dve.wait_ge(base_stored, 16 * NIMG)

            def start(g, i, nth):
                dve_wait(dve, biases_loaded[i], nth * 32 + 32)
                dve_wait(dve, expert_done, g, "end")

            def block(b, i, g):
                for j in range(HT):
                    dve.wait_ge(gelu_done, (b + SBLK) * HT + (j + 1))
                    dve.tensor_copy(GH[:, j, :], g_act[:, j % G_SLOTS, :]).then_inc(gh_done, 1)
                    if j:
                        low_g(dve, b + SBLK, j - 1)
                    if j == 4:
                        dve.wait_ge(info_read, b + 1)
                        dve.tensor_scalar(info_t[:], info[:, :, 0], number[i][:], None,
                                          ALU.is_equal).then_inc(info_done, 1)
                    if j == 5:
                        dve.wait_ge(info_done, b * 4 + 1)
                        dve.tensor_tensor(info_t[:], info_t[:], info[:, :, 1], ALU.mult
                                          ).then_inc(info_done, 1)
                    if j == 6:
                        dve.wait_ge(info_done, b * 4 + 2)
                        dve.tensor_tensor(gate[:], info_t[:], info[:, :, 2], ALU.add
                                          ).then_inc(info_done, 1)
                low_g(dve, b + SBLK, HT - 1)
                next_x(b + 1)
                dve.wait_ge(added, b * 32 + 32)
                dve.tensor_copy(rows_to[:], info[:, :, 3]).then_inc(info_done, 1)
                dve.wait_ge(info_done, b * 4 + 4)
                next_info(b + 1)
                for a in range(2):
                    dve.wait_ge(y_ps, b * 2 + (2 * SBLK + a + 1))
                    dve.tensor_tensor(yt[:, a, :], y_loop[a], pjb[i][:], ALU.add
                                      ).then_inc(yt_done, 1)
                dve.wait_ge(yt_done, b * 2 + 2)
                for a in range(2):
                    dve.tensor_scalar(yb[:, a, :], yt[:, a, :], gate[:, a:a + 1], None, ALU.mult
                                      ).then_inc(y_done, 1)

            def finish(g, i):
                dve.tensor_scalar(number[i][:], number[i][:], 2.0, None, ALU.add
                                  ).then_inc(expert_done, 1)

            experts(dve, block, start, finish)

        block = ctx.enter_context(nc.Block())

        @block.sync
        def _(sp):
            steps(mixer_sync(sp))(sp)
            experts_sync(sp)

        @block.gpsimd
        def _(pool):
            steps(mixer_pool(pool))(pool)
            experts_pool(pool)

        @block.scalar
        def _(act):
            steps(mixer_scalar(act))(act)
            experts_scalar(act)

        @block.vector
        def _(dve):
            steps(mixer_vector(dve))(dve)
            experts_vector(dve)

        @block.tensor
        def _(pe):
            steps(mixer_tensor(pe))(pe)
            experts_tensor(pe)




def kernel(**inputs):
    import numpy as np
    import concourse.bacc as bacc
    from concourse import mybir as my
    from concourse.bass_utils import run_bass_kernel_spmd as run

    g = {k: np.asarray(v) for k, v in inputs.items()}
    x = g["x"]
    nimg, c, length, heads = x.shape
    d = g["L0_tok_Wq_w"].shape[0]
    m = heads * d
    w_qkv = np.concatenate([np.concatenate([g[f"L0_tok_W{i}_w"].T, g[f"L0_tok_W{i}_b"][None]], 0)
                            for i in "qkv"], 1)
    w_resid = np.concatenate([np.broadcast_to(np.eye(c, dtype=x.dtype)[:, None, :], (c, heads, d)),
                              g["L0_tok_out_b"].reshape(1, heads, d)], 0)
    w_proj = np.concatenate([np.broadcast_to(w_qkv[:, None, :], (c + 1, heads, 3 * d)), w_resid], 2)
    arrays = {
        "x": x.reshape(nimg, c, length * heads),
        "cls_tok": g["cls_tok"].reshape(1, m),
        "w_proj": w_proj,
        "bias_t": g["L0_tok_w_bias"].T,
        "mask_t": np.ascontiguousarray(g["L0_tok_local_mask"].T).view(np.int32),
        "out_w": g["L0_tok_out_w"], "ln_g": g["L0_tok_ln_g"], "ln_b": g["L0_tok_ln_b"],
        "w_in": g["L0_attn_W_in"], "w_r": g["L0_attn_W_r"], "w_i": g["L0_attn_W_i"],
        "w_out": g["L0_attn_W_out"], "b_in": g["L0_attn_b_in"], "b_r": g["L0_attn_b_r"],
        "b_i": g["L0_attn_b_i"], "b_out": g["L0_attn_b_out"], "log_a": g["L0_attn_log_a"],
        "w_route": g["L0_ffn_Wr"],
        "fc_w": np.concatenate([g["L0_ffn_Wfc_s"][None], g["L0_ffn_Wfc"]], 0),
        "fc_b": np.concatenate([g["L0_ffn_bfc_s"][None], g["L0_ffn_bfc"]], 0)
        .reshape(-1, g["L0_ffn_bfc"].shape[1] // 128, 128).transpose(0, 2, 1),
        "pj_w": np.concatenate([g["L0_ffn_Wproj_s"][None], g["L0_ffn_Wproj"]], 0),
        "pj_b": np.concatenate([g["L0_ffn_bproj_s"][None], g["L0_ffn_bproj"]], 0)[:, None, :],
    }
    nc = bacc.Bacc("TRN2", target_bir_lowering=False, num_devices=1)
    args = []
    for name, a in list(arrays.items()):
        arrays[name] = a = np.ascontiguousarray(a)
        args.append(nc.dram_tensor(name, a.shape, my.dt.from_np(a.dtype), kind="ExternalInput").ap())
    rows = nimg * (length + 1)
    out = nc.dram_tensor("out", (rows + 1 + 256, m), my.dt.float32, kind="ExternalOutput").ap()
    vit_tower(nc, *args, out)
    r = run(nc, [arrays], core_ids=[0])
    return np.asarray(r.results[0]["out"])[:rows].reshape(nimg, length + 1, m)
```
